# Optimizing a Trainium2 kernel written in Bass

```python
import numpy as np
import jax
import jax.numpy as jnp

def _softmax(x, axis=-1):
    return jax.nn.softmax(x, axis=axis)

def _gelu(x):
    return jax.nn.gelu(x, approximate=True)

def _silu(x):
    return jax.nn.silu(x)

def _sigmoid(x):
    return jax.nn.sigmoid(x)

def _layernorm(x, axis=-1, eps=1e-05):
    m = jnp.mean(x, axis=axis, keepdims=True)
    v = jnp.var(x, axis=axis, keepdims=True)
    return (x - m) / jnp.sqrt(v + eps)

def _scatter_add(tgt, idx, src, axis=0):
    return tgt.at[idx].add(src)

def _segment_sum(src, seg, n):
    return jax.ops.segment_sum(src, seg, n)
kernel_name = 'mk_gnn_preln_d2_gnn_r64_b28158'

def setup_inputs(seed: int=0):
    np.random.seed(seed)
    _w = jnp.asarray

    def _rec_inputs():
        import jax
        import jax.numpy as jnp
        _gk = jax.random.key(seed)
        x = 0.0001712 + 1 * jax.random.normal(jax.random.fold_in(_gk, 1), (100000, 16), jnp.float32)
        _s = jax.random.randint(jax.random.fold_in(_gk, 2), (25000,), 0, 100000, jnp.int32)
        _d = jax.random.randint(jax.random.fold_in(_gk, 3), (25000,), 0, 100000, jnp.int32)
        _loop = jnp.arange(100000, dtype=jnp.int32)
        src = jnp.concatenate([_s, _d, _loop])
        dst = jnp.concatenate([_d, _s, _loop])
        _o = jnp.argsort(dst, stable=True)
        src = src[_o]
        dst = dst[_o]
        return (x, src, dst)
    x, src, dst = _rec_inputs()

    def _L0_gnn_setup():
        import jax, jax.numpy as jnp
        import numpy as np
        STALK_DIM = 16
        N_NODES = 50000
        N_EDGES = 6250
        HIDDEN = 64
        key = jax.random.key(seed)
        k1, k2, k3, k4 = jax.random.split(key, 4)
        d = STALK_DIM
        x = jax.random.normal(k1, (N_NODES, d), dtype=jnp.float32)
        edge_index = jax.random.randint(k2, (2, N_EDGES), 0, N_NODES, dtype=jnp.int64)
        W1 = jax.random.normal(k3, (HIDDEN, 2 * d), dtype=jnp.float32) * (1.0 / np.sqrt(2 * d))
        b1 = jnp.zeros((HIDDEN,), dtype=jnp.float32)
        W2 = jax.random.normal(k4, (d, HIDDEN), dtype=jnp.float32) * (1.0 / np.sqrt(HIDDEN))
        b2 = jnp.zeros((d,), dtype=jnp.float32)
        return {'x': x, 'edge_index': edge_index, 'W1': W1, 'b1': b1, 'W2': W2, 'b2': b2}
    _L0_gnn_all = _L0_gnn_setup()
    _L0_gnn_in = {k: v for k, v in _L0_gnn_all.items() if k in ('W1', 'b1', 'W2', 'b2')}
    del _L0_gnn_all

    def _L1_gnn_setup():
        import jax, jax.numpy as jnp
        import numpy as np
        N, E, D_IN, D, D_OUT = (100000, 50000, 16, 128, 16)
        LN_EPS = 1e-05

        def _layer_norm(x, g, b):
            mu = jnp.mean(x, axis=-1, keepdims=True)
            var = jnp.mean((x - mu) ** 2, axis=-1, keepdims=True)
            return (x - mu) * jax.lax.rsqrt(var + LN_EPS) * g + b
        key = jax.random.key(seed)
        ks = jax.random.split(key, 10)
        s = lambda fan_in: 1.0 / np.sqrt(fan_in)
        return {'X': jax.random.normal(ks[0], (N, D_IN), jnp.float32), 'W_enc0': jax.random.uniform(ks[1], (D_IN, D), jnp.float32, -s(D_IN), s(D_IN)), 'b_enc0': jnp.zeros((D,), jnp.float32), 'W_enc1': jax.random.uniform(ks[2], (D, D), jnp.float32, -s(D), s(D)), 'b_enc1': jnp.zeros((D,), jnp.float32), 'W_conv': jax.random.uniform(ks[3], (D, D), jnp.float32, -s(D), s(D)), 'b_conv': jnp.zeros((D,), jnp.float32), 'ln_g': jnp.ones((D,), jnp.float32), 'ln_b': jnp.zeros((D,), jnp.float32), 'W_dec0': jax.random.uniform(ks[4], (D, D), jnp.float32, -s(D), s(D)), 'b_dec0': jnp.zeros((D,), jnp.float32), 'W_dec1': jax.random.uniform(ks[5], (D, D_OUT), jnp.float32, -s(D), s(D)), 'b_dec1': jnp.zeros((D_OUT,), jnp.float32), 'edge_index': jax.random.randint(ks[6], (2, E), 0, N, jnp.int64), 'msg_steps': 3}
    _L1_gnn_all = _L1_gnn_setup()
    _L1_gnn_in = {k: v for k, v in _L1_gnn_all.items() if k in ('W_enc0', 'b_enc0', 'W_enc1', 'b_enc1', 'W_conv', 'b_conv', 'ln_g', 'ln_b', 'W_dec0', 'b_dec0', 'W_dec1', 'b_dec1')}
    del _L1_gnn_all
    return {'x': x, 'src': src, 'dst': dst, 'L0_gnn_W1': _L0_gnn_in['W1'], 'L0_gnn_b1': _L0_gnn_in['b1'], 'L0_gnn_W2': _L0_gnn_in['W2'], 'L0_gnn_b2': _L0_gnn_in['b2'], 'L1_gnn_W_enc0': _L1_gnn_in['W_enc0'], 'L1_gnn_b_enc0': _L1_gnn_in['b_enc0'], 'L1_gnn_W_enc1': _L1_gnn_in['W_enc1'], 'L1_gnn_b_enc1': _L1_gnn_in['b_enc1'], 'L1_gnn_W_conv': _L1_gnn_in['W_conv'], 'L1_gnn_b_conv': _L1_gnn_in['b_conv'], 'L1_gnn_ln_g': _L1_gnn_in['ln_g'], 'L1_gnn_ln_b': _L1_gnn_in['ln_b'], 'L1_gnn_W_dec0': _L1_gnn_in['W_dec0'], 'L1_gnn_b_dec0': _L1_gnn_in['b_dec0'], 'L1_gnn_W_dec1': _L1_gnn_in['W_dec1'], 'L1_gnn_b_dec1': _L1_gnn_in['b_dec1']}

def reference(x, src, dst, L0_gnn_W1, L0_gnn_b1, L0_gnn_W2, L0_gnn_b2, L1_gnn_W_enc0, L1_gnn_b_enc0, L1_gnn_W_enc1, L1_gnn_b_enc1, L1_gnn_W_conv, L1_gnn_b_conv, L1_gnn_ln_g, L1_gnn_ln_b, L1_gnn_W_dec0, L1_gnn_b_dec0, L1_gnn_W_dec1, L1_gnn_b_dec1):
    import jax
    import jax.numpy as jnp

    def _L0_gnn_ref(x, edge_index, W1, b1, W2, b2):
        import jax, jax.numpy as jnp
        import numpy as np
        STALK_DIM = 16
        N_NODES = 50000
        N_EDGES = 6250
        HIDDEN = 64
        d = x.shape[1]
        n = x.shape[0]
        src, dst = (edge_index[0], edge_index[1])
        xs, xd = (x[src], x[dst])

        def reflection(a, b):
            h = jax.nn.relu(jnp.concatenate([a, b], axis=1) @ W1.T + b1)
            return h @ W2.T + b2

        def householder(v):
            vn = v / jnp.maximum(jnp.linalg.norm(v, axis=1, keepdims=True), 1e-12)
            return jnp.eye(d, dtype=v.dtype)[None] - 2.0 * vn[:, :, None] * vn[:, None, :]
        F_s = householder(reflection(xs, xd))
        F_d = householder(reflection(xd, xs))
        L_sd = -jnp.einsum('eki,ekj->eij', F_s, F_d)
        ones_e = jnp.ones(src.shape[0], dtype=x.dtype)
        deg = jnp.zeros(n, dtype=x.dtype).at[src].add(ones_e).at[dst].add(ones_e)
        deg_inv_sqrt = 1.0 / jnp.sqrt(jnp.maximum(deg, 1e-05))
        coef = deg_inv_sqrt[src] * deg_inv_sqrt[dst]
        msg_s = coef[:, None] * jnp.einsum('eij,ej->ei', L_sd, xd)
        msg_d = coef[:, None] * jnp.einsum('eji,ej->ei', L_sd, xs)
        out = x - jnp.zeros_like(x).at[src].add(msg_s) - jnp.zeros_like(x).at[dst].add(msg_d)
        return jax.nn.relu(out)

    def _L1_gnn_ref(X, W_enc0, b_enc0, W_enc1, b_enc1, W_conv, b_conv, ln_g, ln_b, W_dec0, b_dec0, W_dec1, b_dec1, edge_index, msg_steps):
        import jax, jax.numpy as jnp
        import numpy as np
        N, E, D_IN, D, D_OUT = (100000, 50000, 16, 128, 16)
        LN_EPS = 1e-05

        def _layer_norm(x, g, b):
            mu = jnp.mean(x, axis=-1, keepdims=True)
            var = jnp.mean((x - mu) ** 2, axis=-1, keepdims=True)
            return (x - mu) * jax.lax.rsqrt(var + LN_EPS) * g + b
        n = X.shape[0]
        loops = jnp.arange(n, dtype=edge_index.dtype)
        row = jnp.concatenate([edge_index[0], loops])
        col = jnp.concatenate([edge_index[1], loops])
        deg = jax.ops.segment_sum(jnp.ones_like(col, jnp.float32), col, num_segments=n)
        dinv = jnp.where(deg > 0, jax.lax.rsqrt(deg), 0.0)
        norm = dinv[row] * dinv[col]
        x = jax.nn.relu(X @ W_enc0 + b_enc0)
        x = x @ W_enc1 + b_enc1
        for _ in range(msg_steps):
            h = x @ W_conv
            msg = h[row] * norm[:, None]
            agg = jax.ops.segment_sum(msg, col, num_segments=n) + b_conv
            x = _layer_norm(x + agg, ln_g, ln_b)
        x = jax.nn.relu(x @ W_dec0 + b_dec0)
        x = x @ W_dec1 + b_dec1
        return x
    edge_index = jnp.stack([src, dst])
    h = jnp.maximum(_layernorm(x, axis=-1), 0.0)
    x = x + _L0_gnn_ref(h, edge_index, L0_gnn_W1, L0_gnn_b1, L0_gnn_W2, L0_gnn_b2)
    h = jnp.maximum(_layernorm(x, axis=-1), 0.0)
    x = x + _L1_gnn_ref(h, L1_gnn_W_enc0, L1_gnn_b_enc0, L1_gnn_W_enc1, L1_gnn_b_enc1, L1_gnn_W_conv, L1_gnn_b_conv, L1_gnn_ln_g, L1_gnn_ln_b, L1_gnn_W_dec0, L1_gnn_b_dec0, L1_gnn_W_dec1, L1_gnn_b_dec1, edge_index, 3)
    return x

_drawn_inputs = setup_inputs


def setup_inputs(seed=0):
    import zlib

    import numpy as np

    out = dict(_drawn_inputs(seed))
    spreads = {'L0_gnn_b1': (0.0, 2.0),
     'L0_gnn_b2': (0.0, 0.587),
     'L1_gnn_b_enc0': (0.0, 0.418),
     'L1_gnn_b_enc1': (0.0, 0.1),
     'L1_gnn_b_conv': (0.0, 0.297),
     'L1_gnn_ln_g': (1.0, 0.2),
     'L1_gnn_ln_b': (0.0, 0.318),
     'L1_gnn_b_dec0': (0.0, 0.346),
     'L1_gnn_b_dec1': (0.0, 0.1)}
    factors = {}
    for name, (base, spread) in spreads.items():
        noise = np.random.default_rng([zlib.crc32(name.encode()), seed]).standard_normal(out[name].shape)
        drawn = base * np.exp(spread * noise) if base else spread * noise
        out[name] = jnp.asarray(drawn.astype(out[name].dtype))
    for name, factor in factors.items():
        out[name] = (out[name] * factor).astype(out[name].dtype)
    return out
```

```python
import concourse.bass as bass
from concourse import mybir
from contextlib import ExitStack

F32 = mybir.dt.float32
F16 = mybir.dt.float16
I32 = mybir.dt.int32
ALU = mybir.AluOpType
ACT = mybir.ActivationFunctionType
AX = mybir.AxisListType.X

P = 128
D0 = 16
HID = 64
D = 128
TW = D0 + 2
WIDE = 56
SLOTS = 8
ET = 8
LN_EPS = 1e-5
FAR = 1 << 20


class Steps:

    def __init__(self, eng, sem):
        self.eng, self.sem, self.base, self.n, self.per = eng, sem, 0, 0, 0

    def begin(self, i):
        if isinstance(i, int) and i == 0:
            self.base = 0
        else:
            self.per = self.per or self.n
            self.base = i * self.per
        self.n = 0

    def link(self, ins):
        ins.then_inc(self.sem, 1)
        self.n += 1
        self.eng.wait_ge(self.sem, self.base + self.n)


def spread(ap, n):
    return ap.unsqueeze(len(ap.shape)).to_broadcast([*ap.shape, n])


def along(ap, n):
    return ap.unsqueeze(1).to_broadcast([ap.shape[0], n, ap.shape[1]])


def turns(eng, body, n):
    body(0)
    if n > 1:
        with eng.Fori(1, n) as i:
            body(i)


def live_turns(eng, body, more_sb, n):
    more = eng.value_load(more_sb[0:1, 0:1], min_val=0, max_val=n - 1)
    body(0)
    if n > 1:
        with eng.Fori(1, n) as i:
            with eng.If(i <= more):
                body(i)
            eng.nop()
    return more


def wait_apart(eng, sem, value, passed):
    eng.wait_ge(sem, value)
    eng.sem_inc(passed, 1)


class Shapes:
    def __init__(self, N, E):
        self.N, self.E = N, E
        unit = 2 * WIDE
        self.S = -(-N // (P * unit)) * unit
        self.NP = P * self.S
        self.PAD = self.NP - 1
        self.TRASH = self.NP
        self.L = -(-E // (P * ET)) * ET
        self.PAIRS = -(-E // (2 * ET * P))
        self.CAP = self.PAIRS * 2 * ET * P
        assert N < self.NP and self.S % (2 * SLOTS) == 0 and self.S // 2 <= 512
        assert self.NP + P < FAR and self.CAP < FAR


def phase_edges(nc, K, z, src, dst, T, x):
    S, L, half = z.S, z.L, z.S // 2
    with ExitStack() as ctx:
        sb = lambda n, s, d: ctx.enter_context(nc.sbuf_tensor(n, s, d))
        sem = lambda n: ctx.enter_context(nc.semaphore(n))
        ends = sb("a_ends", [P, 2, L], I32)
        endf = sb("a_endf", [P, 2, L], F32)
        quo = sb("a_quo", [P, 2, L], F32)
        quo_i = sb("a_quo_i", [P, 2, L], I32)
        tmp = sb("a_tmp", [P, 2, L], F32)
        keys = sb("a_keys", [P, L, 5], F32)
        item = sb("a_item", [P, L, 3], I32)
        kept = sb("a_kept", [P, L], F32)
        rank = sb("a_rank", [P, L], F32)
        onesL = sb("a_onesL", [P, L], F32)
        base = sb("a_base", [P, 4], F32)
        count_f = sb("a_count_f", [P, 2], F32)
        count_i = sb("a_count_i", [P, 2], I32)
        fill = sb("a_fill", [P, 2 * z.CAP // P], I32)
        keyb = [sb(f"a_keyb{h}", [P, ET, 5], F32) for h in range(2)]
        itemb = [sb(f"a_itemb{h}", [P, ET, 3], I32) for h in range(2)]
        hot_slot = [sb(f"a_hot_slot{h}", [P, 2, S], F16) for h in range(2)]
        hot_part = [sb(f"a_hot_part{h}", [P, 3, P], F16) for h in range(2)]
        hist = sb("a_hist", [P, 3, S], F32)
        attr = sb("a_attr", [P, S, 4], F32)
        root = sb("a_root", [P, 2, S], F32)
        zero = sb("a_zero", [P, S * D0 // 4], F32)
        zero16 = sb("a_zero16", [P, P], F16)
        ps = [ctx.enter_context(nc.psum_tensor(f"a_ps{j}", [P, 512], F32)) for j in range(6)]
        psb = ctx.enter_context(nc.psum_tensor("a_psb", [P, 4], F32))

        ends_ready = sem("a_ends_ready"); ends_padded = sem("a_ends_padded"); zero_ready = sem("a_zero_ready")
        step = sem("a_step"); totals = sem("a_totals"); bases = sem("a_bases")
        fill_ready = sem("a_fill_ready"); filled = sem("a_filled")
        items_ready = sem("a_items_ready")
        keyb_ready = [sem(f"a_keyb_ready{h}") for h in range(2)]
        itemb_ready = [sem(f"a_itemb_ready{h}") for h in range(2)]
        hot_ready = sem("a_hot_ready"); hot_used = sem("a_hot_used")
        packed = [sem(f"a_packed{h}") for h in range(2)]
        hist_done = sem("a_hist_done"); roots = sem("a_roots"); deg_ready = sem("a_deg_ready")
        attr_ready = sem("a_attr_ready"); stored = sem("a_stored"); zeroed = sem("a_zeroed")
        block = ctx.enter_context(nc.Block())
        NB = L // ET
        TURN = NB // 2
        full = z.E // L
        rest = z.E - full * L
        nfull = z.N // S
        nrest = z.N - nfull * S

        @block.sync
        def _(sp):
            sp.wait_ge(ends_padded, 1)
            for a, v in enumerate((src, dst)):
                sp.dma_start(ends[0:full, a, :], v[0:full * L].rearrange("(p c) -> p c", c=L)).then_inc(ends_ready, 16)
                sp.dma_start(ends[full:full + 1, a, 0:rest], v[full * L:z.E].rearrange("(p c) -> p c", p=1)).then_inc(ends_ready, 16)
            sp.wait_ge(fill_ready, 1)
            sp.dma_start(T["edges"].rearrange("(p c) w -> p (c w)", p=P), fill[:, :]).then_inc(filled, 16)
            sp.wait_ge(zero_ready, 1)
            for name in ("acc_s", "acc_d"):
                for q in range(4):
                    w = S * D0 // 4
                    sp.dma_start(T[name][0:z.NP, :].rearrange("(p s) f -> p (s f)", s=S)[:, q * w:(q + 1) * w], zero[:, :]).then_inc(zeroed, 16)
                sp.dma_start(T[name][z.NP:z.NP + P, :], zero[:, 0:D0]).then_inc(zeroed, 16)
            sp.dma_start(T["acc"][z.NP:z.NP + P, :], zero[:, 0:D]).then_inc(zeroed, 16)
            sp.dma_start(T["x"][0:z.N, :], x[:, :]).then_inc(zeroed, 16)
            left = z.NP - z.N
            sp.dma_start(T["x"][z.N:z.NP, :].rearrange("(p c) f -> p (c f)", c=D0), zero[0:left // D0, 0:D0 * D0]).then_inc(zeroed, 16)
            sp.wait_ge(items_ready, 1)

            def body(i):
                for h in range(2):
                    if not isinstance(i, int):
                        sp.wait_ge(hot_ready, i * (2 * ET) + (h - 1) * ET)
                    c = (2 * i + h) * ET
                    sp.dma_start(keyb[h][:, :, :], keys[:, bass.ds(c, ET), :]).then_inc(keyb_ready[h], 16)
                    if not isinstance(i, int):
                        sp.wait_ge(packed[h], i * (16 * ET))
                    sp.dma_start(itemb[h][:, :, :], item[:, bass.ds(c, ET), :]).then_inc(itemb_ready[h], 16)

            turns(sp, body, TURN)
            if NB % 2:
                sp.wait_ge(hot_ready, (NB - 2) * ET)
                sp.dma_start(keyb[0][:, :, :], keys[:, L - ET:L, :]).then_inc(keyb_ready[0], 16)
                sp.wait_ge(packed[0], TURN * 16 * ET)
                sp.dma_start(itemb[0][:, :, :], item[:, L - ET:L, :]).then_inc(itemb_ready[0], 16)
            sp.wait_ge(attr_ready, 1)
            sp.dma_start(T["attr"].rearrange("(p s) f -> p s f", s=S), attr[:, :, :]).then_inc(stored, 16)
            sp.wait_ge(stored, 16)
            sp.wait_ge(filled, 16)
            sp.wait_ge(zeroed, 16 * 13)

        @block.gpsimd
        def _(pool):
            pool.memset(ends[:, :, :], z.PAD).then_inc(ends_padded, 1)
            pool.memset(fill[:, :], z.PAD).then_inc(fill_ready, 1)

            def scatter(h, n):
                pool.wait_ge(filled, 16)
                wait_apart(pool, itemb_ready[h], n, K["passed"])
                for j in range(ET):
                    pool.indirect_dma_start(
                        T["edges"][:, :], bass.IndirectOffsetOnAxis(ap=itemb[h][:, j, 0:1], axis=0),
                        itemb[h][:, j, 1:3], None, bounds_check=z.CAP - 1, oob_is_err=False,
                    ).then_inc(packed[h], 16)

            def body(i):
                for h in range(2):
                    scatter(h, 16 * (i + 1))

            turns(pool, body, TURN)
            if NB % 2:
                scatter(0, 16 * (TURN + 1))
            pool.wait_ge(packed[0], 16 * ET * ((NB + 1) // 2))
            pool.wait_ge(packed[1], 16 * ET * (NB // 2))

        @block.scalar
        def _(act):
            act.wait_ge(deg_ready, 1)
            nc.scalar.activation(root[:, :, :], root[:, :, :], ACT.Sqrt).then_inc(roots, 1)

        @block.vector
        def _(dve):
            v = nc.vector
            st = Steps(dve, step)
            v.memset(zero[:, :], 0.0).then_inc(zero_ready, 1)
            v.memset(onesL[:, :], 1.0)
            st.link(v.memset(zero16[:, :], 0.0))
            dve.wait_ge(ends_ready, 64)
            v.tensor_copy(item[:, :, 1:3].rearrange("p c a -> p a c"), ends[:, :, :])
            st.link(v.tensor_copy(endf[:, :, :], ends[:, :, :]))
            st.link(v.tensor_scalar(quo[:, :, :], endf[:, :, :], 1.0 / S, None, ALU.mult))
            st.link(v.tensor_copy(quo_i[:, :, :], quo[:, :, :]))
            st.link(v.tensor_copy(quo[:, :, :], quo_i[:, :, :]))
            st.link(v.scalar_tensor_tensor(tmp[:, :, :], quo[:, :, :], -float(S), endf[:, :, :], ALU.mult, ALU.add))
            st.link(v.tensor_scalar(tmp[:, :, :], tmp[:, :, :], 0.0, None, ALU.is_lt))
            st.link(v.tensor_tensor(quo[:, :, :], quo[:, :, :], tmp[:, :, :], ALU.subtract))
            st.link(v.scalar_tensor_tensor(tmp[:, :, :], quo[:, :, :], -float(S), endf[:, :, :], ALU.mult, ALU.add))
            st.link(v.tensor_scalar(tmp[:, :, :], tmp[:, :, :], float(S), None, ALU.is_ge))
            st.link(v.tensor_tensor(quo[:, :, :], quo[:, :, :], tmp[:, :, :], ALU.add))
            st.link(v.scalar_tensor_tensor(tmp[:, :, :], quo[:, :, :], -float(S), endf[:, :, :], ALU.mult, ALU.add))
            v.tensor_copy(keys[:, :, 0:2].rearrange("p c a -> p a c"), tmp[:, :, :])
            v.tensor_copy(keys[:, :, 2:4].rearrange("p c a -> p a c"), quo[:, :, :])
            st.link(v.tensor_tensor(kept[:, :], endf[:, 0, :], endf[:, 1, :], ALU.not_equal))
            v.tensor_scalar(keys[:, :, 4], kept[:, :], -1.0, 1.0, ALU.mult, ALU.add)
            st.link(v.tensor_tensor_scan(rank[:, :], onesL[:, :], kept[:, :], 0.0, ALU.mult, ALU.add))
            st.link(v.tensor_copy(count_f[:, 0:1], rank[:, L - 1:L]))
            v.tensor_copy(count_f[:, 1:2], rank[:, L - 1:L]).then_inc(totals, 1)
            dve.wait_ge(bases, 1)
            st.link(v.tensor_copy(base[:, 0:2], psb[:, 0:2]))
            st.link(v.tensor_scalar(rank[:, :], rank[:, :], base[:, 0:1], -1.0, ALU.add, ALU.add))
            st.link(v.scalar_tensor_tensor(rank[:, :], keys[:, :, 4], float(FAR), rank[:, :], ALU.mult, ALU.add))
            st.link(v.tensor_copy(item[:, :, 0], rank[:, :]))
            both = 2 * ET * P
            st.link(v.tensor_scalar(base[:, 2:3], base[:, 1:2], -1.0, 0.0, ALU.add, ALU.max))
            st.link(v.tensor_copy(count_i[:, 0:1], base[:, 2:3]))
            st.link(v.tensor_scalar(K["more"][:, :], count_i[:, 0:1], both.bit_length() - 1, None, ALU.logical_shift_right))
            v.tensor_copy(count_i[:, 1:2], K["more"][:, :]).then_inc(items_ready, 1)

            def hot(h, n, first):
                dve.wait_ge(keyb_ready[h], n)
                for j in range(ET):
                    q = j % 2
                    if not (first and h == 0 and j < 2):
                        dve.wait_ge(hot_used, hot.base + ET * h + j - 1)
                    v.tensor_scalar(hot_slot[q][:, 0, :], K["iota"][:, 0:S], keyb[h][:, j, 0:1], None, ALU.is_equal)
                    v.tensor_scalar(hot_slot[q][:, 1, :], K["iota"][:, 0:S], keyb[h][:, j, 1:2], None, ALU.is_equal)
                    v.tensor_scalar(hot_part[q][:, 0, :], K["iota"][:, 0:P], keyb[h][:, j, 2:3], None, ALU.is_equal)
                    v.tensor_scalar(hot_part[q][:, 1, :], K["iota"][:, 0:P], keyb[h][:, j, 3:4], None, ALU.is_equal)
                    last = v.tensor_scalar(hot_part[q][:, 2, :], K["iota"][:, 0:P], keyb[h][:, j, 3:4], keyb[h][:, j, 4:5], ALU.is_equal, ALU.mult)
                    last.then_inc(hot_ready, 1)

            def body(i):
                hot.base = i * (2 * ET)
                for h in range(2):
                    hot(h, 16 * (i + 1), isinstance(i, int))

            turns(dve, body, TURN)
            if NB % 2:
                hot.base = TURN * 2 * ET
                hot(0, 16 * (TURN + 1), False)

            dve.wait_ge(hist_done, 1)
            for k in range(3):
                for q in range(2):
                    last = v.tensor_copy(hist[:, k, q * half:(q + 1) * half], ps[2 * k + q][:, 0:half])
            st.link(last)
            st.link(v.tensor_tensor(root[:, 0, :], hist[:, 0, :], hist[:, 1, :], ALU.add))
            v.tensor_scalar(root[:, 0, :], root[:, 0, :], 1e-5, None, ALU.max)
            v.tensor_scalar(root[:, 1, :], hist[:, 1, :], 1.0, None, ALU.add).then_inc(deg_ready, 1)
            dve.wait_ge(roots, 1)
            st.link(v.reciprocal(root[:, :, :], root[:, :, :]))
            v.tensor_copy(attr[:, :, 0:2].rearrange("p s a -> p a s"), root[:, :, :])
            v.tensor_scalar(hist[:, 0, :], hist[:, 2, :], 2.0, None, ALU.mult)
            st.link(v.tensor_scalar(hist[:, 1, :], hist[:, 2, :], 1.0, None, ALU.add))
            st.link(v.tensor_tensor(hist[:, 0:2, :], hist[:, 0:2, :], root[:, :, :], ALU.mult))
            v.tensor_tensor(attr[:, :, 2:4].rearrange("p s a -> p a s"), hist[:, 0:2, :], root[:, :, :], ALU.mult).then_inc(attr_ready, 1)

        @block.tensor
        def _(pe):
            t = nc.tensor
            pe.wait_ge(totals, 1)
            t.matmul(psb[:, 0:1], K["before"][:, :], count_f[:, 0:1], start=True, stop=True)
            t.matmul(psb[:, 1:2], K["ones"][:, :], count_f[:, 1:2], start=True, stop=True).then_inc(bases, 1)
            for j in range(6):
                t.matmul(ps[j][:, 0:half], zero16[:, :], K["iota"][:, 0:half], start=True, stop=False)

            def add(n, j):
                q = j % 2
                pe.wait_ge(hot_ready, n)
                for k, (part, slot) in enumerate(((0, 0), (1, 1), (2, 1))):
                    for w in range(2):
                        last = t.matmul(ps[2 * k + w][:, 0:half], hot_part[q][:, part, :],
                                        hot_slot[q][:, slot, w * half:(w + 1) * half], start=False, stop=False)
                last.then_inc(hot_used, 1)

            def body(i):
                for j in range(2 * ET):
                    add(i * (2 * ET) + j + 1, j)

            turns(pe, body, TURN)
            if NB % 2:
                for j in range(ET):
                    add(TURN * 2 * ET + j + 1, j)
            for j in range(6):
                last = t.matmul(ps[j][:, 0:half], zero16[:, :], K["iota"][:, 0:half], start=False, stop=True)
            last.then_inc(hist_done, 1)




def phase_constants(nc, K, z, w):
    with ExitStack() as ctx:
        sb = lambda n, s, d: ctx.enter_context(nc.sbuf_tensor(n, s, d))
        sem = lambda n: ctx.enter_context(nc.semaphore(n))
        wide = sb("c_wide", [P, max(z.S, P)], I32)
        diff = sb("c_diff", [P, P], I32)
        chan = sb("c_chan", [P, 1], I32)
        patterns = sem("c_patterns"); cleared = sem("c_cleared"); loaded = sem("c_loaded")
        made = sem("c_made")
        block = ctx.enter_context(nc.Block())

        @block.gpsimd
        def _(pool):
            pool.iota(wide[:, :], [[1, max(z.S, P)]], base=0, channel_multiplier=0)
            pool.iota(diff[:, :], [[1, P]], base=0, channel_multiplier=-1)
            pool.iota(chan[:, :], [[0, 1]], base=z.TRASH, channel_multiplier=1).then_inc(patterns, 1)

        @block.vector
        def _(dve):
            v = nc.vector
            for name in ("w_ref", "w_ref_out", "w_self_a", "w_self_b", "w_enc0"):
                last = v.memset(K[name][...], 0.0)
            last.then_inc(cleared, 1)
            v.memset(K["ones"][:, :], 1.0)
            v.memset(K["eps"][:, :], LN_EPS)
            dve.wait_ge(patterns, 1)
            v.tensor_copy(K["iota"][:, :], wide[:, :])
            v.tensor_copy(K["trash"][:, :], chan[:, :])
            v.tensor_scalar(K["ident"][:, :], diff[:, :], 0.0, None, ALU.is_equal)
            v.tensor_scalar(K["earlier"][:, :], diff[:, :], 0.0, None, ALU.is_lt)
            v.tensor_scalar(K["before"][:, :], diff[:, :], 0.0, None, ALU.is_gt).then_inc(made, 1)

        @block.sync
        def _(sp):
            n = 0

            def load(out, in_):
                sp.dma_start(out, in_, allow_slow_non_contiguous=True).then_inc(loaded, 16)

            sp.wait_ge(cleared, 1)
            own = w["L0_gnn_W1"][:, 0:D0].rearrange("m k -> k m")
            other = w["L0_gnn_W1"][:, D0:2 * D0].rearrange("m k -> k m")
            W2T = w["L0_gnn_W2"].rearrange("o h -> h o")
            load(K["w_ref"][0:D0, 0:HID], own)
            load(K["w_ref"][0:D0, HID:P], other)
            load(K["w_ref"][TW:TW + D0, 0:HID], other)
            load(K["w_ref"][TW:TW + D0, HID:P], own)
            load(K["w_ref_out"][0:HID, 0:D0], W2T)
            load(K["w_ref_out"][HID:P, D0:2 * D0], W2T)
            n += 6
            for j in range(SLOTS):
                rows = slice(D0 * j, D0 * (j + 1))
                cols = slice(HID * (j % 2), HID * (j % 2 + 1))
                load(K["w_self_a"][rows, j // 2, cols], own)
                load(K["w_self_b"][rows, j // 2, cols], other)
                load(K["w_enc0"][rows, j, :], w["L1_gnn_W_enc0"])
                n += 3
            for a in range(2):
                load(K["b_ref"][HID * a:HID * (a + 1), :], w["L0_gnn_b1"].rearrange("(m a) -> m a", a=1))
                load(K["b_ref_out"][:, D0 * a:D0 * (a + 1)], w["L0_gnn_b2"].partition_broadcast(P))
                n += 2
            for name in ("enc1", "conv", "dec0", "dec1"):
                load(K["w_" + name][:, :], w["L1_gnn_W_" + name])
                n += 1
            for name in ("b_enc0", "b_dec0"):
                load(K[name][:, :], w["L1_gnn_" + name].rearrange("(m a) -> m a", a=1))
                n += 1
            for name in ("b_enc1", "b_conv", "b_dec1", "ln_g", "ln_b"):
                load(K[name][:, :], w["L1_gnn_" + name].partition_broadcast(P))
                n += 1
            sp.wait_ge(loaded, 16 * n)


def normalise(v, st, act_turn, x, sums, centred, square, out, width, n):
    st.link(v.tensor_reduce(sums[:, 0, :], x, AX, ALU.add))
    st.link(v.tensor_scalar(sums[:, 1, :], sums[:, 0, :], 1.0 / width, None, ALU.mult))
    st.link(v.tensor_tensor(centred, x, spread(sums[:, 1, :], width), ALU.subtract))
    st.link(v.tensor_tensor(square, centred, centred, ALU.mult))
    v.tensor_reduce(sums[:, 2, :], square, AX, ALU.add).then_inc(act_turn[0], 1)
    st.eng.wait_ge(act_turn[1], n)
    st.link(v.reciprocal(sums[:, 3, :], sums[:, 3, :]))
    st.link(v.tensor_tensor(square, centred, spread(sums[:, 3, :], width), ALU.mult))
    return v.tensor_scalar(out, square, 0.0, None, ALU.max)


def phase_rows(nc, K, z, T):
    S, W = z.S, WIDE
    with ExitStack() as ctx:
        sb = lambda n, s, d: ctx.enter_context(nc.sbuf_tensor(n, s, d))
        sem = lambda n: ctx.enter_context(nc.semaphore(n))
        xb = [sb(f"b_x{h}", [P, W, D0], F32) for h in range(2)]
        ab = [sb(f"b_attr{h}", [P, W, 4], F32) for h in range(2)]
        row = [sb(f"b_row{h}", [P, W, TW], F32) for h in range(2)]
        centred = sb("b_centred", [P, W, D0], F32)
        square = sb("b_square", [P, W, D0], F32)
        sums = sb("b_sums", [P, 4, W], F32)
        loaded = [sem(f"b_loaded{h}") for h in range(2)]
        stored = [sem(f"b_stored{h}") for h in range(2)]
        step = sem("b_step"); ready = sem("b_ready"); var_ready = sem("b_var"); root_ready = sem("b_root")
        block = ctx.enter_context(nc.Block())
        TURN = S // (2 * W)
        slots = lambda t, k: t[0:z.NP, :].rearrange("(p s) f -> p s f", s=S)[:, bass.ds(k * W, W), :]

        @block.sync
        def _(sp):
            def body(i):
                for h in range(2):
                    if not isinstance(i, int):
                        sp.wait_ge(ready, 2 * i + (h - 1))
                    sp.dma_start(xb[h][:, :, :], slots(T["x"], 2 * i + h)).then_inc(loaded[h], 16)
                    sp.dma_start(ab[h][:, :, :], slots(T["attr"], 2 * i + h)).then_inc(loaded[h], 16)
            turns(sp, body, TURN)

        @block.vector
        def _(dve):
            v = nc.vector
            st = Steps(dve, step)

            def body(i):
                st.begin(i)
                for h in range(2):
                    dve.wait_ge(loaded[h], 32 * i + 32)
                    if not isinstance(i, int):
                        dve.wait_ge(stored[h], 16 * i)
                    v.tensor_copy(row[h][:, :, D0:TW], ab[h][:, :, 0:2])
                    normalise(v, st, (var_ready, root_ready), xb[h][:, :, :], sums, centred[:, :, :],
                              square[:, :, :], row[h][:, :, 0:D0], D0, 2 * i + h + 1).then_inc(ready, 1)
            turns(dve, body, TURN)

        @block.scalar
        def _(act):
            def body(i):
                for h in range(2):
                    act.wait_ge(var_ready, 2 * i + h + 1)
                    nc.scalar.activation(sums[:, 3, :], sums[:, 2, :], ACT.Sqrt, bias=K["eps"][:, 0:1],
                                         scale=1.0 / D0).then_inc(root_ready, 1)
                    act.wait_ge(ready, 2 * i + h + 1)
                    act.dma_start(slots(T["rows"], 2 * i + h), row[h][:, :, :]).then_inc(stored[h], 16)
            turns(act, body, TURN)
            act.wait_ge(stored[0], 16 * TURN)
            act.wait_ge(stored[1], 16 * TURN)


def phase_reflect_edges(nc, K, z, T):
    B = ET * P
    with ExitStack() as ctx:
        sb = lambda n, s, d: ctx.enter_context(nc.sbuf_tensor(n, s, d))
        sem = lambda n: ctx.enter_context(nc.semaphore(n))
        ends = [sb(f"r_ends{h}", [P, ET, 2], I32) for h in range(2)]
        row = [sb(f"r_row{h}", [P, ET, 2, TW], F32) for h in range(2)]
        rowT = sb("r_rowT", [2 * TW, ET, P], F32)
        hid = sb("r_hid", [P, ET, P], F32)
        endf = sb("r_endf", [P, ET, 2], F32)
        same = sb("r_same", [P, 2, ET, P], F32)
        early = sb("r_early", [P, ET, P], F32)
        first = sb("r_first", [P, 2, ET], F32)
        target = [sb(f"r_target{h}", [P, 2, ET], I32) for h in range(2)]
        plan = [sb(f"r_plan{h}", [P, ET, 4], F32) for h in range(2)]
        vec = sb("r_vec", [P, ET, 2, D0], F32)
        prod = sb("r_prod", [P, ET, 2, D0], F32)
        swap = sb("r_swap", [P, ET, 2, D0], F32)
        msg = sb("r_msg", [P, ET, 2, D0], F32)
        inv = sb("r_inv", [P, ET, 2], F32)
        dot = sb("r_dot", [P, ET, 2], F32)
        coef = sb("r_coef", [P, ET], F32)
        total = [sb(f"r_total{h}", [P, 2, ET, D0], F32) for h in range(2)]
        psT = ctx.enter_context(nc.psum_tensor("r_psT", [2 * TW, ET, P], F32))
        psH = ctx.enter_context(nc.psum_tensor("r_psH", [P, ET, P], F32))
        psV = ctx.enter_context(nc.psum_tensor("r_psV", [P, ET, 2 * D0], F32))
        psR = ctx.enter_context(nc.psum_tensor("r_psR", [P, ET, P], F32))
        psS = ctx.enter_context(nc.psum_tensor("r_psS", [P, 2, ET, D0], F32))
        ends_ready = [sem(f"r_ends_ready{h}") for h in range(2)]
        rows_ready = [sem(f"r_rows_ready{h}") for h in range(2)]
        planned = [sem(f"r_planned{h}") for h in range(2)]
        added_to = [sem(f"r_added_to{a}") for a in range(2)]
        step = sem("r_step"); endf_ready = sem("r_endf_ready"); row_numbers = sem("r_row_numbers")
        numbers_used = sem("r_numbers_used"); rowT_ps = sem("r_rowT_ps"); rowT_ready = sem("r_rowT_ready")
        hid_ps = sem("r_hid_ps"); hid_ready = sem("r_hid_ready"); vec_ps = sem("r_vec_ps")
        msg_ready = sem("r_msg_ready"); sum_ps = sem("r_sum_ps"); totals_ready = sem("r_totals_ready")
        block = ctx.enter_context(nc.Block())
        rows_of = lambda t, k: t[bass.ds(k * B, B), :].rearrange("(p j) w -> p j w", j=ET)

        @block.sync
        def _(sp):
            def body(i):
                for h in range(2):
                    if not isinstance(i, int):
                        sp.wait_ge(totals_ready, 2 * i + (h - 1))
                    sp.dma_start(ends[h][:, :, :], rows_of(T["edges"], 2 * i + h)).then_inc(ends_ready[h], 16)
            live_turns(sp, body, K["more"], z.PAIRS)

        @block.gpsimd
        def _(pool):
            def gather(h, n):
                wait_apart(pool, ends_ready[h], n, K["passed"])
                for j in range(ET):
                    for a in range(2):
                        pool.indirect_dma_start(row[h][:, j, a, :], None, T["rows"][:, :],
                                                bass.IndirectOffsetOnAxis(ap=ends[h][:, j, a:a + 1], axis=0)
                                                ).then_inc(rows_ready[h], 16)

            def scatter(h, n, k):
                wait_apart(pool, totals_ready, n, K["passed"])
                for j in range(ET):
                    for a, acc in enumerate((T["acc_s"], T["acc_d"])):
                        pool.indirect_dma_start(acc[:, :], bass.IndirectOffsetOnAxis(ap=target[h][:, a, j:j + 1], axis=0),
                                                total[h][:, a, j, :], None, compute_op=ALU.add
                                                ).then_inc(added_to[a], 16)
                        if a == 1:
                            for b in range(2):
                                wait_apart(pool, added_to[b], k * (16 * ET) + 16 * (j + 1), K["passed"])

            def body(i):
                gather(0, 16 * (i + 1))
                if not isinstance(i, int):
                    scatter(1, 2 * i, 2 * i + (-1))
                gather(1, 16 * (i + 1))
                scatter(0, 2 * i + 1, 2 * i)

            more = live_turns(pool, body, K["more"], z.PAIRS)
            scatter(1, more * 2 + 2, more * 2 + 1)

        @block.tensor
        def _(pe):
            t = nc.tensor

            def body(i):
                for h in range(2):
                    k = 2 * i + h
                    pe.wait_ge(endf_ready, k + 1)
                    for a in range(2):
                        if not (isinstance(i, int) and h == 0 and a == 0):
                            pe.wait_ge(numbers_used, 2 * k + a)
                        for j in range(ET):
                            last = t.matmul(psR[:, j, :], endf[:, j, a:a + 1].to_broadcast([P, P]), K["ident"][:, :], start=True, stop=True)
                        last.then_inc(row_numbers, 1)
                    wait_apart(pe, rows_ready[h], (i + 1) * (32 * ET), K["passed"])
                    for j in range(ET):
                        last = t.transpose(psT[:, j, :], row[h][:, j, :, :].rearrange("p a f -> p (a f)"), K["ident"][:, :])
                    last.then_inc(rowT_ps, 1)
                    pe.wait_ge(rowT_ready, k + 1)
                    for q in range(ET // 4):
                        last = t.matmul(psH[:, 4 * q:4 * q + 4, :].rearrange("p j n -> p (j n)"), K["w_ref"][0:2 * TW, :],
                                        rowT[:, 4 * q:4 * q + 4, :].rearrange("p j n -> p (j n)"), start=True, stop=True)
                    last.then_inc(hid_ps, 1)
                    pe.wait_ge(hid_ready, k + 1)
                    for j in range(ET):
                        last = t.matmul(psV[:, j, :], hid[:, j, :], K["w_ref_out"][:, :], start=True, stop=True)
                    last.then_inc(vec_ps, 1)
                    pe.wait_ge(msg_ready, k + 1)
                    for a in range(2):
                        for j in range(ET):
                            last = t.matmul(psS[:, a, j, :], same[:, a, j, :], msg[:, j, a, :], start=True, stop=True)
                    last.then_inc(sum_ps, 1)
            live_turns(pe, body, K["more"], z.PAIRS)

        @block.scalar
        def _(act):
            def body(i):
                for h in range(2):
                    k = 2 * i + h
                    act.wait_ge(rowT_ps, k + 1)
                    nc.scalar.activation(rowT[:, :, :], psT[:, :, :], ACT.Copy).then_inc(rowT_ready, 1)
                    act.wait_ge(hid_ps, k + 1)
                    nc.scalar.activation(hid[:, :, :], psH[:, :, :], ACT.Relu, bias=K["b_ref"][:, 0:1]).then_inc(hid_ready, 1)
                    act.wait_ge(totals_ready, k + 1)
                    act.dma_start(rows_of(T["plan"], k), plan[h][:, :, :]).then_inc(planned[h], 16)
            more = live_turns(act, body, K["more"], z.PAIRS)
            for h in range(2):
                wait_apart(act, planned[h], more * 16 + 16, K["passed"])

        @block.vector
        def _(dve):
            v = nc.vector
            st = Steps(dve, step)

            def body(i):
                st.begin(i)
                for h in range(2):
                    k = 2 * i + h
                    dve.wait_ge(ends_ready[h], 16 * (i + 1))
                    if not isinstance(i, int):
                        dve.wait_ge(planned[h], 16 * i)
                        dve.wait_ge(added_to[0], i * (32 * ET) + (h - 1) * (16 * ET))
                        dve.wait_ge(added_to[1], i * (32 * ET) + (h - 1) * (16 * ET))
                    v.tensor_copy(endf[:, :, :], ends[h][:, :, :]).then_inc(endf_ready, 1)
                    dve.wait_ge(endf_ready, k + 1)
                    for a in range(2):
                        dve.wait_ge(row_numbers, 2 * k + a + 1)
                        v.tensor_tensor(same[:, a, :, :], psR[:, :, :], spread(endf[:, :, a], P), ALU.is_equal).then_inc(numbers_used, 1)
                        dve.wait_ge(numbers_used, 2 * k + a + 1)
                        st.link(v.tensor_tensor(early[:, :, :], same[:, a, :, :], along(K["earlier"][:, :], ET), ALU.mult))
                        st.link(v.tensor_reduce(first[:, a, :], early[:, :, :], AX, ALU.max))
                    st.link(v.tensor_scalar(first[:, :, :], first[:, :, :], -1.0, 1.0, ALU.mult, ALU.add))
                    endt = endf[:, :, :].rearrange("p j a -> p a j")
                    st.link(v.scalar_tensor_tensor(first[:, :, :], endt, K["trash"][:, 0:1], first[:, :, :], ALU.subtract, ALU.mult))
                    st.link(v.tensor_scalar(first[:, :, :], first[:, :, :], K["trash"][:, 0:1], None, ALU.add))
                    v.tensor_copy(target[h][:, :, :], first[:, :, :])
                    v.tensor_copy(plan[h][:, :, 0].bitcast(I32), ends[h][:, :, 0])
                    v.tensor_copy(plan[h][:, :, 1].bitcast(I32), first[:, 1, :])
                    v.tensor_copy(plan[h][:, :, 2], endf[:, :, 1])
                    dve.wait_ge(rows_ready[h], (i + 1) * (32 * ET))
                    x = row[h][:, :, :, 0:D0]
                    v.tensor_tensor(plan[h][:, :, 3], row[h][:, :, 0, D0 + 1], row[h][:, :, 1, D0 + 1], ALU.mult)
                    v.tensor_tensor(coef[:, :], row[h][:, :, 0, D0], row[h][:, :, 1, D0], ALU.mult)
                    dve.wait_ge(vec_ps, k + 1)
                    bias = along(K["b_ref_out"][:, :], ET).rearrange("p j (a f) -> p j a f", a=2)
                    st.link(v.tensor_tensor(vec[:, :, :, :], psV[:, :, :].rearrange("p j (a f) -> p j a f", a=2), bias, ALU.add))
                    st.link(v.tensor_tensor(prod[:, :, :, :], vec[:, :, :, :], vec[:, :, :, :], ALU.mult))
                    st.link(v.tensor_reduce(inv[:, :, :], prod[:, :, :, :], AX, ALU.add))
                    st.link(v.tensor_scalar(inv[:, :, :], inv[:, :, :], 1e-24, None, ALU.max))
                    st.link(v.reciprocal(inv[:, :, :], inv[:, :, :]))
                    st.link(v.tensor_tensor(prod[:, :, :, :], vec[:, :, :, :], x, ALU.mult))
                    st.link(v.tensor_reduce(dot[:, :, :], prod[:, :, :, :], AX, ALU.add))
                    st.link(v.scalar_tensor_tensor(dot[:, :, :], dot[:, :, :], 2.0, inv[:, :, :], ALU.mult, ALU.mult))
                    st.link(v.tensor_tensor(prod[:, :, :, :], vec[:, :, :, :], spread(dot[:, :, :], D0), ALU.mult))
                    for a in range(2):
                        last = v.tensor_tensor(swap[:, :, 1 - a, :], x[:, :, a, :], prod[:, :, a, :], ALU.subtract)
                    st.link(last)
                    st.link(v.tensor_tensor(prod[:, :, :, :], vec[:, :, :, :], swap[:, :, :, :], ALU.mult))
                    st.link(v.tensor_reduce(dot[:, :, :], prod[:, :, :, :], AX, ALU.add))
                    st.link(v.scalar_tensor_tensor(dot[:, :, :], dot[:, :, :], 2.0, inv[:, :, :], ALU.mult, ALU.mult))
                    st.link(v.tensor_tensor(prod[:, :, :, :], vec[:, :, :, :], spread(dot[:, :, :], D0), ALU.mult))
                    st.link(v.tensor_tensor(swap[:, :, :, :], swap[:, :, :, :], prod[:, :, :, :], ALU.subtract))
                    both = spread(coef[:, :], 2 * D0).rearrange("p j (a f) -> p j a f", a=2)
                    v.tensor_tensor(msg[:, :, :, :], swap[:, :, :, :], both, ALU.mult).then_inc(msg_ready, 1)
                    dve.wait_ge(sum_ps, k + 1)
                    v.tensor_copy(total[h][:, :, :, :], psS[:, :, :, :]).then_inc(totals_ready, 1)
            live_turns(dve, body, K["more"], z.PAIRS)


def phase_reflect_nodes(nc, K, z, T):
    S, W, G = z.S, WIDE, WIDE // SLOTS
    with ExitStack() as ctx:
        sb = lambda n, s, d: ctx.enter_context(nc.sbuf_tensor(n, s, d))
        sem = lambda n: ctx.enter_context(nc.semaphore(n))
        xb = [sb(f"n_x{h}", [P, W, D0], F32) for h in range(2)]
        ab = [sb(f"n_attr{h}", [P, W, 4], F32) for h in range(2)]
        row = [sb(f"n_row{h}", [P, W, TW], F32) for h in range(2)]
        acc = [sb(f"n_acc{h}", [P, 2, W, D0], F32) for h in range(2)]
        feat = [sb(f"n_feat{h}", [P, W, D0], F32) for h in range(2)]
        hb = [sb(f"n_h{h}", [P, W, D0], F32) for h in range(2)]
        hT = sb("n_hT", [P, G, P], F32)
        hid = [sb(f"n_hid{q}", [P, SLOTS // 2, P], F32) for q in range(2)]
        vec = sb("n_vec", [P, W, D0], F32)
        prod = sb("n_prod", [P, W, D0], F32)
        y = sb("n_y", [P, W, D0], F32)
        inv = sb("n_inv", [P, W], F32)
        dot = sb("n_dot", [P, W], F32)
        sums = sb("n_sums", [P, 4, W], F32)
        psT = ctx.enter_context(nc.psum_tensor("n_psT", [P, 8, P], F32))
        psH = [ctx.enter_context(nc.psum_tensor(f"n_psH{q}", [P, SLOTS // 2, P], F32)) for q in range(2)]
        psV = ctx.enter_context(nc.psum_tensor("n_psV", [P, 64, D0], F32))
        loaded = [sem(f"n_loaded{h}") for h in range(2)]
        stored = [sem(f"n_stored{h}") for h in range(2)]
        packed = sem("n_packed")
        step = sem("n_step"); ready = sem("n_ready"); var_ready = sem("n_var"); root_ready = sem("n_root")
        hT_ps = sem("n_hT_ps"); hT_ready = sem("n_hT_ready"); hid_ps = sem("n_hid_ps"); hid_ready = sem("n_hid_ready")
        vec_ps = sem("n_vec_ps"); vec_used = sem("n_vec_used")
        block = ctx.enter_context(nc.Block())
        TURN = S // (2 * W)
        slots = lambda t, k: t[0:z.NP, :].rearrange("(p s) f -> p s f", s=S)[:, bass.ds(k * W, W), :]

        @block.sync
        def _(sp):
            def body(i):
                for h in range(2):
                    k = 2 * i + h
                    if not isinstance(i, int):
                        wait_apart(sp, stored[h], 32 * i, K["passed"])
                        wait_apart(sp, ready, 2 * i + (h - 1), K["passed"])
                    for to, name in ((row[h][:, :, :], "rows"), (xb[h][:, :, :], "x"), (ab[h][:, :, :], "attr"),
                                     (acc[h][:, 0, :, :], "acc_s"), (acc[h][:, 1, :, :], "acc_d")):
                        sp.dma_start(to, slots(T[name], k)).then_inc(loaded[h], 16)
            turns(sp, body, TURN)

        @block.tensor
        def _(pe):
            t = nc.tensor

            def body(i):
                for h in range(2):
                    k = 2 * i + h
                    pe.wait_ge(packed, k + 1)
                    for g in range(G):
                        last = t.transpose(psT[:, g, :], feat[h][:, SLOTS * g:SLOTS * (g + 1), :].rearrange("p s f -> p (s f)"), K["ident"][:, :])
                    last.then_inc(hT_ps, 1)
                    pe.wait_ge(hT_ready, k + 1)
                    if not (isinstance(i, int) and h == 0):
                        pe.wait_ge(vec_used, k)
                    for g in range(G + 1):
                        if g < G:
                            n = k * G + g
                            if not (isinstance(i, int) and h * G + g < 2):
                                pe.wait_ge(hid_ready, n - 1)
                            for u in range(SLOTS // 2):
                                t.matmul(psH[(h * G + g) % 2][:, u, :], K["w_self_a"][:, u, :], hT[:, g, :], start=True, stop=False)
                                last = t.matmul(psH[(h * G + g) % 2][:, u, :], K["w_self_b"][:, u, :], hT[:, g, :], start=False, stop=True)
                            last.then_inc(hid_ps, 1)
                        if g > 0:
                            pe.wait_ge(hid_ready, k * G + g)
                            for u in range(SLOTS // 2):
                                s0 = SLOTS * (g - 1) + 2 * u
                                last = t.matmul(psV[:, s0:s0 + 2, :].rearrange("p s f -> p (s f)"), hid[(h * G + g - 1) % 2][:, u, :], K["w_ref_out"][:, :], start=True, stop=True)
                            last.then_inc(vec_ps, 1)
            turns(pe, body, TURN)

        @block.scalar
        def _(act):
            def body(i):
                for h in range(2):
                    k = 2 * i + h
                    act.wait_ge(hT_ps, k + 1)
                    nc.scalar.activation(hT[:, :, :], psT[:, 0:G, :], ACT.Copy).then_inc(hT_ready, 1)
                    for g in range(G):
                        n = k * G + g
                        act.wait_ge(hid_ps, n + 1)
                        if not (isinstance(i, int) and h * G + g < 2):
                            act.wait_ge(vec_ps, n - 1)
                        nc.scalar.activation(hid[(h * G + g) % 2][:, :, :], psH[(h * G + g) % 2][:, :, :], ACT.Relu, bias=K["b_ref"][:, 0:1]).then_inc(hid_ready, 1)
                    act.wait_ge(var_ready, k + 1)
                    nc.scalar.activation(sums[:, 3, :], sums[:, 2, :], ACT.Sqrt, bias=K["eps"][:, 0:1], scale=1.0 / D0).then_inc(root_ready, 1)
                    act.wait_ge(ready, k + 1)
                    act.dma_start(slots(T["x"], k), xb[h][:, :, :]).then_inc(stored[h], 16)
                    act.dma_start(slots(T["h"], k), hb[h][:, :, :]).then_inc(stored[h], 16)
            turns(act, body, TURN)
            act.wait_ge(stored[0], 32 * TURN)
            act.wait_ge(stored[1], 32 * TURN)

        @block.gpsimd
        def _(pool):
            def body(i):
                for h in range(2):
                    k = 2 * i + h
                    if not isinstance(i, int):
                        wait_apart(pool, hT_ps, 2 * i + (h - 1), K["passed"])
                    wait_apart(pool, loaded[h], 80 * (i + 1), K["passed"])
                    pool.tensor_copy(feat[h][:, :, :], row[h][:, :, 0:D0]).then_inc(packed, 1)
            turns(pool, body, TURN)

        @block.vector
        def _(dve):
            v = nc.vector
            st = Steps(dve, step)
            bias = K["b_ref_out"][:, 0:D0]

            def body(i):
                st.begin(i)
                for h in range(2):
                    k = 2 * i + h
                    x = row[h][:, :, 0:D0]
                    dve.wait_ge(packed, k + 1)
                    dve.wait_ge(loaded[h], 80 * (i + 1))
                    if not isinstance(i, int):
                        dve.wait_ge(stored[h], 32 * i)
                    dve.wait_ge(vec_ps, (k + 1) * G)
                    v.tensor_tensor(vec[:, :, :], psV[:, 0:W, :], along(bias, W), ALU.add).then_inc(vec_used, 1)
                    dve.wait_ge(vec_used, k + 1)
                    st.link(v.tensor_tensor(prod[:, :, :], vec[:, :, :], vec[:, :, :], ALU.mult))
                    st.link(v.tensor_reduce(inv[:, :], prod[:, :, :], AX, ALU.add))
                    st.link(v.tensor_scalar(inv[:, :], inv[:, :], 1e-24, None, ALU.max))
                    st.link(v.reciprocal(inv[:, :], inv[:, :]))
                    for n in range(2):
                        st.link(v.tensor_tensor(prod[:, :, :], vec[:, :, :], x, ALU.mult))
                        st.link(v.tensor_reduce(dot[:, :], prod[:, :, :], AX, ALU.add))
                        st.link(v.scalar_tensor_tensor(dot[:, :], dot[:, :], 2.0, inv[:, :], ALU.mult, ALU.mult))
                        st.link(v.tensor_tensor(prod[:, :, :], vec[:, :, :], spread(dot[:, :], D0), ALU.mult))
                        st.link(v.tensor_tensor(y[:, :, :], x, prod[:, :, :], ALU.subtract))
                        x = y[:, :, :]
                    st.link(v.tensor_tensor(y[:, :, :], y[:, :, :], spread(ab[h][:, :, 2], D0), ALU.mult))
                    st.link(v.tensor_tensor(y[:, :, :], y[:, :, :], row[h][:, :, 0:D0], ALU.add))
                    for a in range(2):
                        st.link(v.tensor_tensor(y[:, :, :], y[:, :, :], acc[h][:, a, :, :], ALU.add))
                    st.link(v.scalar_tensor_tensor(xb[h][:, :, :], y[:, :, :], 0.0, xb[h][:, :, :], ALU.max, ALU.add))
                    normalise(v, st, (var_ready, root_ready), xb[h][:, :, :], sums, y[:, :, :], prod[:, :, :],
                              hb[h][:, :, :], D0, k + 1).then_inc(ready, 1)
            turns(dve, body, TURN)


def phase_encode(nc, K, z, T):
    S, W = z.S, SLOTS
    with ExitStack() as ctx:
        sb = lambda n, s, d: ctx.enter_context(nc.sbuf_tensor(n, s, d))
        sem = lambda n: ctx.enter_context(nc.semaphore(n))
        hb = [sb(f"e_h{h}", [P, W, D0], F32) for h in range(2)]
        ab = [sb(f"e_attr{h}", [P, W, 4], F32) for h in range(2)]
        hT = [sb(f"e_hT{h}", [P, P], F32) for h in range(2)]
        hid = [sb(f"e_hid{h}", [P, W, P], F32) for h in range(2)]
        feat = [sb(f"e_feat{h}", [P, W, D], F32) for h in range(2)]
        acc = [sb(f"e_acc{h}", [P, W, D], F32) for h in range(2)]
        psT = ctx.enter_context(nc.psum_tensor("e_psT", [P, P], F32))
        psH = ctx.enter_context(nc.psum_tensor("e_psH", [P, W, P], F32))
        psX = [ctx.enter_context(nc.psum_tensor(f"e_psX{h}", [P, W, D], F32)) for h in range(2)]
        loaded = [sem(f"e_loaded{h}") for h in range(2)]
        stored = [sem(f"e_stored{h}") for h in range(2)]
        hT_ps = sem("e_hT_ps"); hT_ready = sem("e_hT_ready"); hid_ps = sem("e_hid_ps"); hid_ready = sem("e_hid_ready")
        feat_ps = sem("e_feat_ps"); feat_ready = sem("e_feat_ready"); acc_ready = sem("e_acc_ready")
        block = ctx.enter_context(nc.Block())
        TURN = S // (2 * W)
        slots = lambda t, k: t[0:z.NP, :].rearrange("(p s) f -> p s f", s=S)[:, bass.ds(k * W, W), :]

        @block.sync
        def _(sp):
            def body(i):
                for h in range(2):
                    if not isinstance(i, int):
                        sp.wait_ge(acc_ready, 2 * i + (h - 1))
                    sp.dma_start(hb[h][:, :, :], slots(T["h"], 2 * i + h)).then_inc(loaded[h], 16)
                    sp.dma_start(ab[h][:, :, :], slots(T["attr"], 2 * i + h)).then_inc(loaded[h], 16)
            turns(sp, body, TURN)

        @block.tensor
        def _(pe):
            t = nc.tensor

            def body(i):
                for h in range(2):
                    k = 2 * i + h
                    pe.wait_ge(loaded[h], 32 * (i + 1))
                    t.transpose(psT[:, :], hb[h][:, :, :].rearrange("p s f -> p (s f)"), K["ident"][:, :]).then_inc(hT_ps, 1)
                    pe.wait_ge(hT_ready, k + 1)
                    for j in range(W):
                        last = t.matmul(psH[:, j, :], K["w_enc0"][:, j, :], hT[h][:, :], start=True, stop=True)
                    last.then_inc(hid_ps, 1)
                    pe.wait_ge(hid_ready, k + 1)
                    if not isinstance(i, int):
                        pe.wait_ge(feat_ready, 2 * i + (h - 1))
                    for j in range(W):
                        last = t.matmul(psX[h][:, j, :], hid[h][:, j, :], K["w_enc1"][:, :], start=True, stop=True)
                    last.then_inc(feat_ps, 1)
            turns(pe, body, TURN)

        @block.scalar
        def _(act):
            def body(i):
                for h in range(2):
                    k = 2 * i + h
                    act.wait_ge(hT_ps, k + 1)
                    nc.scalar.activation(hT[h][:, :], psT[:, :], ACT.Copy).then_inc(hT_ready, 1)
                    act.wait_ge(hid_ps, k + 1)
                    nc.scalar.activation(hid[h][:, :, :], psH[:, :, :], ACT.Relu, bias=K["b_enc0"][:, 0:1]).then_inc(hid_ready, 1)
                    act.wait_ge(acc_ready, k + 1)
                    act.dma_start(slots(T["feat"], k), feat[h][:, :, :]).then_inc(stored[h], 16)
                    act.dma_start(slots(T["acc"], k), acc[h][:, :, :]).then_inc(stored[h], 16)
            turns(act, body, TURN)
            act.wait_ge(stored[0], 32 * TURN)
            act.wait_ge(stored[1], 32 * TURN)

        @block.vector
        def _(dve):
            v = nc.vector

            def body(i):
                for h in range(2):
                    k = 2 * i + h
                    dve.wait_ge(feat_ps, k + 1)
                    if not isinstance(i, int):
                        dve.wait_ge(stored[h], 32 * i)
                    v.tensor_tensor(feat[h][:, :, :], psX[h][:, :, :], along(K["b_enc1"][:, :], W), ALU.add).then_inc(feat_ready, 1)
                    dve.wait_ge(feat_ready, k + 1)
                    dve.wait_ge(loaded[h], 32 * (i + 1))
                    v.tensor_tensor(acc[h][:, :, :], feat[h][:, :, :], spread(ab[h][:, :, 3], D), ALU.mult).then_inc(acc_ready, 1)
            turns(dve, body, TURN)


def phase_spread(nc, K, z, T, layer):
    B = ET * P
    c = f"s{layer}_"
    with ExitStack() as ctx:
        sb = lambda n, s, d: ctx.enter_context(nc.sbuf_tensor(c + n, s, d))
        sem = lambda n: ctx.enter_context(nc.semaphore(c + n))
        plan = [sb(f"plan{h}", [P, ET, 4], F32) for h in range(2)]
        row = [sb(f"row{h}", [P, ET, D], F32) for h in range(2)]
        same = sb("same", [P, ET, P], F32)
        total = [sb(f"total{h}", [P, ET, D], F32) for h in range(2)]
        psR = ctx.enter_context(nc.psum_tensor(c + "psR", [P, ET, P], F32))
        psS = ctx.enter_context(nc.psum_tensor(c + "psS", [P, ET, D], F32))
        plan_ready = [sem(f"plan_ready{h}") for h in range(2)]
        rows_ready = [sem(f"rows_ready{h}") for h in range(2)]
        numbers = sem("numbers"); same_ready = sem("same_ready"); sum_ps = sem("sum_ps")
        totals_ready = sem("totals_ready"); added = sem("added"); step = sem("step")
        block = ctx.enter_context(nc.Block())
        rows_of = lambda t, k: t[bass.ds(k * B, B), :].rearrange("(p j) w -> p j w", j=ET)

        @block.sync
        def _(sp):
            def body(i):
                for h in range(2):
                    if not isinstance(i, int):
                        sp.wait_ge(added, i * (32 * ET) + (h - 1) * (16 * ET))
                    sp.dma_start(plan[h][:, :, :], rows_of(T["plan"], 2 * i + h)).then_inc(plan_ready[h], 16)
            live_turns(sp, body, K["more"], z.PAIRS)

        @block.gpsimd
        def _(pool):
            def gather(h, n, m):
                if m is not None:
                    pool.wait_ge(sum_ps, m)
                wait_apart(pool, plan_ready[h], n, K["passed"])
                for j in range(ET):
                    pool.indirect_dma_start(row[h][:, j, :], None, T["feat"][:, :],
                                            bass.IndirectOffsetOnAxis(ap=plan[h][:, j, 0:1].bitcast(I32), axis=0)
                                            ).then_inc(rows_ready[h], 16)

            def scatter(h, n, k):
                wait_apart(pool, totals_ready, n, K["passed"])
                for j in range(ET):
                    pool.indirect_dma_start(T["acc"][:, :], bass.IndirectOffsetOnAxis(ap=plan[h][:, j, 1:2].bitcast(I32), axis=0),
                                            total[h][:, j, :], None, compute_op=ALU.add).then_inc(added, 16)
                    wait_apart(pool, added, k * (16 * ET) + 16 * (j + 1), K["passed"])

            def body(i):
                first = isinstance(i, int)
                gather(0, 16 * (i + 1), None if first else 2 * i + (-1))
                if not first:
                    scatter(1, 2 * i, 2 * i + (-1))
                gather(1, 16 * (i + 1), None if first else 2 * i)
                scatter(0, 2 * i + 1, 2 * i)

            more = live_turns(pool, body, K["more"], z.PAIRS)
            scatter(1, more * 2 + 2, more * 2 + 1)

        @block.tensor
        def _(pe):
            t = nc.tensor

            def body(i):
                for h in range(2):
                    k = 2 * i + h
                    pe.wait_ge(plan_ready[h], 16 * (i + 1))
                    if not (isinstance(i, int) and h == 0):
                        pe.wait_ge(same_ready, k)
                    for j in range(ET):
                        last = t.matmul(psR[:, j, :], plan[h][:, j, 2:3].to_broadcast([P, P]), K["ident"][:, :], start=True, stop=True)
                    last.then_inc(numbers, 1)
                    pe.wait_ge(same_ready, k + 1)
                    pe.wait_ge(rows_ready[h], (i + 1) * (16 * ET))
                    if not (isinstance(i, int) and h == 0):
                        pe.wait_ge(totals_ready, k)
                    for j in range(ET):
                        last = t.matmul(psS[:, j, :], same[:, j, :], row[h][:, j, :], start=True, stop=True)
                    last.then_inc(sum_ps, 1)
            live_turns(pe, body, K["more"], z.PAIRS)

        @block.vector
        def _(dve):
            v = nc.vector

            def body(i):
                for h in range(2):
                    k = 2 * i + h
                    dve.wait_ge(numbers, k + 1)
                    if not (isinstance(i, int) and h == 0):
                        dve.wait_ge(sum_ps, k)
                    for j in range(ET):
                        last = v.tensor_scalar(same[:, j, :], psR[:, j, :], plan[h][:, j, 2:3], plan[h][:, j, 3:4], ALU.is_equal, ALU.mult)
                    last.then_inc(same_ready, 1)
            live_turns(dve, body, K["more"], z.PAIRS)

        @block.scalar
        def _(act):
            def body(i):
                for h in range(2):
                    k = 2 * i + h
                    if not isinstance(i, int):
                        act.wait_ge(added, i * (32 * ET) + (h - 1) * (16 * ET))
                    act.wait_ge(sum_ps, k + 1)
                    nc.scalar.activation(total[h][:, :, :], psS[:, :, :], ACT.Copy).then_inc(totals_ready, 1)
            live_turns(act, body, K["more"], z.PAIRS)


def phase_convolve(nc, K, z, T, layer, decode):
    S, W = z.S, SLOTS
    c = f"v{layer}_"
    with ExitStack() as ctx:
        sb = lambda n, s, d: ctx.enter_context(nc.sbuf_tensor(c + n, s, d))
        sem = lambda n: ctx.enter_context(nc.semaphore(c + n))
        ps = lambda n, s: ctx.enter_context(nc.psum_tensor(c + n, s, F32))
        feat = [sb(f"feat{h}", [P, W, D], F32) for h in range(2)]
        acc = [sb(f"acc{h}", [P, W, D], F32) for h in range(2)]
        ab = [sb(f"attr{h}", [P, W, 4], F32) for h in range(2)]
        new = [sb(f"new{h}", [P, W, D], F32) for h in range(2)]
        nacc = [sb(f"nacc{h}", [P, W, D], F32) for h in range(2)]
        accT = sb("accT", [P, W, P], F32)
        summed = sb("summed", [P, W, D], F32)
        norm = sb("norm", [P, W, D], F32)
        stats = sb("stats", [P, W, 6], F32)
        mean = sb("mean", [P, 6, W], F32)
        psT = ps("psT", [P, W, P]); psY = ps("psY", [P, W, D])
        loaded = [sem(f"loaded{h}") for h in range(2)]
        stored = [sem(f"stored{h}") for h in range(2)]
        step = sem("step"); accT_ps = sem("accT_ps"); accT_ready = sem("accT_ready"); prod_ps = sem("prod_ps")
        prod_used = sem("prod_used"); var_ready = sem("var"); root_ready = sem("root"); ready = sem("ready")
        if decode:
            xb = [sb(f"x{h}", [P, W, D0], F32) for h in range(2)]
            ob = [sb(f"o{h}", [P, W, D0], F32) for h in range(2)]
            newT = sb("newT", [P, W, P], F32)
            hid = sb("hid", [P, W, P], F32)
            psD = ps("psD", [P, W, P]); psO = ps("psO", [P, W, D0])
            newT_ps = sem("newT_ps"); newT_ready = sem("newT_ready"); hid_ps = sem("hid_ps"); hid_ready = sem("hid_ready")
            out_ps = sem("out_ps"); new_ready = sem("new_ready")
        block = ctx.enter_context(nc.Block())
        TURN = S // (2 * W)
        LOADS = 16 * (4 if decode else 3)
        STORES = 16 * (1 if decode else 2)
        slots = lambda t, k: t[0:z.NP, :].rearrange("(p s) f -> p s f", s=S)[:, bass.ds(k * W, W), :]

        @block.sync
        def _(sp):
            def body(i):
                for h in range(2):
                    k = 2 * i + h
                    if not isinstance(i, int):
                        sp.wait_ge(ready, 2 * i + (h - 1))
                    sp.dma_start(acc[h][:, :, :], slots(T["acc"], k)).then_inc(loaded[h], 16)
                    sp.dma_start(feat[h][:, :, :], slots(T["feat"], k)).then_inc(loaded[h], 16)
                    sp.dma_start(ab[h][:, :, :], slots(T["attr"], k)).then_inc(loaded[h], 16)
                    if decode:
                        sp.dma_start(xb[h][:, :, :], slots(T["x"], k)).then_inc(loaded[h], 16)
            turns(sp, body, TURN)

        @block.tensor
        def _(pe):
            t = nc.tensor

            def body(i):
                for h in range(2):
                    k = 2 * i + h
                    pe.wait_ge(loaded[h], LOADS * (i + 1))
                    for j in range(W):
                        last = t.transpose(psT[:, j, :], acc[h][:, j, :], K["ident"][:, :])
                    last.then_inc(accT_ps, 1)
                    pe.wait_ge(accT_ready, k + 1)
                    if not (isinstance(i, int) and h == 0):
                        pe.wait_ge(prod_used, k)
                    for j in range(W):
                        last = t.matmul(psY[:, j, :], accT[:, j, :], K["w_conv"][:, :], start=True, stop=True)
                    last.then_inc(prod_ps, 1)
                    if decode:
                        pe.wait_ge(new_ready, k + 1)
                        for j in range(W):
                            last = t.transpose(psT[:, j, :], new[h][:, j, :], K["ident"][:, :])
                        last.then_inc(newT_ps, 1)
                        pe.wait_ge(newT_ready, k + 1)
                        for q in range(W // 4):
                            last = t.matmul(psD[:, 4 * q:4 * q + 4, :].rearrange("p j n -> p (j n)"), K["w_dec0"][:, :],
                                            newT[:, 4 * q:4 * q + 4, :].rearrange("p j n -> p (j n)"), start=True, stop=True)
                        last.then_inc(hid_ps, 1)
                        pe.wait_ge(hid_ready, k + 1)
                        for j in range(W):
                            last = t.matmul(psO[:, j, :], hid[:, j, :], K["w_dec1"][:, :], start=True, stop=True)
                        last.then_inc(out_ps, 1)
            turns(pe, body, TURN)

        @block.scalar
        def _(act):
            def body(i):
                for h in range(2):
                    k = 2 * i + h
                    act.wait_ge(accT_ps, k + 1)
                    nc.scalar.activation(accT[:, :, :], psT[:, :, :], ACT.Copy).then_inc(accT_ready, 1)
                    act.wait_ge(var_ready, k + 1)
                    nc.scalar.activation(mean[:, 4, :], mean[:, 3, :], ACT.Sqrt, bias=K["eps"][:, 0:1]).then_inc(root_ready, 1)
                    if decode:
                        act.wait_ge(newT_ps, k + 1)
                        nc.scalar.activation(newT[:, :, :], psT[:, :, :], ACT.Copy).then_inc(newT_ready, 1)
                        act.wait_ge(hid_ps, k + 1)
                        nc.scalar.activation(hid[:, :, :], psD[:, :, :], ACT.Relu, bias=K["b_dec0"][:, 0:1]).then_inc(hid_ready, 1)
                    act.wait_ge(ready, k + 1)
                    if decode:
                        act.dma_start(slots(T["out"], k), ob[h][:, :, :]).then_inc(stored[h], 16)
                    else:
                        act.dma_start(slots(T["feat"], k), new[h][:, :, :]).then_inc(stored[h], 16)
                        act.dma_start(slots(T["acc"], k), nacc[h][:, :, :]).then_inc(stored[h], 16)
            turns(act, body, TURN)
            act.wait_ge(stored[0], STORES * TURN)
            act.wait_ge(stored[1], STORES * TURN)

        @block.vector
        def _(dve):
            v = nc.vector
            st = Steps(dve, step)

            def body(i):
                st.begin(i)
                for h in range(2):
                    k = 2 * i + h
                    dve.wait_ge(loaded[h], LOADS * (i + 1))
                    if not isinstance(i, int):
                        dve.wait_ge(stored[h], STORES * i)
                    st.link(v.tensor_tensor(summed[:, :, :], feat[h][:, :, :], along(K["b_conv"][:, :], W), ALU.add))
                    dve.wait_ge(prod_ps, k + 1)
                    v.tensor_tensor(summed[:, :, :], summed[:, :, :], psY[:, :, :], ALU.add).then_inc(prod_used, 1)
                    dve.wait_ge(prod_used, k + 1)
                    for j in range(W):
                        last = v.bn_stats(stats[:, j, :], summed[:, j, :])
                    st.link(last)
                    m0, m1, q0, q1 = (stats[:, :, n] for n in (1, 4, 2, 5))
                    v.tensor_tensor(mean[:, 0, :], m0, m1, ALU.add)
                    v.tensor_tensor(mean[:, 1, :], m0, m1, ALU.subtract)
                    st.link(v.tensor_tensor(mean[:, 2, :], q0, q1, ALU.add))
                    v.tensor_scalar(mean[:, 0, :], mean[:, 0, :], 0.5, None, ALU.mult)
                    st.link(v.scalar_tensor_tensor(mean[:, 1, :], mean[:, 1, :], 0.25, mean[:, 1, :], ALU.mult, ALU.mult))
                    v.scalar_tensor_tensor(mean[:, 3, :], mean[:, 2, :], 1.0 / D, mean[:, 1, :], ALU.mult, ALU.add).then_inc(var_ready, 1)
                    dve.wait_ge(root_ready, k + 1)
                    st.link(v.reciprocal(mean[:, 5, :], mean[:, 4, :]))
                    for j in range(W):
                        last = v.tensor_scalar(norm[:, j, :], summed[:, j, :], mean[:, 0, j:j + 1], mean[:, 5, j:j + 1], ALU.subtract, ALU.mult)
                    st.link(last)
                    st.link(v.tensor_tensor(norm[:, :, :], norm[:, :, :], along(K["ln_g"][:, :], W), ALU.mult))
                    last = v.tensor_tensor(new[h][:, :, :], norm[:, :, :], along(K["ln_b"][:, :], W), ALU.add)
                    if not decode:
                        st.link(last)
                        v.tensor_tensor(nacc[h][:, :, :], new[h][:, :, :], spread(ab[h][:, :, 3], D), ALU.mult).then_inc(ready, 1)
                    else:
                        last.then_inc(new_ready, 1)
                        st.link(v.tensor_tensor(ob[h][:, :, :], xb[h][:, :, :], along(K["b_dec1"][:, :], W), ALU.add))
                        dve.wait_ge(out_ps, k + 1)
                        v.tensor_tensor(ob[h][:, :, :], ob[h][:, :, :], psO[:, :, :], ALU.add).then_inc(ready, 1)
            turns(dve, body, TURN)


def phase_out(nc, z, T, out):
    with nc.semaphore("o_written") as written, nc.Block() as block:
        @block.sync
        def _(sp):
            sp.dma_start(out[:, :], T["out"][0:z.N, :]).then_inc(written, 16)
            sp.wait_ge(written, 16)


def gnn_kernel(nc, x, src, dst, w, out, stop=99):
    z = Shapes(x.shape[0], src.shape[0])
    T = {}
    for name, rows, width, dt in (
        ("x", z.NP, D0, F32), ("h", z.NP, D0, F32), ("out", z.NP, D0, F32),
        ("attr", z.NP, 4, F32),
        ("rows", z.NP, TW, F32),
        ("acc_s", z.NP + P, D0, F32), ("acc_d", z.NP + P, D0, F32),
        ("edges", z.CAP, 2, I32),
        ("plan", z.CAP, 4, F32),
        ("feat", z.NP, D, F32), ("acc", z.NP + P, D, F32),
    ):
        T[name] = nc.dram_tensor("scratch_" + name, [rows, width], dt).ap()
    with ExitStack() as ctx:
        K = {name: ctx.enter_context(nc.sbuf_tensor("k_" + name, shape, dt)) for name, shape, dt in (
            ("iota", [P, max(z.S, P)], F16), ("ident", [P, P], F32), ("earlier", [P, P], F32),
            ("before", [P, P], F32), ("ones", [P, P], F32), ("trash", [P, 1], F32), ("eps", [P, 1], F32),
            ("more", [P, 1], I32),
            ("w_ref", [64, P], F32), ("b_ref", [P, 1], F32),
            ("w_ref_out", [P, 2 * D0], F32), ("b_ref_out", [P, 2 * D0], F32),
            ("w_self_a", [P, SLOTS // 2, P], F32), ("w_self_b", [P, SLOTS // 2, P], F32),
            ("w_enc0", [P, SLOTS, D], F32), ("b_enc0", [P, 1], F32),
            ("w_enc1", [D, D], F32), ("b_enc1", [P, D], F32),
            ("w_conv", [D, D], F32), ("b_conv", [P, D], F32), ("ln_g", [P, D], F32), ("ln_b", [P, D], F32),
            ("w_dec0", [D, D], F32), ("b_dec0", [P, 1], F32), ("w_dec1", [D, D0], F32), ("b_dec1", [P, D0], F32),
        )}
        K["passed"] = ctx.enter_context(nc.semaphore("passed"))
        phase_constants(nc, K, z, w)
        phase_edges(nc, K, z, src, dst, T, x)
        if stop == 1: return T
        phase_rows(nc, K, z, T)
        if stop == 2: return T
        phase_reflect_edges(nc, K, z, T)
        if stop == 3: return T
        phase_reflect_nodes(nc, K, z, T)
        if stop == 4: return T
        phase_encode(nc, K, z, T)
        if stop == 5: return T
        for layer in range(3):
            phase_spread(nc, K, z, T, layer)
            if stop == 6: return T
            phase_convolve(nc, K, z, T, layer, decode=layer == 2)
            if stop == 7: return T
        phase_out(nc, z, T, out)
    return T


_WEIGHTS = ["L0_gnn_W1", "L0_gnn_b1", "L0_gnn_W2", "L0_gnn_b2", "L1_gnn_W_enc0", "L1_gnn_b_enc0",
            "L1_gnn_W_enc1", "L1_gnn_b_enc1", "L1_gnn_W_conv", "L1_gnn_b_conv", "L1_gnn_ln_g",
            "L1_gnn_ln_b", "L1_gnn_W_dec0", "L1_gnn_b_dec0", "L1_gnn_W_dec1", "L1_gnn_b_dec1"]


def kernel(**inputs):
    import numpy as _np
    import concourse.bacc as _bacc
    from concourse import mybir as _mybir
    from concourse.bass_utils import run_bass_kernel_spmd as _run

    nc = _bacc.Bacc("TRN2", target_bir_lowering=False, num_devices=1)
    arrays, aps = {}, {}
    for name in ["x", "src", "dst", *_WEIGHTS]:
        a = _np.ascontiguousarray(inputs[name])
        arrays[f"in_{name}_dram"] = a
        aps[name] = nc.dram_tensor(f"in_{name}_dram", a.shape, _mybir.dt.from_np(a.dtype), kind="ExternalInput").ap()
    out = nc.dram_tensor("out_0_dram", aps["x"].shape, _mybir.dt.float32, kind="ExternalOutput").ap()
    gnn_kernel(nc, aps["x"], aps["src"], aps["dst"], {n: aps[n] for n in _WEIGHTS}, out)
    r = _run(nc, [arrays], core_ids=[0])
    return _np.asarray(r.results[0]["out_0_dram"])
```

```python
import concourse.bass as bass
from concourse import mybir
from contextlib import ExitStack

F32 = mybir.dt.float32
F16 = mybir.dt.float16
I32 = mybir.dt.int32
ALU = mybir.AluOpType
ACT = mybir.ActivationFunctionType
AX = mybir.AxisListType.X

P = 128
D0 = 16
HID = 64
D = 128
TW = D0 + 2
WIDE = 56
SLOTS = 8
ET = 8
LN_EPS = 1e-5
FAR = 1 << 20


class Steps:

    def __init__(self, eng, sem):
        self.eng, self.sem, self.base, self.n, self.per = eng, sem, 0, 0, 0

    def begin(self, k):
        if isinstance(k, int) and k == 0:
            self.base = 0
        else:
            self.per = self.per or self.n
            self.base = k * self.per
        self.n = 0

    def link(self, ins):
        ins.then_inc(self.sem, 1)
        self.n += 1
        self.eng.wait_ge(self.sem, self.base + self.n)


class Block:

    def __init__(self, i, h, lag):
        back = -((h - lag) // 2)
        self.h = (h - lag) % 2
        self.turn = i - back if isinstance(i, int) else (i + (-back) if back else i)
        self.k = 2 * i + (h - lag)

    def after(self, n):
        return not isinstance(self.k, int) or self.k >= n


def staged(eng, stages, n):
    def at(i, h, wanted):
        for lag, work in stages:
            if wanted(lag):
                work(Block(i, h, lag))

    most = max(lag for lag, _ in stages)
    first = -(-(most + 2) // 2)
    for i in range(min(first, n)):
        for h in range(2):
            at(i, h, lambda lag: 2 * i + h >= lag)
    if n > first:
        with eng.Fori(first, n) as i:
            for h in range(2):
                at(i, h, lambda lag: True)
    for i in range(n, n + (most + 1) // 2):
        for h in range(2):
            at(i, h, lambda lag: 2 * n <= 2 * i + h < 2 * n + lag)


def spread(ap, n):
    return ap.unsqueeze(len(ap.shape)).to_broadcast([*ap.shape, n])


def along(ap, n):
    return ap.unsqueeze(1).to_broadcast([ap.shape[0], n, ap.shape[1]])


def turns(eng, body, n):
    body(0)
    if n > 1:
        with eng.Fori(1, n) as i:
            body(i)


def live_turns(eng, body, more_sb, n):
    more = eng.value_load(more_sb[0:1, 0:1], min_val=0, max_val=n - 1)
    body(0)
    if n > 1:
        with eng.Fori(1, n) as i:
            with eng.If(i <= more):
                body(i)
            eng.nop()
    return more


def wait_apart(eng, sem, value, passed):
    eng.wait_ge(sem, value)
    eng.sem_inc(passed, 1)


def cleared_after(nc, ctx, prefix=""):
    made = []

    def clear():
        nc.clear_and_free_semaphores(made)
        nc.all_engine_barrier()

    ctx.callback(clear)

    def sem(name):
        made.append(nc.alloc_semaphore(prefix + name))
        return made[-1]

    return sem


class Shapes:
    def __init__(self, N, E):
        self.N, self.E = N, E
        unit = 2 * WIDE
        self.S = -(-N // (P * unit)) * unit
        self.NP = P * self.S
        self.PAD = self.NP - 1
        self.TRASH = self.NP
        self.L = -(-E // (P * ET)) * ET
        self.PAIRS = -(-E // (2 * ET * P))
        self.CAP = (self.PAIRS + 1) * 2 * ET * P
        assert N < self.NP and self.S % (2 * SLOTS) == 0 and self.S // 2 <= 512
        assert self.NP + 2 * P < FAR and self.CAP < FAR


def phase_edges(nc, K, z, src, dst, T, x):
    S, L, half = z.S, z.L, z.S // 2
    with ExitStack() as ctx:
        sb = lambda n, s, d: ctx.enter_context(nc.sbuf_tensor(n, s, d))
        sem = lambda n: ctx.enter_context(nc.semaphore(n))
        ends = sb("a_ends", [P, 2, L], I32)
        endf = sb("a_endf", [P, 2, L], F32)
        quo = sb("a_quo", [P, 2, L], F32)
        quo_i = sb("a_quo_i", [P, 2, L], I32)
        tmp = sb("a_tmp", [P, 2, L], F32)
        keys = sb("a_keys", [P, L, 5], F32)
        item = sb("a_item", [P, L, 3], I32)
        kept = sb("a_kept", [P, L], F32)
        rank = sb("a_rank", [P, L], F32)
        onesL = sb("a_onesL", [P, L], F32)
        base = sb("a_base", [P, 4], F32)
        count_f = sb("a_count_f", [P, 2], F32)
        count_i = sb("a_count_i", [P, 2], I32)
        fill = sb("a_fill", [P, 2 * z.CAP // P], I32)
        keyb = [sb(f"a_keyb{h}", [P, ET, 5], F32) for h in range(2)]
        itemb = [sb(f"a_itemb{h}", [P, ET, 3], I32) for h in range(2)]
        hot_slot = [sb(f"a_hot_slot{h}", [P, 2, S], F16) for h in range(2)]
        hot_part = [sb(f"a_hot_part{h}", [P, 3, P], F16) for h in range(2)]
        hist = sb("a_hist", [P, 3, S], F32)
        attr = sb("a_attr", [P, S, 4], F32)
        root = sb("a_root", [P, 2, S], F32)
        zero = sb("a_zero", [P, S * D0 // 4], F32)
        zero16 = sb("a_zero16", [P, P], F16)
        ps = [ctx.enter_context(nc.psum_tensor(f"a_ps{j}", [P, 512], F32)) for j in range(6)]
        psb = ctx.enter_context(nc.psum_tensor("a_psb", [P, 4], F32))

        ends_ready = sem("a_ends_ready"); ends_padded = sem("a_ends_padded"); zero_ready = sem("a_zero_ready")
        step = sem("a_step"); totals = sem("a_totals"); bases = sem("a_bases")
        fill_ready = sem("a_fill_ready"); filled = sem("a_filled")
        items_ready = sem("a_items_ready")
        keyb_ready = [sem(f"a_keyb_ready{h}") for h in range(2)]
        itemb_ready = [sem(f"a_itemb_ready{h}") for h in range(2)]
        hot_ready = sem("a_hot_ready"); hot_used = sem("a_hot_used")
        packed = [sem(f"a_packed{h}") for h in range(2)]
        hist_done = sem("a_hist_done"); roots = sem("a_roots"); deg_ready = sem("a_deg_ready")
        attr_ready = sem("a_attr_ready"); stored = sem("a_stored"); zeroed = sem("a_zeroed")
        block = ctx.enter_context(nc.Block())
        NB = L // ET
        TURN = NB // 2
        full = z.E // L
        rest = z.E - full * L
        nfull = z.N // S
        nrest = z.N - nfull * S

        @block.sync
        def _(sp):
            sp.wait_ge(ends_padded, 1)
            for a, v in enumerate((src, dst)):
                sp.dma_start(ends[0:full, a, :], v[0:full * L].rearrange("(p c) -> p c", c=L)).then_inc(ends_ready, 16)
                sp.dma_start(ends[full:full + 1, a, 0:rest], v[full * L:z.E].rearrange("(p c) -> p c", p=1)).then_inc(ends_ready, 16)
            sp.wait_ge(fill_ready, 1)
            sp.dma_start(T["edges"].rearrange("(p c) w -> p (c w)", p=P), fill[:, :]).then_inc(filled, 16)
            sp.wait_ge(zero_ready, 1)
            for name in ("acc_s", "acc_d"):
                for q in range(4):
                    w = S * D0 // 4
                    sp.dma_start(T[name][0:z.NP, :].rearrange("(p s) f -> p (s f)", s=S)[:, q * w:(q + 1) * w], zero[:, :]).then_inc(zeroed, 16)
                sp.dma_start(T[name][z.NP:z.NP + 2 * P, :].rearrange("(p a) f -> p (a f)", a=2), zero[:, 0:2 * D0]).then_inc(zeroed, 16)
            sp.dma_start(T["acc"][z.NP:z.NP + 2 * P, :].rearrange("(p a) f -> p (a f)", a=2), zero[:, 0:2 * D]).then_inc(zeroed, 16)
            sp.dma_start(T["x"][0:z.N, :], x[:, :]).then_inc(zeroed, 16)
            left = z.NP - z.N
            sp.dma_start(T["x"][z.N:z.NP, :].rearrange("(p c) f -> p (c f)", c=D0), zero[0:left // D0, 0:D0 * D0]).then_inc(zeroed, 16)
            sp.wait_ge(items_ready, 1)

            def body(i):
                for h in range(2):
                    if not isinstance(i, int):
                        sp.wait_ge(hot_ready, i * (2 * ET) + (h - 1) * ET)
                    c = (2 * i + h) * ET
                    sp.dma_start(keyb[h][:, :, :], keys[:, bass.ds(c, ET), :]).then_inc(keyb_ready[h], 16)
                    if not isinstance(i, int):
                        sp.wait_ge(packed[h], i * (16 * ET))
                    sp.dma_start(itemb[h][:, :, :], item[:, bass.ds(c, ET), :]).then_inc(itemb_ready[h], 16)

            turns(sp, body, TURN)
            if NB % 2:
                sp.wait_ge(hot_ready, (NB - 2) * ET)
                sp.dma_start(keyb[0][:, :, :], keys[:, L - ET:L, :]).then_inc(keyb_ready[0], 16)
                sp.wait_ge(packed[0], TURN * 16 * ET)
                sp.dma_start(itemb[0][:, :, :], item[:, L - ET:L, :]).then_inc(itemb_ready[0], 16)
            sp.wait_ge(attr_ready, 1)
            sp.dma_start(T["attr"].rearrange("(p s) f -> p s f", s=S), attr[:, :, :]).then_inc(stored, 16)
            sp.wait_ge(stored, 16)
            sp.wait_ge(filled, 16)
            sp.wait_ge(zeroed, 16 * 13)

        @block.gpsimd
        def _(pool):
            pool.memset(ends[:, :, :], z.PAD).then_inc(ends_padded, 1)
            pool.memset(fill[:, :], z.PAD).then_inc(fill_ready, 1)

            def scatter(h, n):
                pool.wait_ge(filled, 16)
                wait_apart(pool, itemb_ready[h], n, K["passed"])
                for j in range(ET):
                    pool.indirect_dma_start(
                        T["edges"][:, :], bass.IndirectOffsetOnAxis(ap=itemb[h][:, j, 0:1], axis=0),
                        itemb[h][:, j, 1:3], None, bounds_check=z.CAP - 1, oob_is_err=False,
                    ).then_inc(packed[h], 16)

            def body(i):
                for h in range(2):
                    scatter(h, 16 * (i + 1))

            turns(pool, body, TURN)
            if NB % 2:
                scatter(0, 16 * (TURN + 1))
            pool.wait_ge(packed[0], 16 * ET * ((NB + 1) // 2))
            pool.wait_ge(packed[1], 16 * ET * (NB // 2))

        @block.scalar
        def _(act):
            act.wait_ge(deg_ready, 1)
            nc.scalar.activation(root[:, :, :], root[:, :, :], ACT.Sqrt).then_inc(roots, 1)

        @block.vector
        def _(dve):
            v = nc.vector
            st = Steps(dve, step)
            v.memset(zero[:, :], 0.0).then_inc(zero_ready, 1)
            v.memset(onesL[:, :], 1.0)
            st.link(v.memset(zero16[:, :], 0.0))
            dve.wait_ge(ends_ready, 64)
            v.tensor_copy(item[:, :, 1:3].rearrange("p c a -> p a c"), ends[:, :, :])
            st.link(v.tensor_copy(endf[:, :, :], ends[:, :, :]))
            st.link(v.tensor_scalar(quo[:, :, :], endf[:, :, :], 1.0 / S, None, ALU.mult))
            st.link(v.tensor_copy(quo_i[:, :, :], quo[:, :, :]))
            st.link(v.tensor_copy(quo[:, :, :], quo_i[:, :, :]))
            st.link(v.scalar_tensor_tensor(tmp[:, :, :], quo[:, :, :], -float(S), endf[:, :, :], ALU.mult, ALU.add))
            st.link(v.tensor_scalar(tmp[:, :, :], tmp[:, :, :], 0.0, None, ALU.is_lt))
            st.link(v.tensor_tensor(quo[:, :, :], quo[:, :, :], tmp[:, :, :], ALU.subtract))
            st.link(v.scalar_tensor_tensor(tmp[:, :, :], quo[:, :, :], -float(S), endf[:, :, :], ALU.mult, ALU.add))
            st.link(v.tensor_scalar(tmp[:, :, :], tmp[:, :, :], float(S), None, ALU.is_ge))
            st.link(v.tensor_tensor(quo[:, :, :], quo[:, :, :], tmp[:, :, :], ALU.add))
            st.link(v.scalar_tensor_tensor(tmp[:, :, :], quo[:, :, :], -float(S), endf[:, :, :], ALU.mult, ALU.add))
            v.tensor_copy(keys[:, :, 0:2].rearrange("p c a -> p a c"), tmp[:, :, :])
            v.tensor_copy(keys[:, :, 2:4].rearrange("p c a -> p a c"), quo[:, :, :])
            st.link(v.tensor_tensor(kept[:, :], endf[:, 0, :], endf[:, 1, :], ALU.not_equal))
            v.tensor_scalar(keys[:, :, 4], kept[:, :], -1.0, 1.0, ALU.mult, ALU.add)
            st.link(v.tensor_tensor_scan(rank[:, :], onesL[:, :], kept[:, :], 0.0, ALU.mult, ALU.add))
            st.link(v.tensor_copy(count_f[:, 0:1], rank[:, L - 1:L]))
            v.tensor_copy(count_f[:, 1:2], rank[:, L - 1:L]).then_inc(totals, 1)
            dve.wait_ge(bases, 1)
            st.link(v.tensor_copy(base[:, 0:2], psb[:, 0:2]))
            st.link(v.tensor_scalar(rank[:, :], rank[:, :], base[:, 0:1], -1.0, ALU.add, ALU.add))
            st.link(v.scalar_tensor_tensor(rank[:, :], keys[:, :, 4], float(FAR), rank[:, :], ALU.mult, ALU.add))
            st.link(v.tensor_copy(item[:, :, 0], rank[:, :]))
            both = 2 * ET * P
            st.link(v.tensor_scalar(base[:, 2:3], base[:, 1:2], -1.0, 0.0, ALU.add, ALU.max))
            st.link(v.tensor_copy(count_i[:, 0:1], base[:, 2:3]))
            st.link(v.tensor_scalar(K["more"][:, :], count_i[:, 0:1], both.bit_length() - 1, None, ALU.logical_shift_right))
            v.tensor_copy(count_i[:, 1:2], K["more"][:, :]).then_inc(items_ready, 1)

            def hot(h, n, first):
                dve.wait_ge(keyb_ready[h], n)
                for j in range(ET):
                    q = j % 2
                    if not (first and h == 0 and j < 2):
                        dve.wait_ge(hot_used, hot.base + ET * h + j - 1)
                    v.tensor_scalar(hot_slot[q][:, 0, :], K["iota"][:, 0:S], keyb[h][:, j, 0:1], None, ALU.is_equal)
                    v.tensor_scalar(hot_slot[q][:, 1, :], K["iota"][:, 0:S], keyb[h][:, j, 1:2], None, ALU.is_equal)
                    v.tensor_scalar(hot_part[q][:, 0, :], K["iota"][:, 0:P], keyb[h][:, j, 2:3], None, ALU.is_equal)
                    v.tensor_scalar(hot_part[q][:, 1, :], K["iota"][:, 0:P], keyb[h][:, j, 3:4], None, ALU.is_equal)
                    last = v.tensor_scalar(hot_part[q][:, 2, :], K["iota"][:, 0:P], keyb[h][:, j, 3:4], keyb[h][:, j, 4:5], ALU.is_equal, ALU.mult)
                    last.then_inc(hot_ready, 1)

            def body(i):
                hot.base = i * (2 * ET)
                for h in range(2):
                    hot(h, 16 * (i + 1), isinstance(i, int))

            turns(dve, body, TURN)
            if NB % 2:
                hot.base = TURN * 2 * ET
                hot(0, 16 * (TURN + 1), False)

            dve.wait_ge(hist_done, 1)
            for k in range(3):
                for q in range(2):
                    last = v.tensor_copy(hist[:, k, q * half:(q + 1) * half], ps[2 * k + q][:, 0:half])
            st.link(last)
            st.link(v.tensor_tensor(root[:, 0, :], hist[:, 0, :], hist[:, 1, :], ALU.add))
            v.tensor_scalar(root[:, 0, :], root[:, 0, :], 1e-5, None, ALU.max)
            v.tensor_scalar(root[:, 1, :], hist[:, 1, :], 1.0, None, ALU.add).then_inc(deg_ready, 1)
            dve.wait_ge(roots, 1)
            st.link(v.reciprocal(root[:, :, :], root[:, :, :]))
            v.tensor_copy(attr[:, :, 0:2].rearrange("p s a -> p a s"), root[:, :, :])
            v.tensor_scalar(hist[:, 0, :], hist[:, 2, :], 2.0, None, ALU.mult)
            st.link(v.tensor_scalar(hist[:, 1, :], hist[:, 2, :], 1.0, None, ALU.add))
            st.link(v.tensor_tensor(hist[:, 0:2, :], hist[:, 0:2, :], root[:, :, :], ALU.mult))
            v.tensor_tensor(attr[:, :, 2:4].rearrange("p s a -> p a s"), hist[:, 0:2, :], root[:, :, :], ALU.mult).then_inc(attr_ready, 1)

        @block.tensor
        def _(pe):
            t = nc.tensor
            pe.wait_ge(totals, 1)
            t.matmul(psb[:, 0:1], K["before"][:, :], count_f[:, 0:1], start=True, stop=True)
            t.matmul(psb[:, 1:2], K["ones"][:, :], count_f[:, 1:2], start=True, stop=True).then_inc(bases, 1)
            for j in range(6):
                t.matmul(ps[j][:, 0:half], zero16[:, :], K["iota"][:, 0:half], start=True, stop=False)

            def add(n, j):
                q = j % 2
                pe.wait_ge(hot_ready, n)
                for k, (part, slot) in enumerate(((0, 0), (1, 1), (2, 1))):
                    for w in range(2):
                        last = t.matmul(ps[2 * k + w][:, 0:half], hot_part[q][:, part, :],
                                        hot_slot[q][:, slot, w * half:(w + 1) * half], start=False, stop=False)
                last.then_inc(hot_used, 1)

            def body(i):
                for j in range(2 * ET):
                    add(i * (2 * ET) + j + 1, j)

            turns(pe, body, TURN)
            if NB % 2:
                for j in range(ET):
                    add(TURN * 2 * ET + j + 1, j)
            for j in range(6):
                last = t.matmul(ps[j][:, 0:half], zero16[:, :], K["iota"][:, 0:half], start=False, stop=True)
            last.then_inc(hist_done, 1)




def phase_constants(nc, K, z, w):
    with ExitStack() as ctx:
        sb = lambda n, s, d: ctx.enter_context(nc.sbuf_tensor(n, s, d))
        sem = cleared_after(nc, ctx)
        wide = sb("c_wide", [P, max(z.S, P)], I32)
        diff = sb("c_diff", [P, P], I32)
        chan = sb("c_chan", [P, ET], I32)
        patterns = sem("c_patterns"); cleared = sem("c_cleared"); loaded = sem("c_loaded")
        made = sem("c_made")
        block = ctx.enter_context(nc.Block())

        @block.gpsimd
        def _(pool):
            pool.iota(wide[:, :], [[1, max(z.S, P)]], base=0, channel_multiplier=0)
            pool.iota(diff[:, :], [[1, P]], base=0, channel_multiplier=-1)
            pool.iota(chan[:, :], [[0, ET // 2], [P, 2]], base=z.TRASH, channel_multiplier=1).then_inc(patterns, 1)

        @block.vector
        def _(dve):
            v = nc.vector
            for name in ("w_ref", "w_ref_out", "w_self_a", "w_self_b", "w_enc0"):
                last = v.memset(K[name][...], 0.0)
            last.then_inc(cleared, 1)
            v.memset(K["ones"][:, :], 1.0)
            v.memset(K["eps"][:, :], LN_EPS)
            dve.wait_ge(patterns, 1)
            v.tensor_copy(K["iota"][:, :], wide[:, :])
            v.tensor_copy(K["trash"][:, :], chan[:, :])
            v.tensor_scalar(K["ident"][:, :], diff[:, :], 0.0, None, ALU.is_equal)
            v.tensor_scalar(K["earlier"][:, :], diff[:, :], 0.0, None, ALU.is_lt)
            v.tensor_scalar(K["before"][:, :], diff[:, :], 0.0, None, ALU.is_gt).then_inc(made, 1)

        @block.sync
        def _(sp):
            n = 0

            def load(out, in_):
                sp.dma_start(out, in_, allow_slow_non_contiguous=True).then_inc(loaded, 16)

            sp.wait_ge(cleared, 1)
            own = w["L0_gnn_W1"][:, 0:D0].rearrange("m k -> k m")
            other = w["L0_gnn_W1"][:, D0:2 * D0].rearrange("m k -> k m")
            W2T = w["L0_gnn_W2"].rearrange("o h -> h o")
            load(K["w_ref"][0:D0, 0:HID], own)
            load(K["w_ref"][0:D0, HID:P], other)
            load(K["w_ref"][TW:TW + D0, 0:HID], other)
            load(K["w_ref"][TW:TW + D0, HID:P], own)
            load(K["w_ref_out"][0:HID, 0:D0], W2T)
            load(K["w_ref_out"][HID:P, D0:2 * D0], W2T)
            n += 6
            for j in range(SLOTS):
                rows = slice(D0 * j, D0 * (j + 1))
                cols = slice(HID * (j % 2), HID * (j % 2 + 1))
                load(K["w_self_a"][rows, j // 2, cols], own)
                load(K["w_self_b"][rows, j // 2, cols], other)
                load(K["w_enc0"][rows, j, :], w["L1_gnn_W_enc0"])
                n += 3
            for a in range(2):
                load(K["b_ref"][HID * a:HID * (a + 1), :], w["L0_gnn_b1"].rearrange("(m a) -> m a", a=1))
                load(K["b_ref_out"][:, D0 * a:D0 * (a + 1)], w["L0_gnn_b2"].partition_broadcast(P))
                n += 2
            for name in ("enc1", "conv", "dec0", "dec1"):
                load(K["w_" + name][:, :], w["L1_gnn_W_" + name])
                n += 1
            for name in ("b_enc0", "b_dec0"):
                load(K[name][:, :], w["L1_gnn_" + name].rearrange("(m a) -> m a", a=1))
                n += 1
            for name in ("b_enc1", "b_conv", "b_dec1", "ln_g", "ln_b"):
                load(K[name][:, :], w["L1_gnn_" + name].partition_broadcast(P))
                n += 1
            sp.wait_ge(loaded, 16 * n)


def normalise(v, st, act_turn, x, sums, centred, square, out, width, n):
    st.link(v.tensor_reduce(sums[:, 0, :], x, AX, ALU.add))
    st.link(v.tensor_scalar(sums[:, 1, :], sums[:, 0, :], 1.0 / width, None, ALU.mult))
    st.link(v.tensor_tensor(centred, x, spread(sums[:, 1, :], width), ALU.subtract))
    st.link(v.tensor_tensor(square, centred, centred, ALU.mult))
    v.tensor_reduce(sums[:, 2, :], square, AX, ALU.add).then_inc(act_turn[0], 1)
    st.eng.wait_ge(act_turn[1], n)
    st.link(v.reciprocal(sums[:, 3, :], sums[:, 3, :]))
    st.link(v.tensor_tensor(square, centred, spread(sums[:, 3, :], width), ALU.mult))
    return v.tensor_scalar(out, square, 0.0, None, ALU.max)


def phase_rows(nc, K, z, T):
    S, W = z.S, WIDE
    with ExitStack() as ctx:
        sb = lambda n, s, d: ctx.enter_context(nc.sbuf_tensor(n, s, d))
        sem = cleared_after(nc, ctx)
        xb = [sb(f"b_x{h}", [P, W, D0], F32) for h in range(2)]
        ab = [sb(f"b_attr{h}", [P, W, 4], F32) for h in range(2)]
        row = [sb(f"b_row{h}", [P, W, TW], F32) for h in range(2)]
        centred = sb("b_centred", [P, W, D0], F32)
        square = sb("b_square", [P, W, D0], F32)
        sums = sb("b_sums", [P, 4, W], F32)
        loaded = [sem(f"b_loaded{h}") for h in range(2)]
        stored = [sem(f"b_stored{h}") for h in range(2)]
        step = sem("b_step"); ready = sem("b_ready"); var_ready = sem("b_var"); root_ready = sem("b_root")
        block = ctx.enter_context(nc.Block())
        TURN = S // (2 * W)
        slots = lambda t, k: t[0:z.NP, :].rearrange("(p s) f -> p s f", s=S)[:, bass.ds(k * W, W), :]

        @block.sync
        def _(sp):
            def body(i):
                for h in range(2):
                    if not isinstance(i, int):
                        sp.wait_ge(ready, 2 * i + (h - 1))
                    sp.dma_start(xb[h][:, :, :], slots(T["x"], 2 * i + h)).then_inc(loaded[h], 16)
                    sp.dma_start(ab[h][:, :, :], slots(T["attr"], 2 * i + h)).then_inc(loaded[h], 16)
            turns(sp, body, TURN)

        @block.vector
        def _(dve):
            v = nc.vector
            st = Steps(dve, step)

            def body(i):
                st.begin(i)
                for h in range(2):
                    dve.wait_ge(loaded[h], 32 * i + 32)
                    if not isinstance(i, int):
                        dve.wait_ge(stored[h], 16 * i)
                    v.tensor_copy(row[h][:, :, D0:TW], ab[h][:, :, 0:2])
                    normalise(v, st, (var_ready, root_ready), xb[h][:, :, :], sums, centred[:, :, :],
                              square[:, :, :], row[h][:, :, 0:D0], D0, 2 * i + h + 1).then_inc(ready, 1)
            turns(dve, body, TURN)

        @block.scalar
        def _(act):
            def body(i):
                for h in range(2):
                    act.wait_ge(var_ready, 2 * i + h + 1)
                    nc.scalar.activation(sums[:, 3, :], sums[:, 2, :], ACT.Sqrt, bias=K["eps"][:, 0:1],
                                         scale=1.0 / D0).then_inc(root_ready, 1)
                    act.wait_ge(ready, 2 * i + h + 1)
                    act.dma_start(slots(T["rows"], 2 * i + h), row[h][:, :, :]).then_inc(stored[h], 16)
            turns(act, body, TURN)
            act.wait_ge(stored[0], 16 * TURN)
            act.wait_ge(stored[1], 16 * TURN)


def phase_reflect_edges(nc, K, z, T):
    B = ET * P
    with ExitStack() as ctx:
        sb = lambda n, s, d: ctx.enter_context(nc.sbuf_tensor(n, s, d))
        sem = lambda n: ctx.enter_context(nc.semaphore(n))
        ends = [sb(f"r_ends{h}", [P, ET, 2], I32) for h in range(2)]
        row = [sb(f"r_row{h}", [P, ET, 2, TW], F32) for h in range(2)]
        rowT = sb("r_rowT", [2 * TW, ET, P], F32)
        hid = sb("r_hid", [P, ET, P], F32)
        endf = sb("r_endf", [P, ET, 2], F32)
        same = sb("r_same", [P, 2, ET, P], F32)
        cross = sb("r_cross", [P, 2, ET // 2, P], F32)
        early = sb("r_early", [P, ET, P], F32)
        met = sb("r_met", [P, ET // 2], F32)
        first = sb("r_first", [P, 2, ET], F32)
        offset = sb("r_offset", [P, 2, ET], F32)
        target = [sb(f"r_target{h}", [P, 2, ET], I32) for h in range(2)]
        plan = [sb(f"r_plan{h}", [P, ET, 3], F32) for h in range(2)]
        vec = sb("r_vec", [P, ET, 2, D0], F32)
        prod = sb("r_prod", [P, ET, 2, D0], F32)
        swap = sb("r_swap", [P, ET, 2, D0], F32)
        msg = sb("r_msg", [P, ET, 2, D0], F32)
        inv = sb("r_inv", [P, ET, 2], F32)
        dot = sb("r_dot", [P, ET, 2], F32)
        coef = sb("r_coef", [P, ET], F32)
        total = [sb(f"r_total{h}", [P, 2, ET, D0], F32) for h in range(2)]
        psT = ctx.enter_context(nc.psum_tensor("r_psT", [2 * TW, ET, P], F32))
        psH = ctx.enter_context(nc.psum_tensor("r_psH", [P, ET, P], F32))
        psV = ctx.enter_context(nc.psum_tensor("r_psV", [P, ET, 2 * D0], F32))
        psR = ctx.enter_context(nc.psum_tensor("r_psR", [P, ET, P], F32))
        psS = ctx.enter_context(nc.psum_tensor("r_psS", [P, 2, ET, D0], F32))
        ends_ready = [sem(f"r_ends_ready{h}") for h in range(2)]
        rows_ready = [sem(f"r_rows_ready{h}") for h in range(2)]
        planned = [sem(f"r_planned{h}") for h in range(2)]
        added_to = [sem(f"r_added_to{a}") for a in range(2)]
        step = sem("r_step"); ends_used = sem("r_ends_used"); endf_ready = sem("r_endf_ready"); row_numbers = sem("r_row_numbers")
        numbers_used = sem("r_numbers_used"); rowT_ps = sem("r_rowT_ps"); rowT_ready = sem("r_rowT_ready")
        hid_ps = sem("r_hid_ps"); hid_ready = sem("r_hid_ready"); vec_ps = sem("r_vec_ps")
        msg_ready = sem("r_msg_ready"); sum_ps = sem("r_sum_ps"); totals_ready = sem("r_totals_ready")
        block = ctx.enter_context(nc.Block())
        rows_of = lambda t, k: t[bass.ds(k * B, B), :].rearrange("(p j) w -> p j w", j=ET)

        @block.sync
        def _(sp):
            def body(i):
                for h in range(2):
                    if not isinstance(i, int):
                        sp.wait_ge(ends_used, 2 * i + (h - 1))
                    sp.dma_start(ends[h][:, :, :], rows_of(T["edges"], 2 * i + h)).then_inc(ends_ready[h], 16)
            live_turns(sp, body, K["more"], z.PAIRS)

        @block.gpsimd
        def _(pool):
            def gather(h, j):
                for a in range(2):
                    pool.indirect_dma_start(row[h][:, j, a, :], None, T["rows"][:, :],
                                            bass.IndirectOffsetOnAxis(ap=ends[h][:, j, a:a + 1], axis=0)
                                            ).then_inc(rows_ready[h], 16)

            def scatter(h, j, a):
                pool.indirect_dma_start((T["acc_s"], T["acc_d"])[a][:, :],
                                        bass.IndirectOffsetOnAxis(ap=target[h][:, a, j:j + 1], axis=0),
                                        total[h][:, a, j, :], None, compute_op=ALU.add).then_inc(added_to[a], 16)

            def turn(i, h, ahead):
                k = 2 * i + h
                wait_apart(pool, totals_ready, k + 1, K["passed"])
                if ahead:
                    wait_apart(pool, ends_ready[h], 16 * i + 32, K["passed"])
                for u in range(ET // 2):
                    for a in range(2):
                        for j in (2 * u, 2 * u + 1):
                            scatter(h, j, a)
                    if ahead:
                        gather(h, 2 * u)
                        gather(h, 2 * u + 1)
                    for a in range(2):
                        wait_apart(pool, added_to[a], k * (16 * ET) + 32 * (u + 1), K["passed"])

            more = pool.value_load(K["more"][0:1, 0:1], min_val=0, max_val=z.PAIRS - 1)
            for h in range(2):
                pool.wait_ge(ends_ready[h], 16)
                for j in range(ET):
                    gather(h, j)
            with pool.Fori(0, z.PAIRS - 1) as i:
                with pool.If(i < more):
                    for h in range(2):
                        turn(i, h, True)
                pool.nop()
            for h in range(2):
                turn(more, h, False)

        @block.tensor
        def _(pe):
            t = nc.tensor

            def body(i):
                for h in range(2):
                    k = 2 * i + h
                    pe.wait_ge(endf_ready, k + 1)
                    for a in range(2):
                        if not (isinstance(i, int) and h == 0 and a == 0):
                            pe.wait_ge(numbers_used, 2 * k + a)
                        for j in range(ET):
                            last = t.matmul(psR[:, j, :], endf[:, j, a:a + 1].to_broadcast([P, P]), K["ident"][:, :], start=True, stop=True)
                        last.then_inc(row_numbers, 1)
                    wait_apart(pe, rows_ready[h], (i + 1) * (32 * ET), K["passed"])
                    for j in range(ET):
                        last = t.transpose(psT[:, j, :], row[h][:, j, :, :].rearrange("p a f -> p (a f)"), K["ident"][:, :])
                    last.then_inc(rowT_ps, 1)
                    pe.wait_ge(rowT_ready, k + 1)
                    for q in range(ET // 4):
                        last = t.matmul(psH[:, 4 * q:4 * q + 4, :].rearrange("p j n -> p (j n)"), K["w_ref"][0:2 * TW, :],
                                        rowT[:, 4 * q:4 * q + 4, :].rearrange("p j n -> p (j n)"), start=True, stop=True)
                    last.then_inc(hid_ps, 1)
                    pe.wait_ge(hid_ready, k + 1)
                    for j in range(ET):
                        last = t.matmul(psV[:, j, :], hid[:, j, :], K["w_ref_out"][:, :], start=True, stop=True)
                    last.then_inc(vec_ps, 1)
                    pe.wait_ge(msg_ready, k + 1)
                    for a in range(2):
                        for j in range(ET):
                            last = t.matmul(psS[:, a, j, :], same[:, a, j, :], msg[:, j, a, :], start=True, stop=j % 2 == 1)
                            if j % 2 == 0:
                                last = t.matmul(psS[:, a, j, :], cross[:, a, j // 2, :], msg[:, j + 1, a, :], start=False, stop=True)
                    last.then_inc(sum_ps, 1)
            live_turns(pe, body, K["more"], z.PAIRS)

        @block.scalar
        def _(act):
            def body(i):
                for h in range(2):
                    k = 2 * i + h
                    act.wait_ge(rowT_ps, k + 1)
                    nc.scalar.activation(rowT[:, :, :], psT[:, :, :], ACT.Copy).then_inc(rowT_ready, 1)
                    act.wait_ge(hid_ps, k + 1)
                    nc.scalar.activation(hid[:, :, :], psH[:, :, :], ACT.Relu, bias=K["b_ref"][:, 0:1]).then_inc(hid_ready, 1)
                    act.wait_ge(totals_ready, k + 1)
                    act.dma_start(rows_of(T["plan"], k), plan[h][:, :, :]).then_inc(planned[h], 16)
            more = live_turns(act, body, K["more"], z.PAIRS)
            for h in range(2):
                wait_apart(act, planned[h], more * 16 + 16, K["passed"])

        @block.vector
        def _(dve):
            v = nc.vector
            st = Steps(dve, step)

            def body(i):
                st.begin(i)
                for h in range(2):
                    k = 2 * i + h
                    dve.wait_ge(ends_ready[h], 16 * (i + 1))
                    if not isinstance(i, int):
                        dve.wait_ge(planned[h], 16 * i)
                        dve.wait_ge(added_to[0], i * (32 * ET) + (h - 1) * (16 * ET))
                        dve.wait_ge(added_to[1], i * (32 * ET) + (h - 1) * (16 * ET))
                    v.tensor_copy(endf[:, :, :], ends[h][:, :, :]).then_inc(endf_ready, 1)
                    dve.wait_ge(endf_ready, k + 1)
                    for a in range(2):
                        dve.wait_ge(row_numbers, 2 * k + a + 1)
                        v.tensor_tensor(same[:, a, :, :], psR[:, :, :], spread(endf[:, :, a], P), ALU.is_equal)
                        even = psR[:, :, :].rearrange("p (u q) n -> p u q n", q=2)[:, :, 0, :]
                        odd = endf[:, :, :].rearrange("p (u q) a -> p u q a", q=2)[:, :, 1, a]
                        v.tensor_tensor(cross[:, a, :, :], even, spread(odd, P), ALU.is_equal).then_inc(numbers_used, 1)
                        dve.wait_ge(numbers_used, 2 * k + a + 1)
                        st.link(v.tensor_tensor(early[:, :, :], same[:, a, :, :], along(K["earlier"][:, :], ET), ALU.mult))
                        v.tensor_reduce(met[:, :], cross[:, a, :, :], AX, ALU.max)
                        st.link(v.tensor_reduce(first[:, a, :], early[:, :, :], AX, ALU.max))
                        late = first[:, a, :].rearrange("p (u q) -> p u q", q=2)[:, :, 1]
                        st.link(v.tensor_tensor(late, late, met[:, :], ALU.max))
                    st.link(v.tensor_scalar(first[:, :, :], first[:, :, :], -1.0, 1.0, ALU.mult, ALU.add))
                    endt = endf[:, :, :].rearrange("p j a -> p a j")
                    trash = along(K["trash"][:, :], 2)
                    st.link(v.tensor_tensor(offset[:, :, :], endt, trash, ALU.subtract))
                    st.link(v.tensor_tensor(offset[:, :, :], offset[:, :, :], first[:, :, :], ALU.mult))
                    st.link(v.tensor_tensor(offset[:, :, :], offset[:, :, :], trash, ALU.add))
                    v.tensor_copy(target[h][:, :, :], offset[:, :, :])
                    v.tensor_copy(plan[h][:, :, 0].bitcast(I32), offset[:, 1, :])
                    v.tensor_copy(plan[h][:, :, 1], endf[:, :, 1])
                    dve.wait_ge(rows_ready[h], (i + 1) * (32 * ET))
                    x = row[h][:, :, :, 0:D0]
                    v.tensor_tensor(plan[h][:, :, 2], row[h][:, :, 0, D0 + 1], row[h][:, :, 1, D0 + 1], ALU.mult)
                    v.tensor_tensor(coef[:, :], row[h][:, :, 0, D0], row[h][:, :, 1, D0], ALU.mult).then_inc(ends_used, 1)
                    dve.wait_ge(vec_ps, k + 1)
                    bias = along(K["b_ref_out"][:, :], ET).rearrange("p j (a f) -> p j a f", a=2)
                    st.link(v.tensor_tensor(vec[:, :, :, :], psV[:, :, :].rearrange("p j (a f) -> p j a f", a=2), bias, ALU.add))
                    st.link(v.tensor_tensor(prod[:, :, :, :], vec[:, :, :, :], vec[:, :, :, :], ALU.mult))
                    st.link(v.tensor_reduce(inv[:, :, :], prod[:, :, :, :], AX, ALU.add))
                    st.link(v.tensor_scalar(inv[:, :, :], inv[:, :, :], 1e-24, None, ALU.max))
                    st.link(v.reciprocal(inv[:, :, :], inv[:, :, :]))
                    st.link(v.tensor_tensor(prod[:, :, :, :], vec[:, :, :, :], x, ALU.mult))
                    st.link(v.tensor_reduce(dot[:, :, :], prod[:, :, :, :], AX, ALU.add))
                    st.link(v.scalar_tensor_tensor(dot[:, :, :], dot[:, :, :], 2.0, inv[:, :, :], ALU.mult, ALU.mult))
                    st.link(v.tensor_tensor(prod[:, :, :, :], vec[:, :, :, :], spread(dot[:, :, :], D0), ALU.mult))
                    for a in range(2):
                        last = v.tensor_tensor(swap[:, :, 1 - a, :], x[:, :, a, :], prod[:, :, a, :], ALU.subtract)
                    st.link(last)
                    st.link(v.tensor_tensor(prod[:, :, :, :], vec[:, :, :, :], swap[:, :, :, :], ALU.mult))
                    st.link(v.tensor_reduce(dot[:, :, :], prod[:, :, :, :], AX, ALU.add))
                    st.link(v.scalar_tensor_tensor(dot[:, :, :], dot[:, :, :], 2.0, inv[:, :, :], ALU.mult, ALU.mult))
                    st.link(v.tensor_tensor(prod[:, :, :, :], vec[:, :, :, :], spread(dot[:, :, :], D0), ALU.mult))
                    st.link(v.tensor_tensor(swap[:, :, :, :], swap[:, :, :, :], prod[:, :, :, :], ALU.subtract))
                    both = spread(coef[:, :], 2 * D0).rearrange("p j (a f) -> p j a f", a=2)
                    v.tensor_tensor(msg[:, :, :, :], swap[:, :, :, :], both, ALU.mult).then_inc(msg_ready, 1)
                    dve.wait_ge(sum_ps, k + 1)
                    v.tensor_copy(total[h][:, :, :, :], psS[:, :, :, :]).then_inc(totals_ready, 1)
            live_turns(dve, body, K["more"], z.PAIRS)


def phase_reflect_nodes(nc, K, z, T):
    S, W, G = z.S, WIDE, WIDE // SLOTS
    with ExitStack() as ctx:
        sb = lambda n, s, d: ctx.enter_context(nc.sbuf_tensor(n, s, d))
        sem = cleared_after(nc, ctx)
        xb = [sb(f"n_x{h}", [P, W, D0], F32) for h in range(2)]
        ab = [sb(f"n_attr{h}", [P, W, 4], F32) for h in range(2)]
        row = [sb(f"n_row{h}", [P, W, TW], F32) for h in range(2)]
        acc = [sb(f"n_acc{h}", [P, 2, W, D0], F32) for h in range(2)]
        feat = [sb(f"n_feat{h}", [P, W, D0], F32) for h in range(2)]
        hb = [sb(f"n_h{h}", [P, W, D0], F32) for h in range(2)]
        hT = sb("n_hT", [P, G, P], F32)
        hid = [sb(f"n_hid{q}", [P, SLOTS // 2, P], F32) for q in range(2)]
        vec = sb("n_vec", [P, W, D0], F32)
        prod = sb("n_prod", [P, W, D0], F32)
        y = sb("n_y", [P, W, D0], F32)
        centred = [sb(f"n_centred{h}", [P, W, D0], F32) for h in range(2)]
        inv = sb("n_inv", [P, W], F32)
        dot = sb("n_dot", [P, W], F32)
        sums = [sb(f"n_sums{h}", [P, 4, W], F32) for h in range(2)]
        psT = ctx.enter_context(nc.psum_tensor("n_psT", [P, 8, P], F32))
        psH = [ctx.enter_context(nc.psum_tensor(f"n_psH{q}", [P, SLOTS // 2, P], F32)) for q in range(2)]
        psV = [ctx.enter_context(nc.psum_tensor(f"n_psV{h}", [P, 64, D0], F32)) for h in range(2)]
        loaded = [sem(f"n_loaded{h}") for h in range(2)]
        stored = [sem(f"n_stored{h}") for h in range(2)]
        packed = sem("n_packed")
        step = sem("n_step"); step2 = sem("n_step2"); ready = sem("n_ready"); var_ready = sem("n_var"); root_ready = sem("n_root")
        hT_ps = sem("n_hT_ps"); hT_ready = sem("n_hT_ready"); hid_ps = sem("n_hid_ps"); hid_ready = sem("n_hid_ready")
        vec_ps = sem("n_vec_ps"); vec_used = sem("n_vec_used")
        block = ctx.enter_context(nc.Block())
        TURN = S // (2 * W)
        slots = lambda t, k: t[0:z.NP, :].rearrange("(p s) f -> p s f", s=S)[:, bass.ds(k * W, W), :]

        @block.sync
        def _(sp):
            def store(b):
                wait_apart(sp, ready, b.k + 1, K["passed"])
                sp.dma_start(slots(T["x"], b.k), xb[b.h][:, :, :]).then_inc(stored[b.h], 16)
                sp.dma_start(slots(T["h"], b.k), hb[b.h][:, :, :]).then_inc(stored[b.h], 16)

            def load(b):
                if b.after(2):
                    wait_apart(sp, stored[b.h], 32 * b.turn, K["passed"])
                for to, name in ((row[b.h][:, :, :], "rows"), (xb[b.h][:, :, :], "x"), (ab[b.h][:, :, :], "attr"),
                                 (acc[b.h][:, 0, :, :], "acc_s"), (acc[b.h][:, 1, :, :], "acc_d")):
                    sp.dma_start(to, slots(T[name], b.k)).then_inc(loaded[b.h], 16)

            staged(sp, [(2, store), (0, load)], TURN)
            sp.wait_ge(stored[0], 32 * TURN)
            sp.wait_ge(stored[1], 32 * TURN)

        @block.gpsimd
        def _(pool):
            def pack(b):
                if b.after(2):
                    wait_apart(pool, hT_ps, b.k + (-1), K["passed"])
                wait_apart(pool, loaded[b.h], 80 * b.turn + 80, K["passed"])
                pool.tensor_copy(feat[b.h][:, :, :], row[b.h][:, :, 0:D0]).then_inc(packed, 1)
            staged(pool, [(0, pack)], TURN)

        @block.tensor
        def _(pe):
            t = nc.tensor

            def network(b):
                pe.wait_ge(packed, b.k + 1)
                for g in range(G):
                    last = t.transpose(psT[:, g, :], feat[b.h][:, SLOTS * g:SLOTS * (g + 1), :].rearrange("p s f -> p (s f)"), K["ident"][:, :])
                last.then_inc(hT_ps, 1)
                pe.wait_ge(hT_ready, b.k + 1)
                if b.after(2):
                    pe.wait_ge(vec_used, b.k + (-1))
                for g in range(G + 1):
                    q = (b.h * G + g) % 2
                    if g < G:
                        if b.after(1) or g >= 2:
                            pe.wait_ge(hid_ready, b.k * G + (g - 1))
                        for u in range(SLOTS // 2):
                            t.matmul(psH[q][:, u, :], K["w_self_a"][:, u, :], hT[:, g, :], start=True, stop=False)
                            last = t.matmul(psH[q][:, u, :], K["w_self_b"][:, u, :], hT[:, g, :], start=False, stop=True)
                        last.then_inc(hid_ps, 1)
                    if g > 0:
                        pe.wait_ge(hid_ready, b.k * G + g)
                        for u in range(SLOTS // 2):
                            s0 = SLOTS * (g - 1) + 2 * u
                            last = t.matmul(psV[b.h][:, s0:s0 + 2, :].rearrange("p s f -> p (s f)"), hid[1 - q][:, u, :], K["w_ref_out"][:, :], start=True, stop=True)
                        last.then_inc(vec_ps, 1)
            staged(pe, [(0, network)], TURN)

        @block.scalar
        def _(act):
            def serve(b):
                act.wait_ge(hT_ps, b.k + 1)
                nc.scalar.activation(hT[:, :, :], psT[:, 0:G, :], ACT.Copy).then_inc(hT_ready, 1)
                for g in range(G):
                    q = (b.h * G + g) % 2
                    act.wait_ge(hid_ps, b.k * G + (g + 1))
                    if b.after(1) or g >= 2:
                        act.wait_ge(vec_ps, b.k * G + (g - 1))
                    nc.scalar.activation(hid[q][:, :, :], psH[q][:, :, :], ACT.Relu, bias=K["b_ref"][:, 0:1]).then_inc(hid_ready, 1)

            def root(b):
                act.wait_ge(var_ready, b.k + 1)
                nc.scalar.activation(sums[b.h][:, 3, :], sums[b.h][:, 2, :], ACT.Sqrt, bias=K["eps"][:, 0:1], scale=1.0 / D0).then_inc(root_ready, 1)
            staged(act, [(0, serve), (1, root)], TURN)

        @block.vector
        def _(dve):
            v = nc.vector
            st = Steps(dve, step)
            st2 = Steps(dve, step2)
            bias = K["b_ref_out"][:, 0:D0]

            def reflect(b):
                h, sm = b.h, sums[b.h]
                st.begin(b.k)
                x = row[h][:, :, 0:D0]
                dve.wait_ge(loaded[h], 80 * b.turn + 80)
                dve.wait_ge(vec_ps, b.k * G + G)
                v.tensor_tensor(vec[:, :, :], psV[h][:, 0:W, :], along(bias, W), ALU.add).then_inc(vec_used, 1)
                dve.wait_ge(vec_used, b.k + 1)
                st.link(v.tensor_tensor(prod[:, :, :], vec[:, :, :], vec[:, :, :], ALU.mult))
                st.link(v.tensor_reduce(inv[:, :], prod[:, :, :], AX, ALU.add))
                st.link(v.tensor_scalar(inv[:, :], inv[:, :], 1e-24, None, ALU.max))
                st.link(v.reciprocal(inv[:, :], inv[:, :]))
                for n in range(2):
                    st.link(v.tensor_tensor(prod[:, :, :], vec[:, :, :], x, ALU.mult))
                    st.link(v.tensor_reduce(dot[:, :], prod[:, :, :], AX, ALU.add))
                    st.link(v.scalar_tensor_tensor(dot[:, :], dot[:, :], 2.0, inv[:, :], ALU.mult, ALU.mult))
                    st.link(v.tensor_tensor(prod[:, :, :], vec[:, :, :], spread(dot[:, :], D0), ALU.mult))
                    st.link(v.tensor_tensor(y[:, :, :], x, prod[:, :, :], ALU.subtract))
                    x = y[:, :, :]
                st.link(v.tensor_tensor(y[:, :, :], y[:, :, :], spread(ab[h][:, :, 2], D0), ALU.mult))
                st.link(v.tensor_tensor(y[:, :, :], y[:, :, :], row[h][:, :, 0:D0], ALU.add))
                for a in range(2):
                    st.link(v.tensor_tensor(y[:, :, :], y[:, :, :], acc[h][:, a, :, :], ALU.add))
                st.link(v.scalar_tensor_tensor(xb[h][:, :, :], y[:, :, :], 0.0, xb[h][:, :, :], ALU.max, ALU.add))
                st.link(v.tensor_reduce(sm[:, 0, :], xb[h][:, :, :], AX, ALU.add))
                st.link(v.tensor_scalar(sm[:, 1, :], sm[:, 0, :], 1.0 / D0, None, ALU.mult))
                st.link(v.tensor_tensor(centred[h][:, :, :], xb[h][:, :, :], spread(sm[:, 1, :], D0), ALU.subtract))
                st.link(v.tensor_tensor(y[:, :, :], centred[h][:, :, :], centred[h][:, :, :], ALU.mult))
                v.tensor_reduce(sm[:, 2, :], y[:, :, :], AX, ALU.add).then_inc(var_ready, 1)

            def finish(b):
                h, sm = b.h, sums[b.h]
                st2.begin(b.k)
                dve.wait_ge(root_ready, b.k + 1)
                st2.link(v.reciprocal(sm[:, 3, :], sm[:, 3, :]))
                st2.link(v.tensor_tensor(centred[h][:, :, :], centred[h][:, :, :], spread(sm[:, 3, :], D0), ALU.mult))
                if b.after(2):
                    dve.wait_ge(stored[h], 32 * b.turn)
                v.tensor_scalar(hb[h][:, :, :], centred[h][:, :, :], 0.0, None, ALU.max).then_inc(ready, 1)
            staged(dve, [(0, reflect), (1, finish)], TURN)


def phase_encode(nc, K, z, T):
    S, W = z.S, SLOTS
    with ExitStack() as ctx:
        sb = lambda n, s, d: ctx.enter_context(nc.sbuf_tensor(n, s, d))
        sem = cleared_after(nc, ctx)
        hb = [sb(f"e_h{h}", [P, W, D0], F32) for h in range(2)]
        ab = [sb(f"e_attr{h}", [P, W, 4], F32) for h in range(2)]
        hT = [sb(f"e_hT{h}", [P, P], F32) for h in range(2)]
        hid = [sb(f"e_hid{h}", [P, W, P], F32) for h in range(2)]
        feat = [sb(f"e_feat{h}", [P, W, D], F32) for h in range(2)]
        acc = [sb(f"e_acc{h}", [P, W, D], F32) for h in range(2)]
        psT = ctx.enter_context(nc.psum_tensor("e_psT", [P, P], F32))
        psH = ctx.enter_context(nc.psum_tensor("e_psH", [P, W, P], F32))
        psX = [ctx.enter_context(nc.psum_tensor(f"e_psX{h}", [P, W, D], F32)) for h in range(2)]
        loaded = [sem(f"e_loaded{h}") for h in range(2)]
        attr_loaded = [sem(f"e_attr_loaded{h}") for h in range(2)]
        stored = [sem(f"e_stored{h}") for h in range(2)]
        hT_ps = sem("e_hT_ps"); hT_ready = sem("e_hT_ready"); hid_ps = sem("e_hid_ps"); hid_ready = sem("e_hid_ready")
        feat_ps = sem("e_feat_ps"); feat_ready = sem("e_feat_ready"); acc_ready = sem("e_acc_ready")
        block = ctx.enter_context(nc.Block())
        TURN = S // (2 * W)
        slots = lambda t, k: t[0:z.NP, :].rearrange("(p s) f -> p s f", s=S)[:, bass.ds(k * W, W), :]

        @block.sync
        def _(sp):
            def store(b):
                wait_apart(sp, acc_ready, b.k + 1, K["passed"])
                sp.dma_start(slots(T["feat"], b.k), feat[b.h][:, :, :]).then_inc(stored[b.h], 16)
                sp.dma_start(slots(T["acc"], b.k), acc[b.h][:, :, :]).then_inc(stored[b.h], 16)

            def load_h(b):
                if b.after(2):
                    wait_apart(sp, hT_ps, b.k + (-1), K["passed"])
                sp.dma_start(hb[b.h][:, :, :], slots(T["h"], b.k)).then_inc(loaded[b.h], 16)

            def load_attr(b):
                sp.dma_start(ab[b.h][:, :, :], slots(T["attr"], b.k)).then_inc(attr_loaded[b.h], 16)
            staged(sp, [(0, load_h), (2, store), (0, load_attr)], TURN)
            sp.wait_ge(stored[0], 32 * TURN)
            sp.wait_ge(stored[1], 32 * TURN)

        @block.tensor
        def _(pe):
            t = nc.tensor

            def turn_over(b):
                pe.wait_ge(loaded[b.h], 16 * b.turn + 16)
                if b.after(1):
                    pe.wait_ge(hT_ready, b.k)
                t.transpose(psT[:, :], hb[b.h][:, :, :].rearrange("p s f -> p (s f)"), K["ident"][:, :]).then_inc(hT_ps, 1)

            def hidden(b):
                pe.wait_ge(hT_ready, b.k + 1)
                for q in range(2):
                    if b.after(1):
                        pe.wait_ge(hid_ready, b.k * 2 + (q - 1))
                    for j in range(q * W // 2, (q + 1) * W // 2):
                        last = t.matmul(psH[:, j, :], K["w_enc0"][:, j, :], hT[b.h][:, :], start=True, stop=True)
                    last.then_inc(hid_ps, 1)

            def features(b):
                if b.after(2):
                    pe.wait_ge(feat_ready, b.k + (-1))
                for j in range(W):
                    if j % (W // 2) == 0:
                        pe.wait_ge(hid_ready, b.k * 2 + (1 + j // (W // 2)))
                    last = t.matmul(psX[b.h][:, j, :], hid[b.h][:, j, :], K["w_enc1"][:, :], start=True, stop=True)
                last.then_inc(feat_ps, 1)
            staged(pe, [(0, turn_over), (1, features), (0, hidden)], TURN)

        @block.scalar
        def _(act):
            def copy(b):
                act.wait_ge(hT_ps, b.k + 1)
                if b.after(2):
                    act.wait_ge(hid_ps, b.k * 2 + (-2))
                nc.scalar.activation(hT[b.h][:, :], psT[:, :], ACT.Copy).then_inc(hT_ready, 1)

            def relu(b):
                if b.after(2):
                    act.wait_ge(feat_ps, b.k + (-1))
                for q in range(2):
                    act.wait_ge(hid_ps, b.k * 2 + (q + 1))
                    part = slice(q * W // 2, (q + 1) * W // 2)
                    nc.scalar.activation(hid[b.h][:, part, :], psH[:, part, :], ACT.Relu, bias=K["b_enc0"][:, 0:1]).then_inc(hid_ready, 1)
            staged(act, [(0, copy), (0, relu)], TURN)

        @block.vector
        def _(dve):
            v = nc.vector

            def finish(b):
                h = b.h
                dve.wait_ge(feat_ps, b.k + 1)
                if b.after(2):
                    dve.wait_ge(stored[h], 32 * b.turn)
                v.tensor_tensor(feat[h][:, :, :], psX[h][:, :, :], along(K["b_enc1"][:, :], W), ALU.add).then_inc(feat_ready, 1)
                dve.wait_ge(feat_ready, b.k + 1)
                dve.wait_ge(attr_loaded[h], 16 * b.turn + 16)
                v.tensor_tensor(acc[h][:, :, :], feat[h][:, :, :], spread(ab[h][:, :, 3], D), ALU.mult).then_inc(acc_ready, 1)
            staged(dve, [(0, finish)], TURN)


def phase_spread(nc, K, z, T, layer):
    B = ET * P
    c = f"s{layer}_"
    with ExitStack() as ctx:
        sb = lambda n, s, d: ctx.enter_context(nc.sbuf_tensor(c + n, s, d))
        sem = lambda n: ctx.enter_context(nc.semaphore(c + n))
        ends = [sb(f"ends{h}", [P, ET, 2], I32) for h in range(2)]
        plan = [sb(f"plan{h}", [P, ET, 3], F32) for h in range(2)]
        row = [sb(f"row{h}", [P, ET, D], F32) for h in range(2)]
        same = sb("same", [P, ET, P], F32)
        cross = sb("cross", [P, ET // 2, P], F32)
        total = [sb(f"total{h}", [P, ET, D], F32) for h in range(2)]
        psR = ctx.enter_context(nc.psum_tensor(c + "psR", [P, ET, P], F32))
        psS = ctx.enter_context(nc.psum_tensor(c + "psS", [P, ET, D], F32))
        ends_ready = [sem(f"ends_ready{h}") for h in range(2)]
        plan_ready = [sem(f"plan_ready{h}") for h in range(2)]
        rows_ready = [sem(f"rows_ready{h}") for h in range(2)]
        numbers = sem("numbers"); same_ready = sem("same_ready"); sum_ps = sem("sum_ps")
        totals_ready = sem("totals_ready"); added = sem("added"); step = sem("step")
        block = ctx.enter_context(nc.Block())
        rows_of = lambda t, k: t[bass.ds(k * B, B), :].rearrange("(p j) w -> p j w", j=ET)

        @block.sync
        def _(sp):
            def load_ends(i, h):
                sp.dma_start(ends[h][:, :, :], rows_of(T["edges"], 2 * i + h)).then_inc(ends_ready[h], 16)

            def body(i):
                if isinstance(i, int):
                    load_ends(0, 0)
                    load_ends(0, 1)
                for h in range(2):
                    if not isinstance(i, int):
                        wait_apart(sp, added, i * (32 * ET) + (h - 1) * (16 * ET), K["passed"])
                    sp.dma_start(plan[h][:, :, :], rows_of(T["plan"], 2 * i + h)).then_inc(plan_ready[h], 16)
                    wait_apart(sp, rows_ready[h], i * (16 * ET) + 16 * ET, K["passed"])
                    load_ends(i + 1, h)
            more = live_turns(sp, body, K["more"], z.PAIRS)
            for h in range(2):
                wait_apart(sp, ends_ready[h], more * 16 + 32, K["passed"])

        @block.gpsimd
        def _(pool):
            def gather(h, j):
                pool.indirect_dma_start(row[h][:, j, :], None, T["feat"][:, :],
                                        bass.IndirectOffsetOnAxis(ap=ends[h][:, j, 0:1], axis=0)
                                        ).then_inc(rows_ready[h], 16)

            def scatter(h, j):
                pool.indirect_dma_start(T["acc"][:, :], bass.IndirectOffsetOnAxis(ap=plan[h][:, j, 0:1].bitcast(I32), axis=0),
                                        total[h][:, j, :], None, compute_op=ALU.add).then_inc(added, 16)

            def turn(i, h, ahead):
                k = 2 * i + h
                wait_apart(pool, totals_ready, k + 1, K["passed"])
                if ahead:
                    wait_apart(pool, ends_ready[h], 16 * i + 32, K["passed"])
                for u in range(ET // 2):
                    scatter(h, 2 * u)
                    scatter(h, 2 * u + 1)
                    if ahead:
                        gather(h, 2 * u)
                        gather(h, 2 * u + 1)
                    wait_apart(pool, added, k * (16 * ET) + 32 * (u + 1), K["passed"])

            more = pool.value_load(K["more"][0:1, 0:1], min_val=0, max_val=z.PAIRS - 1)
            for h in range(2):
                pool.wait_ge(ends_ready[h], 16)
                for j in range(ET):
                    gather(h, j)
            with pool.Fori(0, z.PAIRS - 1) as i:
                with pool.If(i < more):
                    for h in range(2):
                        turn(i, h, True)
                pool.nop()
            for h in range(2):
                turn(more, h, False)

        @block.tensor
        def _(pe):
            t = nc.tensor

            def body(i):
                for h in range(2):
                    k = 2 * i + h
                    pe.wait_ge(plan_ready[h], 16 * (i + 1))
                    if not (isinstance(i, int) and h == 0):
                        pe.wait_ge(same_ready, k)
                    for j in range(ET):
                        last = t.matmul(psR[:, j, :], plan[h][:, j, 1:2].to_broadcast([P, P]), K["ident"][:, :], start=True, stop=True)
                    last.then_inc(numbers, 1)
                    pe.wait_ge(same_ready, k + 1)
                    pe.wait_ge(rows_ready[h], (i + 1) * (16 * ET))
                    if not (isinstance(i, int) and h == 0):
                        pe.wait_ge(totals_ready, k)
                    for j in range(ET):
                        last = t.matmul(psS[:, j, :], same[:, j, :], row[h][:, j, :], start=True, stop=j % 2 == 1)
                        if j % 2 == 0:
                            last = t.matmul(psS[:, j, :], cross[:, j // 2, :], row[h][:, j + 1, :], start=False, stop=True)
                    last.then_inc(sum_ps, 1)
            live_turns(pe, body, K["more"], z.PAIRS)

        @block.vector
        def _(dve):
            v = nc.vector

            def body(i):
                for h in range(2):
                    k = 2 * i + h
                    dve.wait_ge(numbers, k + 1)
                    if not (isinstance(i, int) and h == 0):
                        dve.wait_ge(sum_ps, k)
                    for j in range(ET):
                        last = v.tensor_scalar(same[:, j, :], psR[:, j, :], plan[h][:, j, 1:2], plan[h][:, j, 2:3], ALU.is_equal, ALU.mult)
                        if j % 2:
                            last = v.tensor_scalar(cross[:, j // 2, :], psR[:, j - 1, :], plan[h][:, j, 1:2], plan[h][:, j, 2:3], ALU.is_equal, ALU.mult)
                    last.then_inc(same_ready, 1)
            live_turns(dve, body, K["more"], z.PAIRS)

        @block.scalar
        def _(act):
            def body(i):
                for h in range(2):
                    k = 2 * i + h
                    if not isinstance(i, int):
                        act.wait_ge(added, i * (32 * ET) + (h - 1) * (16 * ET))
                    act.wait_ge(sum_ps, k + 1)
                    nc.scalar.activation(total[h][:, :, :], psS[:, :, :], ACT.Copy).then_inc(totals_ready, 1)
            live_turns(act, body, K["more"], z.PAIRS)


def phase_convolve(nc, K, z, T, layer, decode):
    S, W = z.S, SLOTS
    c = f"v{layer}_"
    with ExitStack() as ctx:
        sb = lambda n, s, d: ctx.enter_context(nc.sbuf_tensor(c + n, s, d))
        sem = cleared_after(nc, ctx, c)
        ps = lambda n, s: ctx.enter_context(nc.psum_tensor(c + n, s, F32))
        feat = [sb(f"feat{h}", [P, W, D], F32) for h in range(2)]
        acc = [sb(f"acc{h}", [P, W, D], F32) for h in range(2)]
        ab = [sb(f"attr{h}", [P, W, 4], F32) for h in range(2)]
        new = [sb(f"new{h}", [P, W, D], F32) for h in range(2)]
        nacc = [sb(f"nacc{h}", [P, W, D], F32) for h in range(2)]
        biased = [sb(f"biased{h}", [P, W, D], F32) for h in range(2)]
        accT = [sb(f"accT{h}", [P, W, P], F32) for h in range(2)]
        summed = [sb(f"summed{h}", [P, W, D], F32) for h in range(2)]
        norm = sb("norm", [P, W, D], F32)
        stats = sb("stats", [P, W, 6], F32)
        mean = [sb(f"mean{h}", [P, 6, W], F32) for h in range(2)]
        psT = ps("psT", [P, W, P]); psY = ps("psY", [P, W, D])
        loaded = [sem(f"loaded{h}") for h in range(2)]
        last_loaded = [sem(f"last_loaded{h}") for h in range(2)]
        stored = [sem(f"stored{h}") for h in range(2)]
        step = sem("step"); step2 = sem("step2"); step3 = sem("step3"); biased_ready = sem("biased"); accT_ps = sem("accT_ps"); accT_ready = sem("accT_ready"); prod_ps = sem("prod_ps")
        prod_used = sem("prod_used"); var_ready = sem("var"); root_ready = sem("root"); ready = sem("ready"); new_ready = sem("new_ready")
        if decode:
            xb = [sb(f"x{h}", [P, W, D0], F32) for h in range(2)]
            ob = [sb(f"o{h}", [P, W, D0], F32) for h in range(2)]
            newT = sb("newT", [P, W, P], F32)
            hid = sb("hid", [P, W, P], F32)
            psN = ps("psN", [P, W, P]); psD = ps("psD", [P, W, P])
            psO = psD[:, 0, :].rearrange("p (s f) -> p s f", f=D0)
            newT_ps = sem("newT_ps"); newT_ready = sem("newT_ready"); hid_ps = sem("hid_ps"); hid_ready = sem("hid_ready")
            out_ps = sem("out_ps")
        block = ctx.enter_context(nc.Block())
        TURN = S // (2 * W)
        LOADS = 32
        STORES = 16 * (1 if decode else 2)
        slots = lambda t, k: t[0:z.NP, :].rearrange("(p s) f -> p s f", s=S)[:, bass.ds(k * W, W), :]

        @block.sync
        def _(sp):
            def store(b):
                wait_apart(sp, ready, b.k + 1, K["passed"])
                if decode:
                    sp.dma_start(slots(T["out"], b.k), ob[b.h][:, :, :]).then_inc(stored[b.h], 16)
                else:
                    sp.dma_start(slots(T["feat"], b.k), new[b.h][:, :, :]).then_inc(stored[b.h], 16)
                    sp.dma_start(slots(T["acc"], b.k), nacc[b.h][:, :, :]).then_inc(stored[b.h], 16)

            def load_rows(b):
                if b.after(2):
                    wait_apart(sp, accT_ps, b.k + (-1), K["passed"])
                    wait_apart(sp, biased_ready, b.k + (-1), K["passed"])
                sp.dma_start(acc[b.h][:, :, :], slots(T["acc"], b.k)).then_inc(loaded[b.h], 16)
                sp.dma_start(feat[b.h][:, :, :], slots(T["feat"], b.k)).then_inc(loaded[b.h], 16)

            def load_attr(b):
                sp.dma_start(ab[b.h][:, :, :], slots(T["attr"], b.k)).then_inc(last_loaded[b.h], 16)

            def load_x(b):
                sp.dma_start(xb[b.h][:, :, :], slots(T["x"], b.k)).then_inc(last_loaded[b.h], 16)

            if decode:
                staged(sp, [(0, load_rows), (3, store), (1, load_x)], TURN)
            else:
                staged(sp, [(0, load_rows), (2, store), (0, load_attr)], TURN)
            sp.wait_ge(stored[0], STORES * TURN)
            sp.wait_ge(stored[1], STORES * TURN)

        @block.gpsimd
        def _(pool):
            def add_bias(b):
                if b.after(2):
                    wait_apart(pool, prod_used, b.k + (-1), K["passed"])
                pool.wait_ge(loaded[b.h], LOADS * b.turn + LOADS)
                nc.gpsimd.tensor_tensor(biased[b.h][:, :, :], feat[b.h][:, :, :], along(K["b_conv"][:, :], W), ALU.add).then_inc(biased_ready, 1)

            def next_acc(b):
                if b.after(2):
                    wait_apart(pool, stored[b.h], STORES * b.turn, K["passed"])
                wait_apart(pool, last_loaded[b.h], 16 * b.turn + 16, K["passed"])
                pool.wait_ge(new_ready, b.k + 1)
                nc.gpsimd.tensor_tensor(nacc[b.h][:, :, :], new[b.h][:, :, :], spread(ab[b.h][:, :, 3], D), ALU.mult).then_inc(ready, 1)
            staged(pool, [(0, add_bias)] + ([] if decode else [(2, next_acc)]), TURN)

        @block.tensor
        def _(pe):
            t = nc.tensor

            def turn_over(b):
                pe.wait_ge(loaded[b.h], LOADS * b.turn + LOADS)
                if b.after(1):
                    pe.wait_ge(accT_ready, b.k)
                for j in range(W):
                    last = t.transpose(psT[:, j, :], acc[b.h][:, j, :], K["ident"][:, :])
                last.then_inc(accT_ps, 1)

            def product(b):
                pe.wait_ge(accT_ready, b.k + 1)
                if b.after(1):
                    pe.wait_ge(prod_used, b.k)
                for j in range(W):
                    last = t.matmul(psY[:, j, :], accT[b.h][:, j, :], K["w_conv"][:, :], start=True, stop=True)
                last.then_inc(prod_ps, 1)

            def turn_new(b):
                pe.wait_ge(new_ready, b.k + 1)
                if b.after(1):
                    pe.wait_ge(newT_ready, b.k)
                for j in range(W):
                    last = t.transpose(psN[:, j, :], new[b.h][:, j, :], K["ident"][:, :])
                last.then_inc(newT_ps, 1)

            def hidden(b):
                pe.wait_ge(newT_ready, b.k + 1)
                if b.after(1):
                    pe.wait_ge(ready, b.k)
                for q in range(W // 4):
                    last = t.matmul(psD[:, 4 * q:4 * q + 4, :].rearrange("p j n -> p (j n)"), K["w_dec0"][:, :],
                                    newT[:, 4 * q:4 * q + 4, :].rearrange("p j n -> p (j n)"), start=True, stop=True)
                last.then_inc(hid_ps, 1)

            def output(b):
                pe.wait_ge(hid_ready, b.k + 1)
                for j in range(W):
                    last = t.matmul(psO[:, j, :], hid[:, j, :], K["w_dec1"][:, :], start=True, stop=True)
                last.then_inc(out_ps, 1)

            if decode:
                staged(pe, [(2, turn_new), (0, turn_over), (2, hidden), (0, product), (2, output)], TURN)
            else:
                staged(pe, [(0, turn_over), (0, product)], TURN)

        @block.scalar
        def _(act):
            def copy_acc(b):
                act.wait_ge(accT_ps, b.k + 1)
                if b.after(2):
                    act.wait_ge(prod_ps, b.k + (-1))
                nc.scalar.activation(accT[b.h][:, :, :], psT[:, :, :], ACT.Copy).then_inc(accT_ready, 1)

            def root(b):
                act.wait_ge(var_ready, b.k + 1)
                nc.scalar.activation(mean[b.h][:, 4, :], mean[b.h][:, 3, :], ACT.Sqrt, bias=K["eps"][:, 0:1]).then_inc(root_ready, 1)

            def copy_new(b):
                act.wait_ge(newT_ps, b.k + 1)
                if b.after(1):
                    act.wait_ge(hid_ps, b.k)
                nc.scalar.activation(newT[:, :, :], psN[:, :, :], ACT.Copy).then_inc(newT_ready, 1)

            def relu(b):
                act.wait_ge(hid_ps, b.k + 1)
                if b.after(1):
                    act.wait_ge(out_ps, b.k)
                nc.scalar.activation(hid[:, :, :], psD[:, :, :], ACT.Relu, bias=K["b_dec0"][:, 0:1]).then_inc(hid_ready, 1)

            if decode:
                staged(act, [(2, copy_new), (0, copy_acc), (1, root), (2, relu)], TURN)
            else:
                staged(act, [(0, copy_acc), (1, root)], TURN)

        @block.vector
        def _(dve):
            v = nc.vector
            st, st2, st3 = Steps(dve, step), Steps(dve, step2), Steps(dve, step3)

            def statistics(b):
                h, mn = b.h, mean[b.h]
                st.begin(b.k)
                dve.wait_ge(biased_ready, b.k + 1)
                dve.wait_ge(prod_ps, b.k + 1)
                v.tensor_tensor(summed[h][:, :, :], biased[h][:, :, :], psY[:, :, :], ALU.add).then_inc(prod_used, 1)
                dve.wait_ge(prod_used, b.k + 1)
                for j in range(W):
                    last = v.bn_stats(stats[:, j, :], summed[h][:, j, :])
                st.link(last)
                m0, m1, q0, q1 = (stats[:, :, n] for n in (1, 4, 2, 5))
                v.tensor_tensor(mn[:, 0, :], m0, m1, ALU.add)
                v.tensor_tensor(mn[:, 1, :], m0, m1, ALU.subtract)
                st.link(v.tensor_tensor(mn[:, 2, :], q0, q1, ALU.add))
                v.tensor_scalar(mn[:, 0, :], mn[:, 0, :], 0.5, None, ALU.mult)
                st.link(v.scalar_tensor_tensor(mn[:, 1, :], mn[:, 1, :], 0.25, mn[:, 1, :], ALU.mult, ALU.mult))
                v.scalar_tensor_tensor(mn[:, 3, :], mn[:, 2, :], 1.0 / D, mn[:, 1, :], ALU.mult, ALU.add).then_inc(var_ready, 1)

            def normalised(b):
                h, mn = b.h, mean[b.h]
                st2.begin(b.k)
                dve.wait_ge(root_ready, b.k + 1)
                st2.link(v.reciprocal(mn[:, 5, :], mn[:, 4, :]))
                for j in range(W):
                    last = v.tensor_scalar(norm[:, j, :], summed[h][:, j, :], mn[:, 0, j:j + 1], mn[:, 5, j:j + 1], ALU.subtract, ALU.mult)
                st2.link(last)
                st2.link(v.tensor_tensor(norm[:, :, :], norm[:, :, :], along(K["ln_g"][:, :], W), ALU.mult))
                if b.after(2):
                    if decode:
                        dve.wait_ge(newT_ps, b.k + (-1))
                    else:
                        dve.wait_ge(stored[h], STORES * b.turn)
                v.tensor_tensor(new[h][:, :, :], norm[:, :, :], along(K["ln_b"][:, :], W), ALU.add).then_inc(new_ready, 1)

            def add_out(b):
                h = b.h
                st3.begin(b.k)
                if b.after(2):
                    dve.wait_ge(stored[h], STORES * b.turn)
                dve.wait_ge(last_loaded[h], 16 * b.turn + 16)
                st3.link(v.tensor_tensor(ob[h][:, :, :], xb[h][:, :, :], along(K["b_dec1"][:, :], W), ALU.add))
                dve.wait_ge(out_ps, b.k + 1)
                v.tensor_tensor(ob[h][:, :, :], ob[h][:, :, :], psO, ALU.add).then_inc(ready, 1)

            staged(dve, [(0, statistics), (1, normalised)] + ([(2, add_out)] if decode else []), TURN)


def phase_out(nc, z, T, out):
    with nc.semaphore("o_written") as written, nc.Block() as block:
        @block.sync
        def _(sp):
            sp.dma_start(out[:, :], T["out"][0:z.N, :]).then_inc(written, 16)
            sp.wait_ge(written, 16)


def gnn_kernel(nc, x, src, dst, w, out, stop=99):
    z = Shapes(x.shape[0], src.shape[0])
    T = {}
    for name, rows, width, dt in (
        ("x", z.NP, D0, F32), ("h", z.NP, D0, F32), ("out", z.NP, D0, F32),
        ("attr", z.NP, 4, F32),
        ("rows", z.NP, TW, F32),
        ("acc_s", z.NP + 2 * P, D0, F32), ("acc_d", z.NP + 2 * P, D0, F32),
        ("edges", z.CAP, 2, I32),
        ("plan", z.CAP, 3, F32),
        ("feat", z.NP, D, F32), ("acc", z.NP + 2 * P, D, F32),
    ):
        T[name] = nc.dram_tensor("scratch_" + name, [rows, width], dt).ap()
    with ExitStack() as ctx:
        K = {name: ctx.enter_context(nc.sbuf_tensor("k_" + name, shape, dt)) for name, shape, dt in (
            ("iota", [P, max(z.S, P)], F16), ("ident", [P, P], F32), ("earlier", [P, P], F32),
            ("before", [P, P], F32), ("ones", [P, P], F32), ("trash", [P, ET], F32), ("eps", [P, 1], F32),
            ("more", [P, 1], I32),
            ("w_ref", [64, P], F32), ("b_ref", [P, 1], F32),
            ("w_ref_out", [P, 2 * D0], F32), ("b_ref_out", [P, 2 * D0], F32),
            ("w_self_a", [P, SLOTS // 2, P], F32), ("w_self_b", [P, SLOTS // 2, P], F32),
            ("w_enc0", [P, SLOTS, D], F32), ("b_enc0", [P, 1], F32),
            ("w_enc1", [D, D], F32), ("b_enc1", [P, D], F32),
            ("w_conv", [D, D], F32), ("b_conv", [P, D], F32), ("ln_g", [P, D], F32), ("ln_b", [P, D], F32),
            ("w_dec0", [D, D], F32), ("b_dec0", [P, 1], F32), ("w_dec1", [D, D0], F32), ("b_dec1", [P, D0], F32),
        )}
        K["passed"] = ctx.enter_context(nc.semaphore("passed"))
        phase_constants(nc, K, z, w)
        phase_edges(nc, K, z, src, dst, T, x)
        if stop == 1: return T
        phase_rows(nc, K, z, T)
        if stop == 2: return T
        phase_reflect_edges(nc, K, z, T)
        if stop == 3: return T
        phase_reflect_nodes(nc, K, z, T)
        if stop == 4: return T
        phase_encode(nc, K, z, T)
        if stop == 5: return T
        for layer in range(3):
            phase_spread(nc, K, z, T, layer)
            if stop == 6: return T
            phase_convolve(nc, K, z, T, layer, decode=layer == 2)
            if stop == 7: return T
        phase_out(nc, z, T, out)
    return T


_WEIGHTS = ["L0_gnn_W1", "L0_gnn_b1", "L0_gnn_W2", "L0_gnn_b2", "L1_gnn_W_enc0", "L1_gnn_b_enc0",
            "L1_gnn_W_enc1", "L1_gnn_b_enc1", "L1_gnn_W_conv", "L1_gnn_b_conv", "L1_gnn_ln_g",
            "L1_gnn_ln_b", "L1_gnn_W_dec0", "L1_gnn_b_dec0", "L1_gnn_W_dec1", "L1_gnn_b_dec1"]


def kernel(**inputs):
    import numpy as _np
    import concourse.bacc as _bacc
    from concourse import mybir as _mybir
    from concourse.bass_utils import run_bass_kernel_spmd as _run

    nc = _bacc.Bacc("TRN2", target_bir_lowering=False, num_devices=1)
    arrays, aps = {}, {}
    for name in ["x", "src", "dst", *_WEIGHTS]:
        a = _np.ascontiguousarray(inputs[name])
        arrays[f"in_{name}_dram"] = a
        aps[name] = nc.dram_tensor(f"in_{name}_dram", a.shape, _mybir.dt.from_np(a.dtype), kind="ExternalInput").ap()
    out = nc.dram_tensor("out_0_dram", aps["x"].shape, _mybir.dt.float32, kind="ExternalOutput").ap()
    gnn_kernel(nc, aps["x"], aps["src"], aps["dst"], {n: aps[n] for n in _WEIGHTS}, out)
    r = _run(nc, [arrays], core_ids=[0])
    return _np.asarray(r.results[0]["out_0_dram"])
```

```python
import concourse.bass as bass
from concourse import mybir
from contextlib import ExitStack

F32 = mybir.dt.float32
F16 = mybir.dt.float16
I32 = mybir.dt.int32
ALU = mybir.AluOpType
ACT = mybir.ActivationFunctionType
AX = mybir.AxisListType.X

P = 128
D0 = 16
HID = 64
D = 128
TW = D0 + 2
WIDE = 56
SLOTS = 8
ET = 8
RING = 4
LN_EPS = 1e-5
FAR = 1 << 20


class Steps:

    def __init__(self, eng, sem):
        self.eng, self.sem, self.base, self.n, self.per = eng, sem, 0, 0, 0

    def begin(self, k):
        if isinstance(k, int) and k == 0:
            self.base = 0
        else:
            self.per = self.per or self.n
            self.base = k * self.per
        self.n = 0

    def link(self, ins):
        ins.then_inc(self.sem, 1)
        self.n += 1
        self.eng.wait_ge(self.sem, self.base + self.n)


class Block:

    def __init__(self, i, h, lag):
        back = -((h - lag) // 2)
        self.h = (h - lag) % 2
        self.turn = i - back if isinstance(i, int) else (i + (-back) if back else i)
        self.k = 2 * i + (h - lag)

    def after(self, n):
        return not isinstance(self.k, int) or self.k >= n


def staged(eng, stages, n):
    def at(i, h, wanted):
        for lag, work in stages:
            if wanted(lag):
                work(Block(i, h, lag))

    most = max(lag for lag, _ in stages)
    first = -(-(most + 2) // 2)
    for i in range(min(first, n)):
        for h in range(2):
            at(i, h, lambda lag: 2 * i + h >= lag)
    if n > first:
        with eng.Fori(first, n) as i:
            for h in range(2):
                at(i, h, lambda lag: True)
    for i in range(n, n + (most + 1) // 2):
        for h in range(2):
            at(i, h, lambda lag: 2 * n <= 2 * i + h < 2 * n + lag)


def spread(ap, n):
    return ap.unsqueeze(len(ap.shape)).to_broadcast([*ap.shape, n])


def along(ap, n):
    return ap.unsqueeze(1).to_broadcast([ap.shape[0], n, ap.shape[1]])


def turns(eng, body, n):
    body(0)
    if n > 1:
        with eng.Fori(1, n) as i:
            body(i)


def live_turns(eng, body, more_sb, n):
    more = eng.value_load(more_sb[0:1, 0:1], min_val=0, max_val=n - 1)
    body(0)
    if n > 1:
        with eng.Fori(1, n) as i:
            with eng.If(i <= more):
                body(i)
            eng.nop()
    return more


def wait_apart(eng, sem, value, passed):
    eng.wait_ge(sem, value)
    eng.sem_inc(passed, 1)


def cleared_after(nc, ctx, prefix=""):
    made = []

    def clear():
        nc.clear_and_free_semaphores(made)
        nc.all_engine_barrier()

    ctx.callback(clear)

    def sem(name):
        made.append(nc.alloc_semaphore(prefix + name))
        return made[-1]

    return sem


class Shapes:
    def __init__(self, N, E):
        self.N, self.E = N, E
        unit = 2 * WIDE
        self.S = -(-N // (P * unit)) * unit
        self.NP = P * self.S
        self.PAD = self.NP - 1
        self.TRASH = self.NP
        self.L = -(-E // (P * ET)) * ET
        self.PAIRS = -(-E // (2 * ET * P))
        self.CAP = (self.PAIRS + 1) * 2 * ET * P
        assert N < self.NP and self.S % (2 * SLOTS) == 0 and self.S // 2 <= 512
        assert self.NP + 2 * P < FAR and self.CAP < FAR


def phase_edges(nc, K, z, src, dst, T, x):
    S, L, half = z.S, z.L, z.S // 2
    with ExitStack() as ctx:
        sb = lambda n, s, d: ctx.enter_context(nc.sbuf_tensor(n, s, d))
        sem = lambda n: ctx.enter_context(nc.semaphore(n))
        ends = sb("a_ends", [P, 2, L], I32)
        endf = sb("a_endf", [P, 2, L], F32)
        quo = sb("a_quo", [P, 2, L], F32)
        quo_i = sb("a_quo_i", [P, 2, L], I32)
        tmp = sb("a_tmp", [P, 2, L], F32)
        keys = sb("a_keys", [P, L, 5], F32)
        item = sb("a_item", [P, L, 3], I32)
        kept = sb("a_kept", [P, L], F32)
        rank = sb("a_rank", [P, L], F32)
        onesL = sb("a_onesL", [P, L], F32)
        base = sb("a_base", [P, 4], F32)
        count_f = sb("a_count_f", [P, 2], F32)
        count_i = sb("a_count_i", [P, 2], I32)
        fill = sb("a_fill", [P, 2 * z.CAP // P], I32)
        keyb = [sb(f"a_keyb{h}", [P, ET, 5], F32) for h in range(2)]
        itemb = [sb(f"a_itemb{h}", [P, ET, 3], I32) for h in range(2)]
        hot_slot = [sb(f"a_hot_slot{h}", [P, 2, S], F16) for h in range(RING)]
        hot_part = [sb(f"a_hot_part{h}", [P, 3, P], F16) for h in range(RING)]
        away = [sb(f"a_away{h}", [P, P], F16) for h in range(RING)]
        hist = sb("a_hist", [P, 3, S], F32)
        attr = sb("a_attr", [P, S, 4], F32)
        root = sb("a_root", [P, 2, S], F32)
        zero = sb("a_zero", [P, S * D0 // 4], F32)
        zero16 = sb("a_zero16", [P, P], F16)
        ps = [ctx.enter_context(nc.psum_tensor(f"a_ps{j}", [P, 512], F32)) for j in range(6)]
        psb = ctx.enter_context(nc.psum_tensor("a_psb", [P, 4], F32))

        ends_ready = sem("a_ends_ready"); ends_padded = sem("a_ends_padded"); zero_ready = sem("a_zero_ready")
        step = sem("a_step"); totals = sem("a_totals"); bases = sem("a_bases")
        fill_ready = sem("a_fill_ready"); filled = sem("a_filled")
        items_ready = sem("a_items_ready")
        keyb_ready = [sem(f"a_keyb_ready{h}") for h in range(2)]
        itemb_ready = [sem(f"a_itemb_ready{h}") for h in range(2)]
        hot_ready = sem("a_hot_ready"); self_ready = sem("a_self_ready"); away_ready = sem("a_away_ready"); hot_used = sem("a_hot_used")
        packed = [sem(f"a_packed{h}") for h in range(2)]
        hist_done = sem("a_hist_done"); roots = sem("a_roots"); deg_ready = sem("a_deg_ready")
        attr_ready = sem("a_attr_ready"); stored = sem("a_stored"); zeroed = sem("a_zeroed")
        block = ctx.enter_context(nc.Block())
        NB = L // ET
        TURN = NB // 2
        full = z.E // L
        rest = z.E - full * L
        nfull = z.N // S
        nrest = z.N - nfull * S

        @block.sync
        def _(sp):
            sp.wait_ge(ends_padded, 1)
            for a, v in enumerate((src, dst)):
                sp.dma_start(ends[0:full, a, :], v[0:full * L].rearrange("(p c) -> p c", c=L)).then_inc(ends_ready, 16)
                sp.dma_start(ends[full:full + 1, a, 0:rest], v[full * L:z.E].rearrange("(p c) -> p c", p=1)).then_inc(ends_ready, 16)
            sp.wait_ge(fill_ready, 1)
            sp.dma_start(T["edges"].rearrange("(p c) w -> p (c w)", p=P), fill[:, :]).then_inc(filled, 16)
            sp.wait_ge(zero_ready, 1)
            for name in ("acc_s", "acc_d"):
                for q in range(4):
                    w = S * D0 // 4
                    sp.dma_start(T[name][0:z.NP, :].rearrange("(p s) f -> p (s f)", s=S)[:, q * w:(q + 1) * w], zero[:, :]).then_inc(zeroed, 16)
                sp.dma_start(T[name][z.NP:z.NP + 2 * P, :].rearrange("(p a) f -> p (a f)", a=2), zero[:, 0:2 * D0]).then_inc(zeroed, 16)
            sp.dma_start(T["acc"][z.NP:z.NP + 2 * P, :].rearrange("(p a) f -> p (a f)", a=2), zero[:, 0:2 * D]).then_inc(zeroed, 16)
            sp.dma_start(T["x"][0:z.N, :], x[:, :]).then_inc(zeroed, 16)
            left = z.NP - z.N
            sp.dma_start(T["x"][z.N:z.NP, :].rearrange("(p c) f -> p (c f)", c=D0), zero[0:left // D0, 0:D0 * D0]).then_inc(zeroed, 16)
            sp.wait_ge(items_ready, 1)

            def body(i):
                for h in range(2):
                    if not isinstance(i, int):
                        sp.wait_ge(self_ready, i * (2 * ET) + (h - 1) * ET)
                    c = (2 * i + h) * ET
                    sp.dma_start(keyb[h][:, :, :], keys[:, bass.ds(c, ET), :]).then_inc(keyb_ready[h], 16)
                    if not isinstance(i, int):
                        sp.wait_ge(packed[h], i * (16 * ET))
                    sp.dma_start(itemb[h][:, :, :], item[:, bass.ds(c, ET), :]).then_inc(itemb_ready[h], 16)

            turns(sp, body, TURN)
            if NB % 2:
                sp.wait_ge(self_ready, (NB - 2) * ET)
                sp.dma_start(keyb[0][:, :, :], keys[:, L - ET:L, :]).then_inc(keyb_ready[0], 16)
                sp.wait_ge(packed[0], TURN * 16 * ET)
                sp.dma_start(itemb[0][:, :, :], item[:, L - ET:L, :]).then_inc(itemb_ready[0], 16)
            sp.wait_ge(attr_ready, 1)
            sp.dma_start(T["attr"].rearrange("(p s) f -> p s f", s=S), attr[:, :, :]).then_inc(stored, 16)
            sp.wait_ge(stored, 16)
            sp.wait_ge(filled, 16)
            sp.wait_ge(zeroed, 16 * 13)

        @block.gpsimd
        def _(pool):
            pool.memset(ends[:, :, :], z.PAD).then_inc(ends_padded, 1)
            pool.memset(fill[:, :], z.PAD).then_inc(fill_ready, 1)

            def scatter(h, n):
                pool.wait_ge(filled, 16)
                wait_apart(pool, itemb_ready[h], n, K["passed"])
                for j in range(ET):
                    pool.indirect_dma_start(
                        T["edges"][:, :], bass.IndirectOffsetOnAxis(ap=itemb[h][:, j, 0:1], axis=0),
                        itemb[h][:, j, 1:3], None, bounds_check=z.CAP - 1, oob_is_err=False,
                    ).then_inc(packed[h], 16)

            def body(i):
                for h in range(2):
                    scatter(h, 16 * (i + 1))

            turns(pool, body, TURN)
            if NB % 2:
                scatter(0, 16 * (TURN + 1))
            pool.wait_ge(packed[0], 16 * ET * ((NB + 1) // 2))
            pool.wait_ge(packed[1], 16 * ET * (NB // 2))

        @block.scalar
        def _(act):
            def far(h, j, used, block, first):
                if j == 0:
                    act.wait_ge(keyb_ready[h], block)
                if not (first and h == 0 and j < RING):
                    act.wait_ge(hot_used, used)
                nc.scalar.activation(away[j % RING][:, :], K["iota"][:, 0:P], ACT.Abs, bias=keyb[h][:, j, 2:3]).then_inc(away_ready, 1)

            def mark(n, h, j):
                act.wait_ge(away_ready, n)
                nc.scalar.activation(hot_part[j % RING][:, 0, :], away[j % RING][:, :], ACT.Relu, bias=1.0, scale=-1.0)
                act.wait_ge(hot_ready, n)
                nc.scalar.activation(hot_part[j % RING][:, 2, :], hot_part[j % RING][:, 1, :], ACT.Copy,
                                     scale=keyb[h][:, j, 4:5]).then_inc(self_ready, 1)

            def body(i):
                for h in range(2):
                    for j in range(ET):
                        far(h, j, i * (2 * ET) + (h * ET + j + 1 - RING), 16 * (i + 1), isinstance(i, int))
                        mark(i * (2 * ET) + (h * ET + j + 1), h, j)

            turns(act, body, TURN)
            if NB % 2:
                for j in range(ET):
                    far(0, j, TURN * 2 * ET + j + 1 - RING, 16 * (TURN + 1), False)
                    mark(TURN * 2 * ET + j + 1, 0, j)
            act.wait_ge(deg_ready, 1)
            nc.scalar.activation(root[:, :, :], root[:, :, :], ACT.Sqrt).then_inc(roots, 1)

        @block.vector
        def _(dve):
            v = nc.vector
            st = Steps(dve, step)
            v.memset(zero[:, :], 0.0).then_inc(zero_ready, 1)
            v.memset(onesL[:, :], 1.0)
            st.link(v.memset(zero16[:, :], 0.0))
            dve.wait_ge(ends_ready, 64)
            v.tensor_copy(item[:, :, 1:3].rearrange("p c a -> p a c"), ends[:, :, :])
            st.link(v.tensor_copy(endf[:, :, :], ends[:, :, :]))
            st.link(v.tensor_scalar(quo[:, :, :], endf[:, :, :], 1.0 / S, None, ALU.mult))
            st.link(v.tensor_copy(quo_i[:, :, :], quo[:, :, :]))
            st.link(v.tensor_copy(quo[:, :, :], quo_i[:, :, :]))
            st.link(v.scalar_tensor_tensor(tmp[:, :, :], quo[:, :, :], -float(S), endf[:, :, :], ALU.mult, ALU.add))
            st.link(v.tensor_scalar(tmp[:, :, :], tmp[:, :, :], 0.0, None, ALU.is_lt))
            st.link(v.tensor_tensor(quo[:, :, :], quo[:, :, :], tmp[:, :, :], ALU.subtract))
            st.link(v.scalar_tensor_tensor(tmp[:, :, :], quo[:, :, :], -float(S), endf[:, :, :], ALU.mult, ALU.add))
            st.link(v.tensor_scalar(tmp[:, :, :], tmp[:, :, :], float(S), None, ALU.is_ge))
            st.link(v.tensor_tensor(quo[:, :, :], quo[:, :, :], tmp[:, :, :], ALU.add))
            st.link(v.scalar_tensor_tensor(tmp[:, :, :], quo[:, :, :], -float(S), endf[:, :, :], ALU.mult, ALU.add))
            v.tensor_copy(keys[:, :, 0:2].rearrange("p c a -> p a c"), tmp[:, :, :])
            v.tensor_scalar(keys[:, :, 2], quo[:, 0, :], -1.0, None, ALU.mult)
            v.tensor_copy(keys[:, :, 3], quo[:, 1, :])
            st.link(v.tensor_tensor(kept[:, :], endf[:, 0, :], endf[:, 1, :], ALU.not_equal))
            v.tensor_scalar(keys[:, :, 4], kept[:, :], -1.0, 1.0, ALU.mult, ALU.add)
            st.link(v.tensor_tensor_scan(rank[:, :], onesL[:, :], kept[:, :], 0.0, ALU.mult, ALU.add))
            st.link(v.tensor_copy(count_f[:, 0:1], rank[:, L - 1:L]))
            v.tensor_copy(count_f[:, 1:2], rank[:, L - 1:L]).then_inc(totals, 1)
            dve.wait_ge(bases, 1)
            st.link(v.tensor_copy(base[:, 0:2], psb[:, 0:2]))
            st.link(v.tensor_scalar(rank[:, :], rank[:, :], base[:, 0:1], -1.0, ALU.add, ALU.add))
            st.link(v.scalar_tensor_tensor(rank[:, :], keys[:, :, 4], float(FAR), rank[:, :], ALU.mult, ALU.add))
            st.link(v.tensor_copy(item[:, :, 0], rank[:, :]))
            both = 2 * ET * P
            st.link(v.tensor_scalar(base[:, 2:3], base[:, 1:2], -1.0, 0.0, ALU.add, ALU.max))
            st.link(v.tensor_copy(count_i[:, 0:1], base[:, 2:3]))
            st.link(v.tensor_scalar(K["more"][:, :], count_i[:, 0:1], both.bit_length() - 1, None, ALU.logical_shift_right))
            v.tensor_copy(count_i[:, 1:2], K["more"][:, :]).then_inc(items_ready, 1)

            def hot(h, n, first):
                dve.wait_ge(keyb_ready[h], n)
                for j in range(ET):
                    q = j % RING
                    if not (first and h == 0 and j < RING):
                        dve.wait_ge(hot_used, hot.base + (ET * h + j + 1 - RING))
                    v.tensor_scalar(hot_slot[q][:, 0, :], K["iota"][:, 0:S], keyb[h][:, j, 0:1], None, ALU.is_equal)
                    v.tensor_scalar(hot_slot[q][:, 1, :], K["iota"][:, 0:S], keyb[h][:, j, 1:2], None, ALU.is_equal)
                    v.tensor_scalar(hot_part[q][:, 1, :], K["iota"][:, 0:P], keyb[h][:, j, 3:4], None, ALU.is_equal).then_inc(hot_ready, 1)

            def body(i):
                hot.base = i * (2 * ET)
                for h in range(2):
                    hot(h, 16 * (i + 1), isinstance(i, int))

            turns(dve, body, TURN)
            if NB % 2:
                hot.base = TURN * 2 * ET
                hot(0, 16 * (TURN + 1), False)

            dve.wait_ge(hist_done, 1)
            for k in range(3):
                for q in range(2):
                    last = v.tensor_copy(hist[:, k, q * half:(q + 1) * half], ps[2 * k + q][:, 0:half])
            st.link(last)
            st.link(v.tensor_tensor(root[:, 0, :], hist[:, 0, :], hist[:, 1, :], ALU.add))
            v.tensor_scalar(root[:, 0, :], root[:, 0, :], 1e-5, None, ALU.max)
            v.tensor_scalar(root[:, 1, :], hist[:, 1, :], 1.0, None, ALU.add).then_inc(deg_ready, 1)
            dve.wait_ge(roots, 1)
            st.link(v.reciprocal(root[:, :, :], root[:, :, :]))
            v.tensor_copy(attr[:, :, 0:2].rearrange("p s a -> p a s"), root[:, :, :])
            v.tensor_scalar(hist[:, 0, :], hist[:, 2, :], 2.0, None, ALU.mult)
            st.link(v.tensor_scalar(hist[:, 1, :], hist[:, 2, :], 1.0, None, ALU.add))
            st.link(v.tensor_tensor(hist[:, 0:2, :], hist[:, 0:2, :], root[:, :, :], ALU.mult))
            v.tensor_tensor(attr[:, :, 2:4].rearrange("p s a -> p a s"), hist[:, 0:2, :], root[:, :, :], ALU.mult).then_inc(attr_ready, 1)

        @block.tensor
        def _(pe):
            t = nc.tensor
            pe.wait_ge(totals, 1)
            t.matmul(psb[:, 0:1], K["before"][:, :], count_f[:, 0:1], start=True, stop=True)
            t.matmul(psb[:, 1:2], K["ones"][:, :], count_f[:, 1:2], start=True, stop=True).then_inc(bases, 1)
            for j in range(6):
                t.matmul(ps[j][:, 0:half], zero16[:, :], K["iota"][:, 0:half], start=True, stop=False)

            def add(n, j):
                q = j % RING
                pe.wait_ge(hot_ready, n)
                for k, part, slot in ((1, 1, 1), (0, 0, 0), (2, 2, 1)):
                    if k == 0:
                        pe.wait_ge(self_ready, n)
                    for w in range(2):
                        last = t.matmul(ps[2 * k + w][:, 0:half], hot_part[q][:, part, :],
                                        hot_slot[q][:, slot, w * half:(w + 1) * half], start=False, stop=False)
                last.then_inc(hot_used, 1)

            def body(i):
                for j in range(2 * ET):
                    add(i * (2 * ET) + j + 1, j)

            turns(pe, body, TURN)
            if NB % 2:
                for j in range(ET):
                    add(TURN * 2 * ET + j + 1, j)
            for j in range(6):
                last = t.matmul(ps[j][:, 0:half], zero16[:, :], K["iota"][:, 0:half], start=False, stop=True)
            last.then_inc(hist_done, 1)




def phase_constants(nc, K, z, w):
    with ExitStack() as ctx:
        sb = lambda n, s, d: ctx.enter_context(nc.sbuf_tensor(n, s, d))
        sem = cleared_after(nc, ctx)
        wide = sb("c_wide", [P, max(z.S, P)], I32)
        diff = sb("c_diff", [P, P], I32)
        chan = sb("c_chan", [P, ET], I32)
        patterns = sem("c_patterns"); cleared = sem("c_cleared"); loaded = sem("c_loaded")
        made = sem("c_made")
        block = ctx.enter_context(nc.Block())

        @block.gpsimd
        def _(pool):
            pool.iota(wide[:, :], [[1, max(z.S, P)]], base=0, channel_multiplier=0)
            pool.iota(diff[:, :], [[1, P]], base=0, channel_multiplier=-1)
            pool.iota(chan[:, :], [[0, ET // 2], [P, 2]], base=z.TRASH, channel_multiplier=1).then_inc(patterns, 1)

        @block.vector
        def _(dve):
            v = nc.vector
            for name in ("w_ref", "w_ref_out", "w_self_a", "w_self_b", "w_enc0"):
                last = v.memset(K[name][...], 0.0)
            last.then_inc(cleared, 1)
            v.memset(K["ones"][:, :], 1.0)
            v.memset(K["eps"][:, :], LN_EPS)
            dve.wait_ge(patterns, 1)
            v.tensor_copy(K["iota"][:, :], wide[:, :])
            v.tensor_copy(K["trash"][:, :], chan[:, :])
            v.tensor_scalar(K["ident"][:, :], diff[:, :], 0.0, None, ALU.is_equal)
            v.tensor_scalar(K["earlier"][:, :], diff[:, :], 0.0, None, ALU.is_lt)
            v.tensor_scalar(K["before"][:, :], diff[:, :], 0.0, None, ALU.is_gt).then_inc(made, 1)

        @block.sync
        def _(sp):
            n = 0

            def load(out, in_):
                sp.dma_start(out, in_, allow_slow_non_contiguous=True).then_inc(loaded, 16)

            sp.wait_ge(cleared, 1)
            own = w["L0_gnn_W1"][:, 0:D0].rearrange("m k -> k m")
            other = w["L0_gnn_W1"][:, D0:2 * D0].rearrange("m k -> k m")
            W2T = w["L0_gnn_W2"].rearrange("o h -> h o")
            load(K["w_ref"][0:D0, 0:HID], own)
            load(K["w_ref"][0:D0, HID:P], other)
            load(K["w_ref"][TW:TW + D0, 0:HID], other)
            load(K["w_ref"][TW:TW + D0, HID:P], own)
            load(K["w_ref_out"][0:HID, 0:D0], W2T)
            load(K["w_ref_out"][HID:P, D0:2 * D0], W2T)
            n += 6
            for j in range(SLOTS):
                rows = slice(D0 * j, D0 * (j + 1))
                cols = slice(HID * (j % 2), HID * (j % 2 + 1))
                load(K["w_self_a"][rows, j // 2, cols], own)
                load(K["w_self_b"][rows, j // 2, cols], other)
                load(K["w_enc0"][rows, j, :], w["L1_gnn_W_enc0"])
                n += 3
            for a in range(2):
                load(K["b_ref"][HID * a:HID * (a + 1), :], w["L0_gnn_b1"].rearrange("(m a) -> m a", a=1))
                load(K["b_ref_out"][:, D0 * a:D0 * (a + 1)], w["L0_gnn_b2"].partition_broadcast(P))
                n += 2
            for name in ("enc1", "conv", "dec0", "dec1"):
                load(K["w_" + name][:, :], w["L1_gnn_W_" + name])
                n += 1
            for name, col in (("b_enc0", "b_enc0"), ("b_dec0", "b_dec0"), ("b_enc1", "b_enc1_col"),
                              ("ln_g", "ln_g_col"), ("ln_b", "ln_b_col")):
                load(K[col][:, :], w["L1_gnn_" + name].rearrange("(m a) -> m a", a=1))
                n += 1
            for name in ("b_enc1", "b_conv", "b_dec1", "ln_g", "ln_b"):
                load(K[name][:, :], w["L1_gnn_" + name].partition_broadcast(P))
                n += 1
            sp.wait_ge(loaded, 16 * n)


def normalise(v, st, act_turn, x, sums, centred, square, out, width, n):
    st.link(v.tensor_reduce(sums[:, 0, :], x, AX, ALU.add))
    st.link(v.tensor_scalar(sums[:, 1, :], sums[:, 0, :], 1.0 / width, None, ALU.mult))
    st.link(v.tensor_tensor(centred, x, spread(sums[:, 1, :], width), ALU.subtract))
    st.link(v.tensor_tensor(square, centred, centred, ALU.mult))
    v.tensor_reduce(sums[:, 2, :], square, AX, ALU.add).then_inc(act_turn[0], 1)
    st.eng.wait_ge(act_turn[1], n)
    st.link(v.reciprocal(sums[:, 3, :], sums[:, 3, :]))
    st.link(v.tensor_tensor(square, centred, spread(sums[:, 3, :], width), ALU.mult))
    return v.tensor_scalar(out, square, 0.0, None, ALU.max)


def phase_rows(nc, K, z, T):
    S, W = z.S, WIDE
    with ExitStack() as ctx:
        sb = lambda n, s, d: ctx.enter_context(nc.sbuf_tensor(n, s, d))
        sem = cleared_after(nc, ctx)
        xb = [sb(f"b_x{h}", [P, W, D0], F32) for h in range(2)]
        ab = [sb(f"b_attr{h}", [P, W, 4], F32) for h in range(2)]
        row = [sb(f"b_row{h}", [P, W, TW], F32) for h in range(2)]
        centred = sb("b_centred", [P, W, D0], F32)
        square = sb("b_square", [P, W, D0], F32)
        sums = sb("b_sums", [P, 4, W], F32)
        loaded = [sem(f"b_loaded{h}") for h in range(2)]
        stored = [sem(f"b_stored{h}") for h in range(2)]
        step = sem("b_step"); ready = sem("b_ready"); var_ready = sem("b_var"); root_ready = sem("b_root")
        block = ctx.enter_context(nc.Block())
        TURN = S // (2 * W)
        slots = lambda t, k: t[0:z.NP, :].rearrange("(p s) f -> p s f", s=S)[:, bass.ds(k * W, W), :]

        @block.sync
        def _(sp):
            def body(i):
                for h in range(2):
                    if not isinstance(i, int):
                        sp.wait_ge(ready, 2 * i + (h - 1))
                    sp.dma_start(xb[h][:, :, :], slots(T["x"], 2 * i + h)).then_inc(loaded[h], 16)
                    sp.dma_start(ab[h][:, :, :], slots(T["attr"], 2 * i + h)).then_inc(loaded[h], 16)
            turns(sp, body, TURN)

        @block.vector
        def _(dve):
            v = nc.vector
            st = Steps(dve, step)

            def body(i):
                st.begin(i)
                for h in range(2):
                    dve.wait_ge(loaded[h], 32 * i + 32)
                    if not isinstance(i, int):
                        dve.wait_ge(stored[h], 16 * i)
                    v.tensor_copy(row[h][:, :, D0:TW], ab[h][:, :, 0:2])
                    normalise(v, st, (var_ready, root_ready), xb[h][:, :, :], sums, centred[:, :, :],
                              square[:, :, :], row[h][:, :, 0:D0], D0, 2 * i + h + 1).then_inc(ready, 1)
            turns(dve, body, TURN)

        @block.scalar
        def _(act):
            def body(i):
                for h in range(2):
                    act.wait_ge(var_ready, 2 * i + h + 1)
                    nc.scalar.activation(sums[:, 3, :], sums[:, 2, :], ACT.Sqrt, bias=K["eps"][:, 0:1],
                                         scale=1.0 / D0).then_inc(root_ready, 1)
                    act.wait_ge(ready, 2 * i + h + 1)
                    act.dma_start(slots(T["rows"], 2 * i + h), row[h][:, :, :]).then_inc(stored[h], 16)
            turns(act, body, TURN)
            act.wait_ge(stored[0], 16 * TURN)
            act.wait_ge(stored[1], 16 * TURN)


def phase_reflect_edges(nc, K, z, T):
    B = ET * P
    with ExitStack() as ctx:
        sb = lambda n, s, d: ctx.enter_context(nc.sbuf_tensor(n, s, d))
        sem = lambda n: ctx.enter_context(nc.semaphore(n))
        ends = [sb(f"r_ends{h}", [P, ET, 2], I32) for h in range(2)]
        row = [sb(f"r_row{h}", [P, ET, 2, TW], F32) for h in range(2)]
        rowT = sb("r_rowT", [2 * TW, ET, P], F32)
        hid = sb("r_hid", [P, ET, P], F32)
        endf = sb("r_endf", [P, ET, 2], F32)
        same = sb("r_same", [P, 2, ET, P], F32)
        cross = sb("r_cross", [P, 2, ET // 2, P], F32)
        early = sb("r_early", [P, ET, P], F32)
        met = sb("r_met", [P, ET // 2], F32)
        first = sb("r_first", [P, 2, ET], F32)
        offset = sb("r_offset", [P, 2, ET], F32)
        target = [sb(f"r_target{h}", [P, 2, ET], I32) for h in range(2)]
        plan = [sb(f"r_plan{h}", [P, ET, 3], F32) for h in range(2)]
        vec = sb("r_vec", [P, ET, 2, D0], F32)
        prod = sb("r_prod", [P, ET, 2, D0], F32)
        swap = sb("r_swap", [P, ET, 2, D0], F32)
        msg = sb("r_msg", [P, ET, 2, D0], F32)
        inv = sb("r_inv", [P, ET, 2], F32)
        dot = sb("r_dot", [P, ET, 2], F32)
        coef = sb("r_coef", [P, ET], F32)
        total = [sb(f"r_total{h}", [P, 2, ET, D0], F32) for h in range(2)]
        psT = ctx.enter_context(nc.psum_tensor("r_psT", [2 * TW, ET, P], F32))
        psH = ctx.enter_context(nc.psum_tensor("r_psH", [P, ET, P], F32))
        psV = ctx.enter_context(nc.psum_tensor("r_psV", [P, ET, 2 * D0], F32))
        psR = ctx.enter_context(nc.psum_tensor("r_psR", [P, ET, P], F32))
        psS = ctx.enter_context(nc.psum_tensor("r_psS", [P, 2, ET, D0], F32))
        ends_ready = [sem(f"r_ends_ready{h}") for h in range(2)]
        rows_ready = [sem(f"r_rows_ready{h}") for h in range(2)]
        planned = [sem(f"r_planned{h}") for h in range(2)]
        added_to = [sem(f"r_added_to{a}") for a in range(2)]
        step = sem("r_step"); ends_used = sem("r_ends_used"); endf_ready = sem("r_endf_ready"); row_numbers = sem("r_row_numbers")
        numbers_used = sem("r_numbers_used"); rowT_ps = sem("r_rowT_ps"); rowT_ready = sem("r_rowT_ready")
        hid_ps = sem("r_hid_ps"); hid_ready = sem("r_hid_ready"); vec_ps = sem("r_vec_ps")
        msg_ready = sem("r_msg_ready"); sum_ps = sem("r_sum_ps"); totals_ready = sem("r_totals_ready")
        block = ctx.enter_context(nc.Block())
        rows_of = lambda t, k: t[bass.ds(k * B, B), :].rearrange("(p j) w -> p j w", j=ET)

        @block.sync
        def _(sp):
            def body(i):
                for h in range(2):
                    if not isinstance(i, int):
                        sp.wait_ge(ends_used, 2 * i + (h - 1))
                    sp.dma_start(ends[h][:, :, :], rows_of(T["edges"], 2 * i + h)).then_inc(ends_ready[h], 16)
            live_turns(sp, body, K["more"], z.PAIRS)

        @block.gpsimd
        def _(pool):
            def gather(h, j):
                for a in range(2):
                    pool.indirect_dma_start(row[h][:, j, a, :], None, T["rows"][:, :],
                                            bass.IndirectOffsetOnAxis(ap=ends[h][:, j, a:a + 1], axis=0)
                                            ).then_inc(rows_ready[h], 16)

            def scatter(h, j, a):
                pool.indirect_dma_start((T["acc_s"], T["acc_d"])[a][:, :],
                                        bass.IndirectOffsetOnAxis(ap=target[h][:, a, j:j + 1], axis=0),
                                        total[h][:, a, j, :], None, compute_op=ALU.add).then_inc(added_to[a], 16)

            def turn(i, h, ahead):
                k = 2 * i + h
                wait_apart(pool, totals_ready, k + 1, K["passed"])
                if ahead:
                    wait_apart(pool, ends_ready[h], 16 * i + 32, K["passed"])
                for u in range(ET // 2):
                    for a in range(2):
                        for j in (2 * u, 2 * u + 1):
                            scatter(h, j, a)
                    if ahead:
                        gather(h, 2 * u)
                        gather(h, 2 * u + 1)
                    for a in range(2):
                        wait_apart(pool, added_to[a], k * (16 * ET) + 32 * (u + 1), K["passed"])

            more = pool.value_load(K["more"][0:1, 0:1], min_val=0, max_val=z.PAIRS - 1)
            for h in range(2):
                pool.wait_ge(ends_ready[h], 16)
                for j in range(ET):
                    gather(h, j)
            with pool.Fori(0, z.PAIRS - 1) as i:
                with pool.If(i < more):
                    for h in range(2):
                        turn(i, h, True)
                pool.nop()
            for h in range(2):
                turn(more, h, False)

        @block.tensor
        def _(pe):
            t = nc.tensor

            def body(i):
                for h in range(2):
                    k = 2 * i + h
                    pe.wait_ge(endf_ready, k + 1)
                    for a in range(2):
                        if not (isinstance(i, int) and h == 0 and a == 0):
                            pe.wait_ge(numbers_used, 2 * k + a)
                        for j in range(ET):
                            last = t.matmul(psR[:, j, :], endf[:, j, a:a + 1].to_broadcast([P, P]), K["ident"][:, :], start=True, stop=True)
                        last.then_inc(row_numbers, 1)
                    wait_apart(pe, rows_ready[h], (i + 1) * (32 * ET), K["passed"])
                    for j in range(ET):
                        last = t.transpose(psT[:, j, :], row[h][:, j, :, :].rearrange("p a f -> p (a f)"), K["ident"][:, :])
                    last.then_inc(rowT_ps, 1)
                    pe.wait_ge(rowT_ready, k + 1)
                    for q in range(ET // 4):
                        last = t.matmul(psH[:, 4 * q:4 * q + 4, :].rearrange("p j n -> p (j n)"), K["w_ref"][0:2 * TW, :],
                                        rowT[:, 4 * q:4 * q + 4, :].rearrange("p j n -> p (j n)"), start=True, stop=True)
                    last.then_inc(hid_ps, 1)
                    pe.wait_ge(hid_ready, k + 1)
                    for j in range(ET):
                        last = t.matmul(psV[:, j, :], hid[:, j, :], K["w_ref_out"][:, :], start=True, stop=True)
                    last.then_inc(vec_ps, 1)
                    pe.wait_ge(msg_ready, k + 1)
                    for a in range(2):
                        for j in range(ET):
                            last = t.matmul(psS[:, a, j, :], same[:, a, j, :], msg[:, j, a, :], start=True, stop=j % 2 == 1)
                            if j % 2 == 0:
                                last = t.matmul(psS[:, a, j, :], cross[:, a, j // 2, :], msg[:, j + 1, a, :], start=False, stop=True)
                    last.then_inc(sum_ps, 1)
            live_turns(pe, body, K["more"], z.PAIRS)

        @block.scalar
        def _(act):
            def body(i):
                for h in range(2):
                    k = 2 * i + h
                    act.wait_ge(rowT_ps, k + 1)
                    nc.scalar.activation(rowT[:, :, :], psT[:, :, :], ACT.Copy).then_inc(rowT_ready, 1)
                    act.wait_ge(hid_ps, k + 1)
                    nc.scalar.activation(hid[:, :, :], psH[:, :, :], ACT.Relu, bias=K["b_ref"][:, 0:1]).then_inc(hid_ready, 1)
                    act.wait_ge(totals_ready, k + 1)
                    act.dma_start(rows_of(T["plan"], k), plan[h][:, :, :]).then_inc(planned[h], 16)
            more = live_turns(act, body, K["more"], z.PAIRS)
            for h in range(2):
                wait_apart(act, planned[h], more * 16 + 16, K["passed"])

        @block.vector
        def _(dve):
            v = nc.vector
            st = Steps(dve, step)

            def body(i):
                st.begin(i)
                for h in range(2):
                    k = 2 * i + h
                    dve.wait_ge(ends_ready[h], 16 * (i + 1))
                    if not isinstance(i, int):
                        dve.wait_ge(planned[h], 16 * i)
                        dve.wait_ge(added_to[0], i * (32 * ET) + (h - 1) * (16 * ET))
                        dve.wait_ge(added_to[1], i * (32 * ET) + (h - 1) * (16 * ET))
                    v.tensor_copy(endf[:, :, :], ends[h][:, :, :]).then_inc(endf_ready, 1)
                    dve.wait_ge(endf_ready, k + 1)
                    for a in range(2):
                        dve.wait_ge(row_numbers, 2 * k + a + 1)
                        v.tensor_tensor(same[:, a, :, :], psR[:, :, :], spread(endf[:, :, a], P), ALU.is_equal)
                        even = psR[:, :, :].rearrange("p (u q) n -> p u q n", q=2)[:, :, 0, :]
                        odd = endf[:, :, :].rearrange("p (u q) a -> p u q a", q=2)[:, :, 1, a]
                        v.tensor_tensor(cross[:, a, :, :], even, spread(odd, P), ALU.is_equal).then_inc(numbers_used, 1)
                        dve.wait_ge(numbers_used, 2 * k + a + 1)
                        st.link(v.tensor_tensor(early[:, :, :], same[:, a, :, :], along(K["earlier"][:, :], ET), ALU.mult))
                        v.tensor_reduce(met[:, :], cross[:, a, :, :], AX, ALU.max)
                        st.link(v.tensor_reduce(first[:, a, :], early[:, :, :], AX, ALU.max))
                        late = first[:, a, :].rearrange("p (u q) -> p u q", q=2)[:, :, 1]
                        st.link(v.tensor_tensor(late, late, met[:, :], ALU.max))
                    st.link(v.tensor_scalar(first[:, :, :], first[:, :, :], -1.0, 1.0, ALU.mult, ALU.add))
                    endt = endf[:, :, :].rearrange("p j a -> p a j")
                    trash = along(K["trash"][:, :], 2)
                    st.link(v.tensor_tensor(offset[:, :, :], endt, trash, ALU.subtract))
                    st.link(v.tensor_tensor(offset[:, :, :], offset[:, :, :], first[:, :, :], ALU.mult))
                    st.link(v.tensor_tensor(offset[:, :, :], offset[:, :, :], trash, ALU.add))
                    v.tensor_copy(target[h][:, :, :], offset[:, :, :])
                    v.tensor_copy(plan[h][:, :, 0].bitcast(I32), offset[:, 1, :])
                    v.tensor_copy(plan[h][:, :, 1], endf[:, :, 1])
                    dve.wait_ge(rows_ready[h], (i + 1) * (32 * ET))
                    x = row[h][:, :, :, 0:D0]
                    v.tensor_tensor(plan[h][:, :, 2], row[h][:, :, 0, D0 + 1], row[h][:, :, 1, D0 + 1], ALU.mult)
                    v.tensor_tensor(coef[:, :], row[h][:, :, 0, D0], row[h][:, :, 1, D0], ALU.mult).then_inc(ends_used, 1)
                    dve.wait_ge(vec_ps, k + 1)
                    bias = along(K["b_ref_out"][:, :], ET).rearrange("p j (a f) -> p j a f", a=2)
                    st.link(v.tensor_tensor(vec[:, :, :, :], psV[:, :, :].rearrange("p j (a f) -> p j a f", a=2), bias, ALU.add))
                    st.link(v.tensor_tensor(prod[:, :, :, :], vec[:, :, :, :], vec[:, :, :, :], ALU.mult))
                    st.link(v.tensor_reduce(inv[:, :, :], prod[:, :, :, :], AX, ALU.add))
                    st.link(v.tensor_scalar(inv[:, :, :], inv[:, :, :], 1e-24, None, ALU.max))
                    st.link(v.reciprocal(inv[:, :, :], inv[:, :, :]))
                    st.link(v.tensor_tensor(prod[:, :, :, :], vec[:, :, :, :], x, ALU.mult))
                    st.link(v.tensor_reduce(dot[:, :, :], prod[:, :, :, :], AX, ALU.add))
                    st.link(v.scalar_tensor_tensor(dot[:, :, :], dot[:, :, :], 2.0, inv[:, :, :], ALU.mult, ALU.mult))
                    st.link(v.tensor_tensor(prod[:, :, :, :], vec[:, :, :, :], spread(dot[:, :, :], D0), ALU.mult))
                    for a in range(2):
                        last = v.tensor_tensor(swap[:, :, 1 - a, :], x[:, :, a, :], prod[:, :, a, :], ALU.subtract)
                    st.link(last)
                    st.link(v.tensor_tensor(prod[:, :, :, :], vec[:, :, :, :], swap[:, :, :, :], ALU.mult))
                    st.link(v.tensor_reduce(dot[:, :, :], prod[:, :, :, :], AX, ALU.add))
                    st.link(v.scalar_tensor_tensor(dot[:, :, :], dot[:, :, :], 2.0, inv[:, :, :], ALU.mult, ALU.mult))
                    st.link(v.tensor_tensor(prod[:, :, :, :], vec[:, :, :, :], spread(dot[:, :, :], D0), ALU.mult))
                    st.link(v.tensor_tensor(swap[:, :, :, :], swap[:, :, :, :], prod[:, :, :, :], ALU.subtract))
                    both = spread(coef[:, :], 2 * D0).rearrange("p j (a f) -> p j a f", a=2)
                    v.tensor_tensor(msg[:, :, :, :], swap[:, :, :, :], both, ALU.mult).then_inc(msg_ready, 1)
                    dve.wait_ge(sum_ps, k + 1)
                    v.tensor_copy(total[h][:, :, :, :], psS[:, :, :, :]).then_inc(totals_ready, 1)
            live_turns(dve, body, K["more"], z.PAIRS)


def phase_reflect_nodes(nc, K, z, T):
    S, W, G = z.S, WIDE, WIDE // SLOTS
    with ExitStack() as ctx:
        sb = lambda n, s, d: ctx.enter_context(nc.sbuf_tensor(n, s, d))
        sem = cleared_after(nc, ctx)
        xb = [sb(f"n_x{h}", [P, W, D0], F32) for h in range(2)]
        xo = [sb(f"n_xo{h}", [P, W, D0], F32) for h in range(2)]
        ab = [sb(f"n_attr{h}", [P, W, 4], F32) for h in range(2)]
        row = [sb(f"n_row{h}", [P, W, TW], F32) for h in range(2)]
        acc = [sb(f"n_acc{h}", [P, 2, W, D0], F32) for h in range(2)]
        feat = [sb(f"n_feat{h}", [P, W, D0], F32) for h in range(2)]
        rest = [sb(f"n_rest{h}", [P, W, D0], F32) for h in range(2)]
        hb = [sb(f"n_h{h}", [P, W, D0], F32) for h in range(2)]
        hT = sb("n_hT", [P, G, P], F32)
        hid = [sb(f"n_hid{q}", [P, SLOTS // 2, P], F32) for q in range(2)]
        vec = sb("n_vec", [P, W, D0], F32)
        prod = sb("n_prod", [P, W, D0], F32)
        y = sb("n_y", [P, W, D0], F32)
        centred = [sb(f"n_centred{h}", [P, W, D0], F32) for h in range(2)]
        inv = sb("n_inv", [P, W], F32)
        dot = sb("n_dot", [P, W], F32)
        sums = [sb(f"n_sums{h}", [P, 4, W], F32) for h in range(2)]
        psT = ctx.enter_context(nc.psum_tensor("n_psT", [P, 8, P], F32))
        psH = [ctx.enter_context(nc.psum_tensor(f"n_psH{q}", [P, SLOTS // 2, P], F32)) for q in range(2)]
        psV = [ctx.enter_context(nc.psum_tensor(f"n_psV{h}", [P, 64, D0], F32)) for h in range(2)]
        loaded = [sem(f"n_loaded{h}") for h in range(2)]
        stored = [sem(f"n_stored{h}") for h in range(2)]
        packed = sem("n_packed"); sums_added = sem("n_sums_added"); rest_ready = sem("n_rest_ready")
        step = sem("n_step"); step2 = sem("n_step2"); ready = sem("n_ready"); var_ready = sem("n_var"); root_ready = sem("n_root")
        hT_ps = sem("n_hT_ps"); hT_ready = sem("n_hT_ready"); hid_ps = sem("n_hid_ps"); hid_ready = sem("n_hid_ready")
        vec_ps = sem("n_vec_ps"); vec_used = sem("n_vec_used")
        block = ctx.enter_context(nc.Block())
        TURN = S // (2 * W)
        slots = lambda t, k: t[0:z.NP, :].rearrange("(p s) f -> p s f", s=S)[:, bass.ds(k * W, W), :]

        @block.sync
        def _(sp):
            def store(b):
                wait_apart(sp, ready, b.k + 1, K["passed"])
                sp.dma_start(slots(T["x"], b.k), xo[b.h][:, :, :]).then_inc(stored[b.h], 16)
                sp.dma_start(slots(T["h"], b.k), hb[b.h][:, :, :]).then_inc(stored[b.h], 16)

            def load(b):
                if b.after(2):
                    wait_apart(sp, var_ready, b.k + (-1), K["passed"])
                for to, name in ((row[b.h][:, :, :], "rows"), (xb[b.h][:, :, :], "x"), (ab[b.h][:, :, :], "attr"),
                                 (acc[b.h][:, 0, :, :], "acc_s"), (acc[b.h][:, 1, :, :], "acc_d")):
                    sp.dma_start(to, slots(T[name], b.k)).then_inc(loaded[b.h], 16)

            staged(sp, [(0, load), (2, store)], TURN)
            sp.wait_ge(stored[0], 32 * TURN)
            sp.wait_ge(stored[1], 32 * TURN)

        @block.gpsimd
        def _(pool):
            def pack(b):
                if b.after(2):
                    wait_apart(pool, hT_ps, b.k + (-1), K["passed"])
                wait_apart(pool, loaded[b.h], 80 * b.turn + 80, K["passed"])
                pool.tensor_copy(feat[b.h][:, :, :], row[b.h][:, :, 0:D0]).then_inc(packed, 1)

            def add_sums(b):
                h = b.h
                if b.after(2):
                    wait_apart(pool, var_ready, b.k + (-1), K["passed"])
                pool.tensor_tensor(rest[h][:, :, :], acc[h][:, 0, :, :], acc[h][:, 1, :, :], ALU.add).then_inc(sums_added, 1)
                wait_apart(pool, sums_added, b.k + 1, K["passed"])
                pool.tensor_tensor(rest[h][:, :, :], rest[h][:, :, :], row[h][:, :, 0:D0], ALU.add).then_inc(rest_ready, 1)
            staged(pool, [(0, pack), (0, add_sums)], TURN)

        @block.tensor
        def _(pe):
            t = nc.tensor

            def network(b):
                pe.wait_ge(packed, b.k + 1)
                for g in range(G):
                    last = t.transpose(psT[:, g, :], feat[b.h][:, SLOTS * g:SLOTS * (g + 1), :].rearrange("p s f -> p (s f)"), K["ident"][:, :])
                last.then_inc(hT_ps, 1)
                pe.wait_ge(hT_ready, b.k + 1)
                if b.after(2):
                    pe.wait_ge(vec_used, b.k + (-1))
                for g in range(G + 1):
                    q = (b.h * G + g) % 2
                    if g < G:
                        if b.after(1) or g >= 2:
                            pe.wait_ge(hid_ready, b.k * G + (g - 1))
                        for u in range(SLOTS // 2):
                            t.matmul(psH[q][:, u, :], K["w_self_a"][:, u, :], hT[:, g, :], start=True, stop=False)
                            last = t.matmul(psH[q][:, u, :], K["w_self_b"][:, u, :], hT[:, g, :], start=False, stop=True)
                        last.then_inc(hid_ps, 1)
                    if g > 0:
                        pe.wait_ge(hid_ready, b.k * G + g)
                        for u in range(SLOTS // 2):
                            s0 = SLOTS * (g - 1) + 2 * u
                            last = t.matmul(psV[b.h][:, s0:s0 + 2, :].rearrange("p s f -> p (s f)"), hid[1 - q][:, u, :], K["w_ref_out"][:, :], start=True, stop=True)
                        last.then_inc(vec_ps, 1)
            staged(pe, [(0, network)], TURN)

        @block.scalar
        def _(act):
            def serve(b):
                act.wait_ge(hT_ps, b.k + 1)
                nc.scalar.activation(hT[:, :, :], psT[:, 0:G, :], ACT.Copy).then_inc(hT_ready, 1)
                for g in range(G):
                    q = (b.h * G + g) % 2
                    act.wait_ge(hid_ps, b.k * G + (g + 1))
                    if b.after(1) or g >= 2:
                        act.wait_ge(vec_ps, b.k * G + (g - 1))
                    nc.scalar.activation(hid[q][:, :, :], psH[q][:, :, :], ACT.Relu, bias=K["b_ref"][:, 0:1]).then_inc(hid_ready, 1)

            def root(b):
                act.wait_ge(var_ready, b.k + 1)
                nc.scalar.activation(sums[b.h][:, 3, :], sums[b.h][:, 2, :], ACT.Sqrt, bias=K["eps"][:, 0:1], scale=1.0 / D0).then_inc(root_ready, 1)
            staged(act, [(0, serve), (1, root)], TURN)

        @block.vector
        def _(dve):
            v = nc.vector
            st = Steps(dve, step)
            st2 = Steps(dve, step2)
            bias = K["b_ref_out"][:, 0:D0]

            def reflect(b):
                h, sm = b.h, sums[b.h]
                st.begin(b.k)
                x = row[h][:, :, 0:D0]
                dve.wait_ge(loaded[h], 80 * b.turn + 80)
                dve.wait_ge(vec_ps, b.k * G + G)
                v.tensor_tensor(vec[:, :, :], psV[h][:, 0:W, :], along(bias, W), ALU.add).then_inc(vec_used, 1)
                dve.wait_ge(vec_used, b.k + 1)
                st.link(v.tensor_tensor(prod[:, :, :], vec[:, :, :], vec[:, :, :], ALU.mult))
                st.link(v.tensor_reduce(inv[:, :], prod[:, :, :], AX, ALU.add))
                st.link(v.tensor_scalar(inv[:, :], inv[:, :], 1e-24, None, ALU.max))
                st.link(v.reciprocal(inv[:, :], inv[:, :]))
                for n in range(2):
                    st.link(v.tensor_tensor(prod[:, :, :], vec[:, :, :], x, ALU.mult))
                    st.link(v.tensor_reduce(dot[:, :], prod[:, :, :], AX, ALU.add))
                    st.link(v.scalar_tensor_tensor(dot[:, :], dot[:, :], 2.0, inv[:, :], ALU.mult, ALU.mult))
                    st.link(v.tensor_tensor(prod[:, :, :], vec[:, :, :], spread(dot[:, :], D0), ALU.mult))
                    st.link(v.tensor_tensor(y[:, :, :], x, prod[:, :, :], ALU.subtract))
                    x = y[:, :, :]
                st.link(v.tensor_tensor(y[:, :, :], y[:, :, :], spread(ab[h][:, :, 2], D0), ALU.mult))
                dve.wait_ge(rest_ready, b.k + 1)
                st.link(v.tensor_tensor(y[:, :, :], y[:, :, :], rest[h][:, :, :], ALU.add))
                if b.after(2):
                    dve.wait_ge(stored[h], 32 * b.turn)
                st.link(v.scalar_tensor_tensor(xo[h][:, :, :], y[:, :, :], 0.0, xb[h][:, :, :], ALU.max, ALU.add))
                st.link(v.tensor_reduce(sm[:, 0, :], xo[h][:, :, :], AX, ALU.add))
                st.link(v.tensor_scalar(sm[:, 1, :], sm[:, 0, :], 1.0 / D0, None, ALU.mult))
                st.link(v.tensor_tensor(centred[h][:, :, :], xo[h][:, :, :], spread(sm[:, 1, :], D0), ALU.subtract))
                st.link(v.tensor_tensor(y[:, :, :], centred[h][:, :, :], centred[h][:, :, :], ALU.mult))
                v.tensor_reduce(sm[:, 2, :], y[:, :, :], AX, ALU.add).then_inc(var_ready, 1)

            def finish(b):
                h, sm = b.h, sums[b.h]
                st2.begin(b.k)
                dve.wait_ge(root_ready, b.k + 1)
                st2.link(v.reciprocal(sm[:, 3, :], sm[:, 3, :]))
                st2.link(v.tensor_tensor(centred[h][:, :, :], centred[h][:, :, :], spread(sm[:, 3, :], D0), ALU.mult))
                v.tensor_scalar(hb[h][:, :, :], centred[h][:, :, :], 0.0, None, ALU.max).then_inc(ready, 1)
            staged(dve, [(1, finish), (0, reflect)], TURN)


def phase_mix(nc, K, z):
    with ExitStack() as ctx:
        sem = cleared_after(nc, ctx)
        turned = ctx.enter_context(nc.sbuf_tensor("m_turned", [P, D], F32))
        psT = ctx.enter_context(nc.psum_tensor("m_psT", [P, D], F32))
        psW = ctx.enter_context(nc.psum_tensor("m_psW", [P, D], F32))
        psB = ctx.enter_context(nc.psum_tensor("m_psB", [P, D], F32))
        turned_ps = sem("m_turned_ps"); turned_ready = sem("m_turned_ready"); mixed = sem("m_mixed")
        block = ctx.enter_context(nc.Block())

        @block.tensor
        def _(pe):
            nc.tensor.transpose(psT[:, :], K["w_enc1"][:, :], K["ident"][:, :]).then_inc(turned_ps, 1)
            pe.wait_ge(turned_ready, 1)
            nc.tensor.matmul(psW[:, :], turned[:, :], K["w_conv"][:, :], start=True, stop=True)
            nc.tensor.matmul(psB[:, :], K["b_enc1_col"][:, 0:1].to_broadcast([P, P]), K["w_conv"][:, :],
                             start=True, stop=True).then_inc(mixed, 1)

        @block.vector
        def _(dve):
            v = nc.vector
            dve.wait_ge(turned_ps, 1)
            v.tensor_copy(turned[:, :], psT[:, :]).then_inc(turned_ready, 1)
            v.tensor_tensor(K["b_base"][:, :], K["b_enc1"][:, :], K["b_conv"][:, :], ALU.add)
            dve.wait_ge(mixed, 1)
            v.tensor_copy(K["w_mix"][:, :], psW[:, :])
            v.tensor_copy(K["b_mix"][:, :], psB[:, :])
            v.tensor_tensor(K["b_next"][:, :], K["ln_b"][:, :], K["b_conv"][:, :], ALU.add)


def phase_encode(nc, K, z, T):
    S, W = z.S, SLOTS
    with ExitStack() as ctx:
        sb = lambda n, s, d: ctx.enter_context(nc.sbuf_tensor(n, s, d))
        sem = cleared_after(nc, ctx)
        hb = [sb(f"e_h{h}", [P, W, D0], F32) for h in range(2)]
        ab = [sb(f"e_attr{h}", [P, W, 4], F32) for h in range(2)]
        hT = [sb(f"e_hT{h}", [P, P], F32) for h in range(2)]
        hid = [sb(f"e_hid{h}", [P, W, P], F32) for h in range(2)]
        base = [sb(f"e_base{h}", [P, W, D], F32) for h in range(2)]
        feat = [sb(f"e_feat{h}", [P, W, D], F32) for h in range(2)]
        scaled = [sb(f"e_scaled{h}", [P, W, D], F32) for h in range(2)]
        acc = [sb(f"e_acc{h}", [P, W, D], F32) for h in range(2)]
        psT = ctx.enter_context(nc.psum_tensor("e_psT", [P, P], F32))
        psH = ctx.enter_context(nc.psum_tensor("e_psH", [P, W, P], F32))
        psX = ctx.enter_context(nc.psum_tensor("e_psX", [P, W, D], F32))
        psM = ctx.enter_context(nc.psum_tensor("e_psM", [P, W, D], F32))
        loaded = [sem(f"e_loaded{h}") for h in range(2)]
        attr_loaded = [sem(f"e_attr_loaded{h}") for h in range(2)]
        feat_stored = [sem(f"e_feat_stored{h}") for h in range(2)]
        acc_stored = [sem(f"e_acc_stored{h}") for h in range(2)]
        hT_ps = sem("e_hT_ps"); hT_ready = sem("e_hT_ready"); hid_ps = sem("e_hid_ps"); hid_ready = sem("e_hid_ready")
        base_ps = sem("e_base_ps"); base_ready = sem("e_base_ready"); feat_ps = sem("e_feat_ps")
        feat_ready = sem("e_feat_ready"); scaled_ready = sem("e_scaled_ready"); acc_ready = sem("e_acc_ready")
        block = ctx.enter_context(nc.Block())
        TURN = S // (2 * W)
        slots = lambda t, k: t[0:z.NP, :].rearrange("(p s) f -> p s f", s=S)[:, bass.ds(k * W, W), :]

        @block.sync
        def _(sp):
            def load_h(b):
                if b.after(2):
                    wait_apart(sp, hT_ps, b.k + (-1), K["passed"])
                sp.dma_start(hb[b.h][:, :, :], slots(T["h"], b.k)).then_inc(loaded[b.h], 16)

            def load_attr(b):
                if b.after(2):
                    wait_apart(sp, scaled_ready, b.k + (-1), K["passed"])
                sp.dma_start(ab[b.h][:, :, :], slots(T["attr"], b.k)).then_inc(attr_loaded[b.h], 16)

            def store_feat(b):
                wait_apart(sp, feat_ready, b.k + 1, K["passed"])
                sp.dma_start(slots(T["feat"], b.k), feat[b.h][:, :, :]).then_inc(feat_stored[b.h], 16)

            def store_acc(b):
                wait_apart(sp, acc_ready, b.k + 1, K["passed"])
                sp.dma_start(slots(T["acc"], b.k), acc[b.h][:, :, :]).then_inc(acc_stored[b.h], 16)
            staged(sp, [(0, load_h), (1, load_attr), (2, store_feat), (3, store_acc)], TURN)
            for h in range(2):
                sp.wait_ge(feat_stored[h], 16 * TURN)
                sp.wait_ge(acc_stored[h], 16 * TURN)

        @block.tensor
        def _(pe):
            t = nc.tensor

            def turn_over(b):
                pe.wait_ge(loaded[b.h], 16 * b.turn + 16)
                if b.after(1):
                    pe.wait_ge(hT_ready, b.k)
                t.transpose(psT[:, :], hb[b.h][:, :, :].rearrange("p s f -> p (s f)"), K["ident"][:, :]).then_inc(hT_ps, 1)

            def hidden(b):
                pe.wait_ge(hT_ready, b.k + 1)
                for q in range(2):
                    if b.after(1):
                        pe.wait_ge(hid_ready, b.k * 2 + (q - 1))
                    for j in range(q * W // 2, (q + 1) * W // 2):
                        last = t.matmul(psH[:, j, :], K["w_enc0"][:, j, :], hT[b.h][:, :], start=True, stop=True)
                    last.then_inc(hid_ps, 1)

            def features(b):
                if b.after(1):
                    pe.wait_ge(base_ready, b.k)
                for j in range(W):
                    if j % (W // 2) == 0:
                        pe.wait_ge(hid_ready, b.k * 2 + (1 + j // (W // 2)))
                    last = t.matmul(psX[:, j, :], hid[b.h][:, j, :], K["w_enc1"][:, :], start=True, stop=True)
                last.then_inc(base_ps, 1)
                if b.after(1):
                    pe.wait_ge(feat_ready, b.k)
                for j in range(W):
                    last = t.matmul(psM[:, j, :], hid[b.h][:, j, :], K["w_mix"][:, :], start=True, stop=True)
                last.then_inc(feat_ps, 1)
            staged(pe, [(0, turn_over), (1, features), (0, hidden)], TURN)

        @block.scalar
        def _(act):
            def copy(b):
                act.wait_ge(hT_ps, b.k + 1)
                if b.after(2):
                    act.wait_ge(hid_ps, b.k * 2 + (-2))
                nc.scalar.activation(hT[b.h][:, :], psT[:, :], ACT.Copy).then_inc(hT_ready, 1)

            def relu(b):
                if b.after(2):
                    act.wait_ge(feat_ps, b.k + (-1))
                for q in range(2):
                    act.wait_ge(hid_ps, b.k * 2 + (q + 1))
                    part = slice(q * W // 2, (q + 1) * W // 2)
                    nc.scalar.activation(hid[b.h][:, part, :], psH[:, part, :], ACT.Relu, bias=K["b_enc0"][:, 0:1]).then_inc(hid_ready, 1)
            staged(act, [(0, copy), (0, relu)], TURN)

        @block.vector
        def _(dve):
            v = nc.vector

            def add_bias(b):
                h = b.h
                dve.wait_ge(base_ps, b.k + 1)
                if b.after(2):
                    dve.wait_ge(acc_ready, b.k + (-1))
                v.tensor_tensor(base[h][:, :, :], psX[:, :, :], along(K["b_base"][:, :], W), ALU.add).then_inc(base_ready, 1)
                dve.wait_ge(feat_ps, b.k + 1)
                if b.after(2):
                    dve.wait_ge(feat_stored[h], 16 * b.turn)
                v.tensor_tensor(feat[h][:, :, :], psM[:, :, :], along(K["b_mix"][:, :], W), ALU.add).then_inc(feat_ready, 1)
            staged(dve, [(0, add_bias)], TURN)

        @block.gpsimd
        def _(pool):
            def add_loops(b):
                h = b.h
                wait_apart(pool, attr_loaded[h], 16 * b.turn + 16, K["passed"])
                wait_apart(pool, feat_ready, b.k + 1, K["passed"])
                if b.after(2):
                    wait_apart(pool, acc_ready, b.k + (-1), K["passed"])
                pool.tensor_tensor(scaled[h][:, :, :], feat[h][:, :, :], spread(ab[h][:, :, 3], D), ALU.mult).then_inc(scaled_ready, 1)
                if b.after(2):
                    wait_apart(pool, acc_stored[h], 16 * b.turn, K["passed"])
                pool.wait_ge(scaled_ready, b.k + 1)
                pool.tensor_tensor(acc[h][:, :, :], scaled[h][:, :, :], base[h][:, :, :], ALU.add).then_inc(acc_ready, 1)
            staged(pool, [(0, add_loops)], TURN)


def phase_spread(nc, K, z, T, layer):
    B = ET * P
    c = f"s{layer}_"
    with ExitStack() as ctx:
        sb = lambda n, s, d: ctx.enter_context(nc.sbuf_tensor(c + n, s, d))
        sem = lambda n: ctx.enter_context(nc.semaphore(c + n))
        ends = [sb(f"ends{h}", [P, ET, 2], I32) for h in range(2)]
        plan = [sb(f"plan{h}", [P, ET, 3], F32) for h in range(2)]
        row = [sb(f"row{h}", [P, ET, D], F32) for h in range(2)]
        same = sb("same", [P, ET, P], F32)
        cross = sb("cross", [P, ET // 2, P], F32)
        total = [sb(f"total{h}", [P, ET, D], F32) for h in range(2)]
        psR = ctx.enter_context(nc.psum_tensor(c + "psR", [P, ET, P], F32))
        psS = ctx.enter_context(nc.psum_tensor(c + "psS", [P, ET, D], F32))
        ends_ready = [sem(f"ends_ready{h}") for h in range(2)]
        plan_ready = [sem(f"plan_ready{h}") for h in range(2)]
        rows_ready = [sem(f"rows_ready{h}") for h in range(2)]
        numbers = sem("numbers"); same_ready = sem("same_ready"); sum_ps = sem("sum_ps")
        totals_ready = sem("totals_ready"); added = sem("added"); step = sem("step")
        block = ctx.enter_context(nc.Block())
        rows_of = lambda t, k: t[bass.ds(k * B, B), :].rearrange("(p j) w -> p j w", j=ET)

        @block.sync
        def _(sp):
            def load_ends(i, h):
                sp.dma_start(ends[h][:, :, :], rows_of(T["edges"], 2 * i + h)).then_inc(ends_ready[h], 16)

            def body(i):
                if isinstance(i, int):
                    load_ends(0, 0)
                    load_ends(0, 1)
                for h in range(2):
                    if not isinstance(i, int):
                        wait_apart(sp, added, i * (32 * ET) + (h - 1) * (16 * ET), K["passed"])
                    sp.dma_start(plan[h][:, :, :], rows_of(T["plan"], 2 * i + h)).then_inc(plan_ready[h], 16)
                    wait_apart(sp, rows_ready[h], i * (16 * ET) + 16 * ET, K["passed"])
                    load_ends(i + 1, h)
            more = live_turns(sp, body, K["more"], z.PAIRS)
            for h in range(2):
                wait_apart(sp, ends_ready[h], more * 16 + 32, K["passed"])

        @block.gpsimd
        def _(pool):
            def gather(h, j):
                pool.indirect_dma_start(row[h][:, j, :], None, T["feat"][:, :],
                                        bass.IndirectOffsetOnAxis(ap=ends[h][:, j, 0:1], axis=0)
                                        ).then_inc(rows_ready[h], 16)

            def scatter(h, j):
                pool.indirect_dma_start(T["acc"][:, :], bass.IndirectOffsetOnAxis(ap=plan[h][:, j, 0:1].bitcast(I32), axis=0),
                                        total[h][:, j, :], None, compute_op=ALU.add).then_inc(added, 16)

            def turn(i, h, ahead):
                k = 2 * i + h
                wait_apart(pool, totals_ready, k + 1, K["passed"])
                if ahead:
                    wait_apart(pool, ends_ready[h], 16 * i + 32, K["passed"])
                for u in range(ET // 2):
                    scatter(h, 2 * u)
                    scatter(h, 2 * u + 1)
                    if ahead:
                        gather(h, 2 * u)
                        gather(h, 2 * u + 1)
                    wait_apart(pool, added, k * (16 * ET) + 32 * (u + 1), K["passed"])

            more = pool.value_load(K["more"][0:1, 0:1], min_val=0, max_val=z.PAIRS - 1)
            for h in range(2):
                pool.wait_ge(ends_ready[h], 16)
                for j in range(ET):
                    gather(h, j)
            with pool.Fori(0, z.PAIRS - 1) as i:
                with pool.If(i < more):
                    for h in range(2):
                        turn(i, h, True)
                pool.nop()
            for h in range(2):
                turn(more, h, False)

        @block.tensor
        def _(pe):
            t = nc.tensor

            def body(i):
                for h in range(2):
                    k = 2 * i + h
                    pe.wait_ge(plan_ready[h], 16 * (i + 1))
                    if not (isinstance(i, int) and h == 0):
                        pe.wait_ge(same_ready, k)
                    for j in range(ET):
                        last = t.matmul(psR[:, j, :], plan[h][:, j, 1:2].to_broadcast([P, P]), K["ident"][:, :], start=True, stop=True)
                    last.then_inc(numbers, 1)
                    pe.wait_ge(same_ready, k + 1)
                    pe.wait_ge(rows_ready[h], (i + 1) * (16 * ET))
                    if not (isinstance(i, int) and h == 0):
                        pe.wait_ge(totals_ready, k)
                    for j in range(ET):
                        last = t.matmul(psS[:, j, :], same[:, j, :], row[h][:, j, :], start=True, stop=j % 2 == 1)
                        if j % 2 == 0:
                            last = t.matmul(psS[:, j, :], cross[:, j // 2, :], row[h][:, j + 1, :], start=False, stop=True)
                    last.then_inc(sum_ps, 1)
            live_turns(pe, body, K["more"], z.PAIRS)

        @block.vector
        def _(dve):
            v = nc.vector

            def body(i):
                for h in range(2):
                    k = 2 * i + h
                    dve.wait_ge(numbers, k + 1)
                    if not (isinstance(i, int) and h == 0):
                        dve.wait_ge(sum_ps, k)
                    for j in range(ET):
                        last = v.tensor_scalar(same[:, j, :], psR[:, j, :], plan[h][:, j, 1:2], plan[h][:, j, 2:3], ALU.is_equal, ALU.mult)
                        if j % 2:
                            last = v.tensor_scalar(cross[:, j // 2, :], psR[:, j - 1, :], plan[h][:, j, 1:2], plan[h][:, j, 2:3], ALU.is_equal, ALU.mult)
                    last.then_inc(same_ready, 1)
            live_turns(dve, body, K["more"], z.PAIRS)

        @block.scalar
        def _(act):
            def body(i):
                for h in range(2):
                    k = 2 * i + h
                    if not isinstance(i, int):
                        act.wait_ge(added, i * (32 * ET) + (h - 1) * (16 * ET))
                    act.wait_ge(sum_ps, k + 1)
                    nc.scalar.activation(total[h][:, :, :], psS[:, :, :], ACT.Copy).then_inc(totals_ready, 1)
            live_turns(act, body, K["more"], z.PAIRS)


def phase_convolve(nc, K, z, T, layer, decode):
    S, W = z.S, SLOTS
    c = f"v{layer}_"
    with ExitStack() as ctx:
        sb = lambda n, s, d: ctx.enter_context(nc.sbuf_tensor(c + n, s, d))
        sem = cleared_after(nc, ctx, c)
        ps = lambda n, s: ctx.enter_context(nc.psum_tensor(c + n, s, F32))
        acc = [sb(f"acc{h}", [P, W, D], F32) for h in range(2)]
        newT = [sb(f"newT{h}", [P, W, P], F32) for h in range(2)]
        norm = [sb(f"norm{h}", [P, W, D], F32) for h in range(2)]
        stats = sb("stats", [P, W, 6], F32)
        mean = [sb(f"mean{h}", [P, 6, W], F32) for h in range(2)]
        psN = ps("psN", [P, W, P])
        loaded = [sem(f"loaded{h}") for h in range(2)]
        last_loaded = [sem(f"last_loaded{h}") for h in range(2)]
        stored = [sem(f"stored{h}") for h in range(2)]
        step = sem("step"); step2 = sem("step2")
        var_ready = sem("var"); root_ready = sem("root"); scale_ready = sem("scale_ready"); norm_ready = sem("norm_ready"); rest_ready = sem("rest_ready")
        newT_ps = sem("newT_ps"); newT_ready = sem("newT_ready"); ready = sem("ready")
        if decode:
            step3 = sem("step3")
            xb = [sb(f"x{h}", [P, W, D0], F32) for h in range(2)]
            ob = [sb(f"o{h}", [P, W, D0], F32) for h in range(2)]
            hid = [sb(f"hid{h}", [P, W, P], F32) for h in range(2)]
            psD = [ps(f"psD{h}", [P, W, P]) for h in range(2)]
            psO = [ps(f"psO{h}", [P, W, D0]) for h in range(2)]
            hid_ps = sem("hid_ps"); hid_ready = sem("hid_ready"); out_ps = sem("out_ps")
        else:
            gained_ready = sem("gained_ready")
            gained = [sb(f"gained{h}", [P, W, D], F32) for h in range(2)]
            ab = [sb(f"attr{h}", [P, W, 4], F32) for h in range(2)]
            feat = [sb(f"feat{h}", [P, W, D], F32) for h in range(2)]
            biased = [sb(f"biased{h}", [P, W, D], F32) for h in range(2)]
            scaled = [sb(f"scaled{h}", [P, W, D], F32) for h in range(2)]
            nacc = [sb(f"nacc{h}", [P, W, D], F32) for h in range(2)]
            psY = [ps(f"psY{h}", [P, W, D]) for h in range(2)]
            feat_stored = [sem(f"feat_stored{h}") for h in range(2)]
            prod_ps = sem("prod_ps"); feat_ready = sem("feat_ready"); biased_ready = sem("biased"); scaled_ready = sem("scaled")
        block = ctx.enter_context(nc.Block())
        TURN = S // (2 * W)
        A = 5 if decode else 7
        slots = lambda t, k: t[0:z.NP, :].rearrange("(p s) f -> p s f", s=S)[:, bass.ds(k * W, W), :]

        @block.sync
        def _(sp):
            def load_acc(b):
                if b.after(2):
                    wait_apart(sp, norm_ready, b.k + (-1), K["passed"])
                    wait_apart(sp, rest_ready, b.k + (-1), K["passed"])
                sp.dma_start(acc[b.h][:, :, :], slots(T["acc"], b.k)).then_inc(loaded[b.h], 16)

            def load_attr(b):
                if b.after(2):
                    wait_apart(sp, scaled_ready, b.k + (-1), K["passed"])
                sp.dma_start(ab[b.h][:, :, :], slots(T["attr"], b.k)).then_inc(last_loaded[b.h], 16)

            def load_x(b):
                if b.after(2):
                    wait_apart(sp, ready, b.k + (-1), K["passed"])
                sp.dma_start(xb[b.h][:, :, :], slots(T["x"], b.k)).then_inc(last_loaded[b.h], 16)

            def store_feat(b):
                wait_apart(sp, feat_ready, b.k + 1, K["passed"])
                sp.dma_start(slots(T["feat"], b.k), feat[b.h][:, :, :]).then_inc(feat_stored[b.h], 16)

            def store_acc(b):
                wait_apart(sp, ready, b.k + 1, K["passed"])
                sp.dma_start(slots(T["acc"], b.k), nacc[b.h][:, :, :]).then_inc(stored[b.h], 16)

            def store_out(b):
                wait_apart(sp, ready, b.k + 1, K["passed"])
                sp.dma_start(slots(T["out"], b.k), ob[b.h][:, :, :]).then_inc(stored[b.h], 16)

            if decode:
                staged(sp, [(0, load_acc), (4, load_x), (6, store_out)], TURN)
            else:
                staged(sp, [(0, load_acc), (3, load_attr), (4, store_feat), (5, store_acc)], TURN)
                for h in range(2):
                    sp.wait_ge(feat_stored[h], 16 * TURN)
            for h in range(2):
                sp.wait_ge(stored[h], 16 * TURN)

        @block.vector
        def _(dve):
            v = nc.vector
            st, st2 = Steps(dve, step), Steps(dve, step2)

            def statistics(b):
                h, mn = b.h, mean[b.h]
                st.begin(b.k)
                dve.wait_ge(loaded[h], 16 * b.turn + 16)
                if b.after(2):
                    dve.wait_ge(norm_ready, b.k + (-1))
                for j in range(W):
                    last = v.bn_stats(stats[:, j, :], acc[h][:, j, :])
                st.link(last)
                m0, m1, q0, q1 = (stats[:, :, n] for n in (1, 4, 2, 5))
                v.tensor_tensor(mn[:, 0, :], m0, m1, ALU.add)
                v.tensor_tensor(mn[:, 1, :], m0, m1, ALU.subtract)
                st.link(v.tensor_tensor(mn[:, 2, :], q0, q1, ALU.add))
                v.tensor_scalar(mn[:, 0, :], mn[:, 0, :], 0.5, None, ALU.mult)
                st.link(v.scalar_tensor_tensor(mn[:, 1, :], mn[:, 1, :], 0.25, mn[:, 1, :], ALU.mult, ALU.mult))
                v.scalar_tensor_tensor(mn[:, 3, :], mn[:, 2, :], 1.0 / D, mn[:, 1, :], ALU.mult, ALU.add).then_inc(var_ready, 1)

            def scales(b):
                mn = mean[b.h]
                st2.begin(b.k)
                dve.wait_ge(root_ready, b.k + 1)
                st2.link(v.reciprocal(mn[:, 5, :], mn[:, 4, :]))
                v.scalar_tensor_tensor(mn[:, 1, :], mn[:, 0, :], -1.0, mn[:, 5, :], ALU.mult, ALU.mult).then_inc(scale_ready, 1)
                if b.after(2):
                    dve.wait_ge(newT_ps, b.k + (-1))
                for j in range(A, W):
                    last = v.tensor_scalar(norm[b.h][:, j, :], acc[b.h][:, j, :], mn[:, 0, j:j + 1], mn[:, 5, j:j + 1], ALU.subtract, ALU.mult)
                last.then_inc(rest_ready, 1)

            if decode:
                st3 = Steps(dve, step3)

                def add_out(b):
                    h = b.h
                    st3.begin(b.k)
                    if b.after(2):
                        dve.wait_ge(stored[h], 16 * b.turn)
                    dve.wait_ge(last_loaded[h], 16 * b.turn + 16)
                    st3.link(v.tensor_tensor(ob[h][:, :, :], xb[h][:, :, :], along(K["b_dec1"][:, :], W), ALU.add))
                    dve.wait_ge(out_ps, b.k + 1)
                    v.tensor_tensor(ob[h][:, :, :], ob[h][:, :, :], psO[h][:, :, :], ALU.add).then_inc(ready, 1)
                staged(dve, [(0, statistics), (0, scales), (5, add_out)], TURN)
            else:
                def gain(b):
                    h = b.h
                    dve.wait_ge(norm_ready, b.k + 1)
                    dve.wait_ge(rest_ready, b.k + 1)
                    if b.after(2):
                        dve.wait_ge(biased_ready, b.k + (-1))
                    v.tensor_tensor(gained[h][:, :, :], norm[h][:, :, :], along(K["ln_g"][:, :], W), ALU.mult).then_inc(gained_ready, 1)

                def scale(b):
                    h = b.h
                    dve.wait_ge(last_loaded[h], 16 * b.turn + 16)
                    if b.after(2):
                        dve.wait_ge(ready, b.k + (-1))
                    dve.wait_ge(feat_ready, b.k + 1)
                    v.tensor_tensor(scaled[h][:, :, :], feat[h][:, :, :], spread(ab[h][:, :, 3], D), ALU.mult).then_inc(scaled_ready, 1)
                staged(dve, [(1, scales), (2, gain), (0, statistics), (3, scale)], TURN)

        @block.scalar
        def _(act):
            def root(b):
                act.wait_ge(var_ready, b.k + 1)
                nc.scalar.activation(mean[b.h][:, 4, :], mean[b.h][:, 3, :], ACT.Sqrt, bias=K["eps"][:, 0:1]).then_inc(root_ready, 1)

            def apply(b):
                h, mn = b.h, mean[b.h]
                act.wait_ge(scale_ready, b.k + 1)
                if b.after(2):
                    act.wait_ge(newT_ps, b.k + (-1))
                    if not decode:
                        act.wait_ge(gained_ready, b.k + (-1))
                for j in range(A):
                    last = nc.scalar.activation(norm[h][:, j, :], acc[h][:, j, :], ACT.Identity, bias=mn[:, 1, j:j + 1], scale=mn[:, 5, j:j + 1])
                last.then_inc(norm_ready, 1)

            def copy_new(b):
                act.wait_ge(newT_ps, b.k + 1)
                if b.after(2):
                    act.wait_ge(hid_ps if decode else prod_ps, b.k + (-1))
                nc.scalar.activation(newT[b.h][:, :, :], psN[:, :, :], ACT.Identity, bias=K["ln_b_col"][:, 0:1],
                                     scale=K["ln_g_col"][:, 0:1]).then_inc(newT_ready, 1)

            if decode:
                def relu(b):
                    act.wait_ge(hid_ps, b.k + 1)
                    if b.after(2):
                        act.wait_ge(out_ps, b.k + (-1))
                    nc.scalar.activation(hid[b.h][:, :, :], psD[b.h][:, :, :], ACT.Relu, bias=K["b_dec0"][:, 0:1]).then_inc(hid_ready, 1)
                staged(act, [(0, root), (0, apply), (2, relu), (0, copy_new)], TURN)
            else:
                def copy_feat(b):
                    act.wait_ge(prod_ps, b.k + 1)
                    if b.after(2):
                        act.wait_ge(feat_stored[b.h], 16 * b.turn)
                        act.wait_ge(scaled_ready, b.k + (-1))
                    nc.scalar.activation(feat[b.h][:, :, :], psY[b.h][:, :, :], ACT.Copy).then_inc(feat_ready, 1)
                staged(act, [(1, apply), (3, copy_feat), (2, copy_new), (0, root)], TURN)

        @block.tensor
        def _(pe):
            t = nc.tensor

            def turn_new(b):
                pe.wait_ge(norm_ready, b.k + 1)
                pe.wait_ge(rest_ready, b.k + 1)
                if b.after(1):
                    pe.wait_ge(newT_ready, b.k)
                for j in range(W):
                    last = t.transpose(psN[:, j, :], norm[b.h][:, j, :], K["ident"][:, :])
                last.then_inc(newT_ps, 1)

            if decode:
                def hidden(b):
                    pe.wait_ge(newT_ready, b.k + 1)
                    if b.after(2):
                        pe.wait_ge(hid_ready, b.k + (-1))
                    for q in range(W // 4):
                        last = t.matmul(psD[b.h][:, 4 * q:4 * q + 4, :].rearrange("p j n -> p (j n)"), K["w_dec0"][:, :],
                                        newT[b.h][:, 4 * q:4 * q + 4, :].rearrange("p j n -> p (j n)"), start=True, stop=True)
                    last.then_inc(hid_ps, 1)

                def output(b):
                    pe.wait_ge(hid_ready, b.k + 1)
                    if b.after(2):
                        pe.wait_ge(ready, b.k + (-1))
                    for j in range(W):
                        last = t.matmul(psO[b.h][:, j, :], hid[b.h][:, j, :], K["w_dec1"][:, :], start=True, stop=True)
                    last.then_inc(out_ps, 1)
                staged(pe, [(0, turn_new), (1, hidden), (3, output)], TURN)
            else:
                def product(b):
                    pe.wait_ge(newT_ready, b.k + 1)
                    if b.after(2):
                        pe.wait_ge(feat_ready, b.k + (-1))
                    for j in range(W):
                        last = t.matmul(psY[b.h][:, j, :], newT[b.h][:, j, :], K["w_conv"][:, :], start=True, stop=True)
                    last.then_inc(prod_ps, 1)
                staged(pe, [(2, turn_new), (2, product)], TURN)

        if not decode:
            @block.gpsimd
            def _(pool):
                def add_bias(b):
                    if b.after(2):
                        wait_apart(pool, ready, b.k + (-1), K["passed"])
                    pool.wait_ge(gained_ready, b.k + 1)
                    pool.tensor_tensor(biased[b.h][:, :, :], gained[b.h][:, :, :], along(K["b_next"][:, :], W), ALU.add).then_inc(biased_ready, 1)

                def next_acc(b):
                    if b.after(2):
                        wait_apart(pool, stored[b.h], 16 * b.turn, K["passed"])
                    wait_apart(pool, biased_ready, b.k + 1, K["passed"])
                    pool.wait_ge(scaled_ready, b.k + 1)
                    pool.tensor_tensor(nacc[b.h][:, :, :], biased[b.h][:, :, :], scaled[b.h][:, :, :], ALU.add).then_inc(ready, 1)
                staged(pool, [(2, add_bias), (3, next_acc)], TURN)


def phase_out(nc, z, T, out):
    with nc.semaphore("o_written") as written, nc.Block() as block:
        @block.sync
        def _(sp):
            sp.dma_start(out[:, :], T["out"][0:z.N, :]).then_inc(written, 16)
            sp.wait_ge(written, 16)


def gnn_kernel(nc, x, src, dst, w, out, stop=99):
    z = Shapes(x.shape[0], src.shape[0])
    T = {}
    for name, rows, width, dt in (
        ("x", z.NP, D0, F32), ("h", z.NP, D0, F32), ("out", z.NP, D0, F32),
        ("attr", z.NP, 4, F32),
        ("rows", z.NP, TW, F32),
        ("acc_s", z.NP + 2 * P, D0, F32), ("acc_d", z.NP + 2 * P, D0, F32),
        ("edges", z.CAP, 2, I32),
        ("plan", z.CAP, 3, F32),
        ("feat", z.NP, D, F32), ("acc", z.NP + 2 * P, D, F32),
    ):
        T[name] = nc.dram_tensor("scratch_" + name, [rows, width], dt).ap()
    with ExitStack() as ctx:
        K = {name: ctx.enter_context(nc.sbuf_tensor("k_" + name, shape, dt)) for name, shape, dt in (
            ("iota", [P, max(z.S, P)], F16), ("ident", [P, P], F32), ("earlier", [P, P], F32),
            ("before", [P, P], F32), ("ones", [P, P], F32), ("trash", [P, ET], F32), ("eps", [P, 1], F32),
            ("more", [P, 1], I32),
            ("w_ref", [64, P], F32), ("b_ref", [P, 1], F32),
            ("w_ref_out", [P, 2 * D0], F32), ("b_ref_out", [P, 2 * D0], F32),
            ("w_self_a", [P, SLOTS // 2, P], F32), ("w_self_b", [P, SLOTS // 2, P], F32),
            ("w_enc0", [P, SLOTS, D], F32), ("b_enc0", [P, 1], F32),
            ("w_enc1", [D, D], F32), ("b_enc1", [P, D], F32),
            ("b_enc1_col", [P, 1], F32), ("w_mix", [D, D], F32), ("b_mix", [P, D], F32), ("b_base", [P, D], F32),
            ("b_next", [P, D], F32),
            ("w_conv", [D, D], F32), ("b_conv", [P, D], F32), ("ln_g", [P, D], F32), ("ln_b", [P, D], F32),
            ("w_dec0", [D, D], F32), ("b_dec0", [P, 1], F32), ("ln_g_col", [P, 1], F32), ("ln_b_col", [P, 1], F32), ("w_dec1", [D, D0], F32), ("b_dec1", [P, D0], F32),
        )}
        K["passed"] = ctx.enter_context(nc.semaphore("passed"))
        phase_constants(nc, K, z, w)
        phase_edges(nc, K, z, src, dst, T, x)
        if stop == 1: return T
        phase_rows(nc, K, z, T)
        if stop == 2: return T
        phase_reflect_edges(nc, K, z, T)
        if stop == 3: return T
        phase_reflect_nodes(nc, K, z, T)
        if stop == 4: return T
        phase_mix(nc, K, z)
        phase_encode(nc, K, z, T)
        if stop == 5: return T
        for layer in range(3):
            phase_spread(nc, K, z, T, layer)
            if stop == 6: return T
            phase_convolve(nc, K, z, T, layer, decode=layer == 2)
            if stop == 7: return T
        phase_out(nc, z, T, out)
    return T


_WEIGHTS = ["L0_gnn_W1", "L0_gnn_b1", "L0_gnn_W2", "L0_gnn_b2", "L1_gnn_W_enc0", "L1_gnn_b_enc0",
            "L1_gnn_W_enc1", "L1_gnn_b_enc1", "L1_gnn_W_conv", "L1_gnn_b_conv", "L1_gnn_ln_g",
            "L1_gnn_ln_b", "L1_gnn_W_dec0", "L1_gnn_b_dec0", "L1_gnn_W_dec1", "L1_gnn_b_dec1"]


def kernel(**inputs):
    import numpy as _np
    import concourse.bacc as _bacc
    from concourse import mybir as _mybir
    from concourse.bass_utils import run_bass_kernel_spmd as _run

    nc = _bacc.Bacc("TRN2", target_bir_lowering=False, num_devices=1)
    arrays, aps = {}, {}
    for name in ["x", "src", "dst", *_WEIGHTS]:
        a = _np.ascontiguousarray(inputs[name])
        arrays[f"in_{name}_dram"] = a
        aps[name] = nc.dram_tensor(f"in_{name}_dram", a.shape, _mybir.dt.from_np(a.dtype), kind="ExternalInput").ap()
    out = nc.dram_tensor("out_0_dram", aps["x"].shape, _mybir.dt.float32, kind="ExternalOutput").ap()
    gnn_kernel(nc, aps["x"], aps["src"], aps["dst"], {n: aps[n] for n in _WEIGHTS}, out)
    r = _run(nc, [arrays], core_ids=[0])
    return _np.asarray(r.results[0]["out_0_dram"])
```
